# Optimizing a Trainium2 kernel written in Bass

```python
import numpy as np
import jax
import jax.numpy as jnp

def _softmax(x, axis=-1):
    return jax.nn.softmax(x, axis=axis)

def _gelu(x):
    return jax.nn.gelu(x, approximate=True)

def _silu(x):
    return jax.nn.silu(x)

def _sigmoid(x):
    return jax.nn.sigmoid(x)

def _layernorm(x, axis=-1, eps=1e-05):
    m = jnp.mean(x, axis=axis, keepdims=True)
    v = jnp.var(x, axis=axis, keepdims=True)
    return (x - m) / jnp.sqrt(v + eps)

def _scatter_add(tgt, idx, src, axis=0):
    return tgt.at[idx].add(src)

def _segment_sum(src, seg, n):
    return jax.ops.segment_sum(src, seg, n)
kernel_name = 'mk_xattn_ffn_d1_seqx_r8_32c9e2'

def setup_inputs(seed: int=0):
    np.random.seed(seed)
    _w = jnp.asarray

    def _rec_inputs():
        import jax
        import jax.numpy as jnp
        _rk = jax.random.key(seed)
        x = 7.22e-05 + 1 * jax.random.normal(jax.random.fold_in(_rk, 1), (8, 256, 128), jnp.float32)
        _lenS = 256 - jax.random.randint(jax.random.fold_in(_rk, 7), (8,), 0, max(1, 256 // 4) + 1, jnp.int32)
        _lenS2 = 64 - jax.random.randint(jax.random.fold_in(_rk, 8), (8,), 0, max(1, 64 // 4) + 1, jnp.int32)
        _ctx_1024P = jax.random.normal(jax.random.fold_in(_rk, 11), (8, 16, 128), jnp.float32)
        _ctx_1024c = jax.random.dirichlet(jax.random.fold_in(_rk, 511), 0.3 * jnp.ones((16,), jnp.float32), (8, 64))
        _ctx_1024t = jnp.einsum('bsk,bkd->bsd', _ctx_1024c, _ctx_1024P)
        _ctx_1024t = _ctx_1024t * jax.lax.rsqrt(jnp.mean(jnp.square(_ctx_1024t)) + 1e-12) * 0.953939
        ctx_1024 = 4.13588e-05 + 0.999923 * (_ctx_1024t + 0.3 * jax.random.normal(jax.random.fold_in(_rk, 611), (8, 64, 128), jnp.float32))
        return (x, ctx_1024)
    x, ctx_1024 = _rec_inputs()

    def _L0_xattn_setup():
        import math
        import jax, jax.numpy as jnp
        import numpy as np
        H = 16
        D_MODEL = 128
        DK = D_MODEL // H
        K_FACTOR = 2

        def _time_delay_agg_inference(v, corr):
            B, _, _, L = v.shape
            top_k = min(int(K_FACTOR * math.log(L)), L)
            mean_value = jnp.mean(corr, axis=(1, 2))
            weights, delay = jax.lax.top_k(mean_value, top_k)
            tmp_corr = jax.nn.softmax(weights, axis=-1)
            idx = (delay[:, :, None] + jnp.arange(L)) % L
            gathered = jnp.take_along_axis(v[:, None], idx[:, :, None, None, :], axis=-1)
            return jnp.einsum('bk,bkhdl->bhdl', tmp_corr, gathered)
        key = jax.random.key(seed)
        ks = jax.random.split(key, 11)
        B, L, D = (4, 256, D_MODEL)
        s = 1.0 / math.sqrt(D)
        return {'queries': jax.random.normal(ks[0], (B, L, D), jnp.float32), 'keys': jax.random.normal(ks[1], (B, L, D), jnp.float32), 'values': jax.random.normal(ks[2], (B, L, D), jnp.float32), 'Wq': jax.random.normal(ks[3], (D, H * DK), jnp.float32) * s, 'bq': jnp.zeros((H * DK,), jnp.float32), 'Wk': jax.random.normal(ks[4], (D, H * DK), jnp.float32) * s, 'bk': jnp.zeros((H * DK,), jnp.float32), 'Wv': jax.random.normal(ks[5], (D, H * DK), jnp.float32) * s, 'bv': jnp.zeros((H * DK,), jnp.float32), 'Wo': jax.random.normal(ks[6], (H * DK, D), jnp.float32) * s, 'bo': jnp.zeros((D,), jnp.float32)}
    _L0_xattn_all = _L0_xattn_setup()
    _L0_xattn_in = {k: v for k, v in _L0_xattn_all.items() if k in ('Wq', 'bq', 'Wk', 'bk', 'Wv', 'bv', 'Wo', 'bo')}
    del _L0_xattn_all

    def _L0_ffn_setup():
        import jax, jax.numpy as jnp
        import numpy as np
        D_MODEL = 128
        N_HEADS = 16
        HEAD_DIM = D_MODEL // N_HEADS
        KV_LATENT = 64
        N_EXPERTS = 4
        D_HIDDEN = 4 * D_MODEL
        B, T = (2, 128)

        def rmsnorm(x, w, eps=1e-06):
            return w * (x * jax.lax.rsqrt(jnp.mean(x * x, axis=-1, keepdims=True) + eps))

        def layernorm(x, g, b, eps=1e-05):
            mu = jnp.mean(x, axis=-1, keepdims=True)
            var = jnp.mean((x - mu) ** 2, axis=-1, keepdims=True)
            return (x - mu) * jax.lax.rsqrt(var + eps) * g + b

        def apply_rope(x):
            t, d = (x.shape[2], x.shape[3])
            half = d // 2
            pos = jnp.arange(t, dtype=x.dtype)[:, None]
            inv_freq = 1.0 / 10000.0 ** (jnp.arange(half, dtype=x.dtype) / half)
            ang = pos * inv_freq[None, :]
            sin, cos = (jnp.sin(ang), jnp.cos(ang))
            x1, x2 = (x[..., :half], x[..., half:])
            return jnp.concatenate([x1 * cos - x2 * sin, x1 * sin + x2 * cos], axis=-1)

        def mla_attention(x, Wq, Wdkv, Wuk, Wuv, Wo, ln_g, ln_b):
            b, t, _ = x.shape
            q = (x @ Wq.T).reshape(b, t, N_HEADS, HEAD_DIM).transpose(0, 2, 1, 3)
            latent = layernorm(x @ Wdkv.T, ln_g, ln_b)
            k = (latent @ Wuk.T).reshape(b, t, N_HEADS, HEAD_DIM).transpose(0, 2, 1, 3)
            v = (latent @ Wuv.T).reshape(b, t, N_HEADS, HEAD_DIM).transpose(0, 2, 1, 3)
            q = apply_rope(q)
            k = apply_rope(k)
            scores = jnp.einsum('bhqd,bhkd->bhqk', q, k) / np.sqrt(HEAD_DIM)
            causal = jnp.tril(jnp.ones((t, t), dtype=bool))
            scores = jnp.where(causal, scores, -jnp.inf)
            attn = jax.nn.softmax(scores, axis=-1)
            out = jnp.einsum('bhqk,bhkd->bhqd', attn, v).transpose(0, 2, 1, 3).reshape(b, t, D_MODEL)
            return out @ Wo.T

        def moe(x, gate_w, gate_b, W1, b1, W2, b2):
            logits = x @ gate_w.T + gate_b
            top = jnp.argmax(logits, axis=-1)
            onehot = jax.nn.one_hot(top, N_EXPERTS, dtype=x.dtype)
            h = jax.nn.relu(jnp.einsum('btd,ehd->bteh', x, W1) + b1)
            y = jnp.einsum('bteh,edh->bted', h, W2) + b2
            return jnp.einsum('bted,bte->btd', y, onehot)
        key = jax.random.key(seed)
        ks = jax.random.split(key, 16)
        s = lambda fan_in: 1.0 / np.sqrt(fan_in)
        return {'x': jax.random.normal(ks[0], (B, T, D_MODEL), jnp.float32), 'norm1_w': jnp.ones((D_MODEL,), jnp.float32), 'norm2_w': jnp.ones((D_MODEL,), jnp.float32), 'Wq': jax.random.normal(ks[1], (D_MODEL, D_MODEL), jnp.float32) * s(D_MODEL), 'Wdkv': jax.random.normal(ks[2], (KV_LATENT, D_MODEL), jnp.float32) * s(D_MODEL), 'Wuk': jax.random.normal(ks[3], (D_MODEL, KV_LATENT), jnp.float32) * s(KV_LATENT), 'Wuv': jax.random.normal(ks[4], (D_MODEL, KV_LATENT), jnp.float32) * s(KV_LATENT), 'Wo': jax.random.normal(ks[5], (D_MODEL, D_MODEL), jnp.float32) * s(D_MODEL), 'ln_g': jnp.ones((KV_LATENT,), jnp.float32), 'ln_b': jnp.zeros((KV_LATENT,), jnp.float32), 'gate_w': jax.random.normal(ks[6], (N_EXPERTS, D_MODEL), jnp.float32) * s(D_MODEL), 'gate_b': jnp.zeros((N_EXPERTS,), jnp.float32), 'W1': jax.random.normal(ks[7], (N_EXPERTS, D_HIDDEN, D_MODEL), jnp.float32) * s(D_MODEL), 'b1': jnp.zeros((N_EXPERTS, D_HIDDEN), jnp.float32), 'W2': jax.random.normal(ks[8], (N_EXPERTS, D_MODEL, D_HIDDEN), jnp.float32) * s(D_HIDDEN), 'b2': jnp.zeros((N_EXPERTS, D_MODEL), jnp.float32)}
    _L0_ffn_all = _L0_ffn_setup()
    _L0_ffn_in = {k: v for k, v in _L0_ffn_all.items() if k in ('norm1_w', 'norm2_w', 'Wq', 'Wdkv', 'Wuk', 'Wuv', 'Wo', 'ln_g', 'ln_b', 'gate_w', 'gate_b', 'W1', 'b1', 'W2', 'b2')}
    del _L0_ffn_all
    return {'x': x, 'ctx_1024': ctx_1024, 'L0_xattn_Wq': _L0_xattn_in['Wq'], 'L0_xattn_bq': _L0_xattn_in['bq'], 'L0_xattn_Wk': _L0_xattn_in['Wk'], 'L0_xattn_bk': _L0_xattn_in['bk'], 'L0_xattn_Wv': _L0_xattn_in['Wv'], 'L0_xattn_bv': _L0_xattn_in['bv'], 'L0_xattn_Wo': _L0_xattn_in['Wo'], 'L0_xattn_bo': _L0_xattn_in['bo'], 'L0_ffn_norm1_w': _L0_ffn_in['norm1_w'], 'L0_ffn_norm2_w': _L0_ffn_in['norm2_w'], 'L0_ffn_Wq': _L0_ffn_in['Wq'], 'L0_ffn_Wdkv': _L0_ffn_in['Wdkv'], 'L0_ffn_Wuk': _L0_ffn_in['Wuk'], 'L0_ffn_Wuv': _L0_ffn_in['Wuv'], 'L0_ffn_Wo': _L0_ffn_in['Wo'], 'L0_ffn_ln_g': _L0_ffn_in['ln_g'], 'L0_ffn_ln_b': _L0_ffn_in['ln_b'], 'L0_ffn_gate_w': _L0_ffn_in['gate_w'], 'L0_ffn_gate_b': _L0_ffn_in['gate_b'], 'L0_ffn_W1': _L0_ffn_in['W1'], 'L0_ffn_b1': _L0_ffn_in['b1'], 'L0_ffn_W2': _L0_ffn_in['W2'], 'L0_ffn_b2': _L0_ffn_in['b2']}

def reference(x, ctx_1024, L0_xattn_Wq, L0_xattn_bq, L0_xattn_Wk, L0_xattn_bk, L0_xattn_Wv, L0_xattn_bv, L0_xattn_Wo, L0_xattn_bo, L0_ffn_norm1_w, L0_ffn_norm2_w, L0_ffn_Wq, L0_ffn_Wdkv, L0_ffn_Wuk, L0_ffn_Wuv, L0_ffn_Wo, L0_ffn_ln_g, L0_ffn_ln_b, L0_ffn_gate_w, L0_ffn_gate_b, L0_ffn_W1, L0_ffn_b1, L0_ffn_W2, L0_ffn_b2):
    import jax
    import jax.numpy as jnp

    def _L0_xattn_ref(queries, keys, values, Wq, bq, Wk, bk, Wv, bv, Wo, bo):
        import math
        import jax, jax.numpy as jnp
        import numpy as np
        H = 16
        D_MODEL = 128
        DK = D_MODEL // H
        K_FACTOR = 2

        def _time_delay_agg_inference(v, corr):
            B, _, _, L = v.shape
            top_k = min(int(K_FACTOR * math.log(L)), L)
            mean_value = jnp.mean(corr, axis=(1, 2))
            weights, delay = jax.lax.top_k(mean_value, top_k)
            tmp_corr = jax.nn.softmax(weights, axis=-1)
            idx = (delay[:, :, None] + jnp.arange(L)) % L
            gathered = jnp.take_along_axis(v[:, None], idx[:, :, None, None, :], axis=-1)
            return jnp.einsum('bk,bkhdl->bhdl', tmp_corr, gathered)
        B, Lq, _ = queries.shape
        Lk = keys.shape[1]
        q = (queries @ Wq + bq).reshape(B, Lq, H, DK)
        k = (keys @ Wk + bk).reshape(B, Lk, H, DK)
        v = (values @ Wv + bv).reshape(B, Lk, H, DK)
        if Lq > Lk:
            pad = ((0, 0), (0, Lq - Lk), (0, 0), (0, 0))
            k = jnp.pad(k, pad)
            v = jnp.pad(v, pad)
        else:
            k = k[:, :Lq]
            v = v[:, :Lq]
        qt = jnp.transpose(q, (0, 2, 3, 1))
        kt = jnp.transpose(k, (0, 2, 3, 1))
        vt = jnp.transpose(v, (0, 2, 3, 1))
        qf = jnp.fft.rfft(qt)
        kf = jnp.fft.rfft(kt)
        c = qf.real * kf.real + 1j * -(qf.imag * kf.imag)
        corr = jnp.fft.irfft(c, n=Lq).astype(qt.dtype)
        agg = _time_delay_agg_inference(vt, corr)
        out = jnp.transpose(agg, (0, 3, 1, 2)).reshape(B, Lq, H * DK)
        return out @ Wo + bo

    def _L0_ffn_ref(x, norm1_w, norm2_w, Wq, Wdkv, Wuk, Wuv, Wo, ln_g, ln_b, gate_w, gate_b, W1, b1, W2, b2):
        import jax, jax.numpy as jnp
        import numpy as np
        D_MODEL = 128
        N_HEADS = 16
        HEAD_DIM = D_MODEL // N_HEADS
        KV_LATENT = 64
        N_EXPERTS = 4
        D_HIDDEN = 4 * D_MODEL
        B, T = (2, 128)

        def rmsnorm(x, w, eps=1e-06):
            return w * (x * jax.lax.rsqrt(jnp.mean(x * x, axis=-1, keepdims=True) + eps))

        def layernorm(x, g, b, eps=1e-05):
            mu = jnp.mean(x, axis=-1, keepdims=True)
            var = jnp.mean((x - mu) ** 2, axis=-1, keepdims=True)
            return (x - mu) * jax.lax.rsqrt(var + eps) * g + b

        def apply_rope(x):
            t, d = (x.shape[2], x.shape[3])
            half = d // 2
            pos = jnp.arange(t, dtype=x.dtype)[:, None]
            inv_freq = 1.0 / 10000.0 ** (jnp.arange(half, dtype=x.dtype) / half)
            ang = pos * inv_freq[None, :]
            sin, cos = (jnp.sin(ang), jnp.cos(ang))
            x1, x2 = (x[..., :half], x[..., half:])
            return jnp.concatenate([x1 * cos - x2 * sin, x1 * sin + x2 * cos], axis=-1)

        def mla_attention(x, Wq, Wdkv, Wuk, Wuv, Wo, ln_g, ln_b):
            b, t, _ = x.shape
            q = (x @ Wq.T).reshape(b, t, N_HEADS, HEAD_DIM).transpose(0, 2, 1, 3)
            latent = layernorm(x @ Wdkv.T, ln_g, ln_b)
            k = (latent @ Wuk.T).reshape(b, t, N_HEADS, HEAD_DIM).transpose(0, 2, 1, 3)
            v = (latent @ Wuv.T).reshape(b, t, N_HEADS, HEAD_DIM).transpose(0, 2, 1, 3)
            q = apply_rope(q)
            k = apply_rope(k)
            scores = jnp.einsum('bhqd,bhkd->bhqk', q, k) / np.sqrt(HEAD_DIM)
            causal = jnp.tril(jnp.ones((t, t), dtype=bool))
            scores = jnp.where(causal, scores, -jnp.inf)
            attn = jax.nn.softmax(scores, axis=-1)
            out = jnp.einsum('bhqk,bhkd->bhqd', attn, v).transpose(0, 2, 1, 3).reshape(b, t, D_MODEL)
            return out @ Wo.T

        def moe(x, gate_w, gate_b, W1, b1, W2, b2):
            logits = x @ gate_w.T + gate_b
            top = jnp.argmax(logits, axis=-1)
            onehot = jax.nn.one_hot(top, N_EXPERTS, dtype=x.dtype)
            h = jax.nn.relu(jnp.einsum('btd,ehd->bteh', x, W1) + b1)
            y = jnp.einsum('bteh,edh->bted', h, W2) + b2
            return jnp.einsum('bted,bte->btd', y, onehot)
        x = x + mla_attention(rmsnorm(x, norm1_w), Wq, Wdkv, Wuk, Wuv, Wo, ln_g, ln_b)
        x = x + moe(rmsnorm(x, norm2_w), gate_w, gate_b, W1, b1, W2, b2)
        return x
    x = x + _L0_xattn_ref(_layernorm(x, axis=-1), ctx_1024, ctx_1024, L0_xattn_Wq, L0_xattn_bq, L0_xattn_Wk, L0_xattn_bk, L0_xattn_Wv, L0_xattn_bv, L0_xattn_Wo, L0_xattn_bo)
    x = x + _L0_ffn_ref(_layernorm(x, axis=-1), L0_ffn_norm1_w, L0_ffn_norm2_w, L0_ffn_Wq, L0_ffn_Wdkv, L0_ffn_Wuk, L0_ffn_Wuv, L0_ffn_Wo, L0_ffn_ln_g, L0_ffn_ln_b, L0_ffn_gate_w, L0_ffn_gate_b, L0_ffn_W1, L0_ffn_b1, L0_ffn_W2, L0_ffn_b2)
    return x

_drawn_inputs = setup_inputs


def setup_inputs(seed=0):
    import zlib

    import numpy as np

    out = dict(_drawn_inputs(seed))
    spreads = {'L0_xattn_bq': (0.0, 0.1),
     'L0_xattn_bk': (0.0, 0.1),
     'L0_xattn_bv': (0.0, 0.1),
     'L0_xattn_bo': (0.0, 0.1),
     'L0_ffn_norm1_w': (1.0, 0.2),
     'L0_ffn_norm2_w': (1.0, 0.2),
     'L0_ffn_ln_g': (1.0, 0.2),
     'L0_ffn_ln_b': (0.0, 0.1),
     'L0_ffn_gate_b': (0.0, 0.1),
     'L0_ffn_b1': (0.0, 0.1),
     'L0_ffn_b2': (0.0, 0.1)}
    factors = {}
    for name, (base, spread) in spreads.items():
        noise = np.random.default_rng([zlib.crc32(name.encode()), seed]).standard_normal(out[name].shape)
        drawn = base * np.exp(spread * noise) if base else spread * noise
        out[name] = jnp.asarray(drawn.astype(out[name].dtype))
    for name, factor in factors.items():
        out[name] = (out[name] * factor).astype(out[name].dtype)
    return out
```

```python
from contextlib import ExitStack

import concourse.bass as bass
import numpy as np
from concourse import mybir

F32 = mybir.dt.float32
F16 = mybir.dt.float16
BF16 = mybir.dt.bfloat16
ALU = mybir.AluOpType
ACT = mybir.ActivationFunctionType
AX_X = mybir.AxisListType.X

P = 128
B, T, D = 8, 256, 128
S = 64
TT = T // P
NT = B * TT
PAIRS = B // 2
LN_EPS, RMS_EPS = 1e-5, 1e-6
TOPK = 11
LOWEST = -3.0e38

WKT, WVT, WQB, WO, BKV, CTX, BO = 0, 128, 256, 385, 513, 515, 1027
PACK1 = BO + D

H, DH, L = 16, 8, 64
SCALE = float(DH) ** -0.5
SROWS = 4 * DH + 1
RING = 4
CHUNK = 2 * (T + P)
UNITS = H // 2
MAXU = 3 * H // 4
WQ, WQR, WDKV, WOF, N1, N2, ROPE = 0, 128, 256, 320, 448, 449, 450
WUK, WUKR, WUV, LNG, LNB = 962, 1090, 1218, 1346, 1347
PACK2 = 1348

E, HID = 4, 512
HK = HID // P
GROUPS = NT // 4
W1, W2, B1, GATE, GB, B2 = 0, 2048, 4096, 4112, 4116, 4120
PACK3 = B2 + E * D


def build(nc, x, pack1, dft_x, dft_k, inv, pack2, pack3, out):
    with ExitStack() as ctx:
        def sb(name, shape, dt=F32):
            return ctx.enter_context(nc.sbuf_tensor(name, shape, dt))

        def sem(name):
            return ctx.enter_context(nc.semaphore(name))

        PS = ctx.enter_context(nc.psum_tensor("PS", [P, 8, 512], F32))

        X = sb("X", [P, NT, D])
        XB = sb("XB", [P, NT, D])
        XN = sb("XN", [P, NT, D])
        w1 = sb("w1", [P, PACK1])
        fx = sb("fx", [P, TT, T])
        fk = sb("fk", [P, T])
        iv = sb("iv", [P, TT, T])
        bst = sb("bst", [P, NT, 6])
        mv = sb("mv", [P, NT, 2])
        rstd = sb("rstd", [P, NT, 2])
        half = sb("half", [P, 2 * NT])
        bkv = sb("bkv", [P, 2, P])
        mn = sb("mn", [P, 257])
        biasbc = sb("biasbc", [P, 257])
        kqv = sb("kqv", [P, PAIRS, 257])
        kb = sb("kb", [P, PAIRS, 2])
        flat = sb("flat", [P, T])
        kd = sb("kd", [P, 4, 512])
        prod = sb("prod", [P, 4, 512])
        cross = sb("cross", [P, 2, PAIRS, 2])
        mean = sb("mean", [B, T])
        top = sb("top", [B, 24])
        work = sb("work", [B, 2, T])
        soft = sb("soft", [B, 2 * T])
        tot = sb("tot", [B, 4])
        circ = sb("circ", [P, PAIRS, T])

        def tiles(a, par, g):
            return a[:].rearrange("p (g a c h) d -> p g c a (h d)", a=2, c=2, h=TT)[:, g, par]

        w2 = sb("w2", [P, PACK2])
        ident = sb("ident", [P, P])
        identb = sb("identb", [P, P], BF16)
        causal = sb("causal", [P, 4, P], BF16)
        ast = sb("ast", [P, TT, 6])
        amv = sb("amv", [P, TT, 2])
        aeps = sb("aeps", [P, 2, TT])
        ars = sb("ars", [P, 2, TT])
        hs = sb("hs", [P, TT, D])
        hT = sb("hT", [P, T])
        rope = sb("rope", [P, 512])
        qk = sb("qk", [P, T])
        parts = sb("parts", [P, 2, 2, T], F16)
        lat = sb("lat", [P, TT, L])
        lst = sb("lst", [P, TT, 6])
        lmv = sb("lmv", [P, TT, 2])
        leps = sb("leps", [P, TT])
        lrs = sb("lrs", [P, TT])
        latn = sb("latn", [P, TT, L])
        latT = sb("latT", [L, T])
        vst = sb("vst", [P, 2, TT, H, P])
        qs = sb("qs", [SROWS, 2, H, T], F16)
        ks = sb("ks", [SROWS, 2, H, T], F16)
        mx = sb("mx", [P, 2, TT, H])
        mneg = sb("mneg", [H // 2, 2, T], F16)
        probs = sb("probs", [P, RING, CHUNK])
        rec = sb("rec", [P // 2, 2 * T])
        attnT = sb("attnT", [P, T])
        EX = [PS[:, 2 * n:2 * n + 2, :].rearrange("p a b -> p (a b)") for n in range(2)]
        AV = PS[:, 6, :]

        def blocks(a, first):
            return bass.AP(a.tensor, a.offset + first, [list(a.ap[0]), [P * H // 2, 2 * TT], [P + DH, H // 2], [1, DH]])

        MISC = PS[:, 7, :]

        def tile_of(a, b, t=0, n=1):
            return a[:].rearrange("p n d -> p (n d)")[:, bass.ds(b * T + t * P, n * P)]

        settled = sem("settled")
        w3 = sb("w3", [P, PACK3])
        y = vst[:, 1, 0].rearrange("p h c -> p (h c)").rearrange("p (t d) -> p t d", d=D)
        yT = vst[:, 1, 1].rearrange("p h c -> p (h c)")
        ssq = sb("ssq", [P, NT])
        sqe = sb("sqe", [P, NT])
        rr = sb("rr", [P, NT])
        logit = sb("logit", [P, NT, E])
        hit = sb("hit", [P, NT, E])
        lead = sb("lead", [P, NT, 1])
        rank = sb("rank", [P, NT, E])
        ones = sb("ones", [1, P])
        hid = vst[:, 0].rearrange("p a h c -> p (a h c)").rearrange("p (n k t) -> p n k t", n=2, k=HK)
        tmp = sb("tmp", [P, 4, D])
        acc = sb("acc", [P, 4, D])
        w3_in, w3_ok, y_ok, yT_pe, yT_ok, gate_pe, gate_ok, rank_ok = (sem(n) for n in (
            "w3_in", "w3_ok", "y_ok", "yT_pe", "yT_ok", "gate_pe", "gate_ok", "rank_ok"))
        hid_pe, hid_ok, out_pe, tmp_ok, acc_ok, sum_ok = (sem(n) for n in (
            "hid_pe", "hid_ok", "out_pe", "tmp_ok", "acc_ok", "sum_ok"))
        w2_in, ids, w2_ok = sem("w2_in"), sem("ids"), sem("w2_ok")
        a_stats, a_aggr, a_eps, a_rstd, hs_ok, xn1_ok = (sem(n) for n in (
            "a_stats", "a_aggr", "a_eps", "a_rstd", "hs_ok", "xn1_ok"))
        prep_pe, hT_sb, q_tmp, q_sum, q_hi, q_ok = (sem(n) for n in (
            "prep_pe", "hT_sb", "q_tmp", "q_sum", "q_hi", "q_ok"))
        lat_sb, l_stats, l_aggr, l_eps, l_rstd, latn_ok, latT_sb = (sem(n) for n in (
            "lat_sb", "l_stats", "l_aggr", "l_eps", "l_rstd", "latn_ok", "latT_sb"))
        k_tmp, k_sum, k_hi, k_ok, v_sb = (sem(n) for n in ("k_tmp", "k_sum", "k_hi", "k_ok", "v_sb"))
        stack_in, m_in = sem("stack_in"), [sem("m_in0"), sem("m_in1")]
        max_pe, max_ok, m_pe, m_neg = sem("max_pe"), sem("max_ok"), sem("m_pe"), sem("m_neg")
        sc_pe, exp_ok, mask_ok, av_pe = sem("sc_pe"), sem("exp_ok"), sem("mask_ok"), sem("av_pe")
        rec_ok, attn_ok, fin_pe, x2_ok, xs_ok, vst_ok = (sem(n) for n in (
            "rec_ok", "attn_ok", "fin_pe", "x2_ok", "xs_ok", "vst_ok"))

        x_in = [sem(f"x_in{c}") for c in range(4)]
        w1_in, fx_in, fk_in, iv_in = sem("w1_in"), sem("fx_in"), sem("fk_in"), sem("iv_in")
        stats_a, stats_b, var_eps, rstd_ok, xn_ok, xb_ok = (sem(n) for n in (
            "stats_a", "stats_b", "var_eps", "rstd_ok", "xn_ok", "xb_ok"))
        consts, bias_rows = sem("consts"), sem("bias_rows")
        fold_pe, fold_sb, kqv_pe, kqv_sb = sem("fold_pe"), sem("fold_sb"), sem("kqv_pe"), sem("kqv_sb")
        kdft_pe, kdft_sb, xdft_pe, prod_ok, cross_ok = (sem(n) for n in (
            "kdft_pe", "kdft_sb", "xdft_pe", "prod_ok", "cross_ok"))
        mean_pe, topk, mean_exp_in, mean_exp, soft_ok, circ_in, x1_pe, x1_ok = (sem(n) for n in (
            "mean_pe", "topk", "mean_exp_in", "mean_exp", "soft_ok", "circ_in", "x1_pe", "x1_ok"))
        stored = sem("stored")
        block = ctx.enter_context(nc.Block())

        def has(b):
            return not isinstance(b, int) or 0 <= b < B

        def steps(eng, first, last):
            for i in range(first, 1):
                yield i, i % 2
            with eng.Fori(1, 5, 2) as i:
                yield i, 1
                yield i + 1, 0
            for i in range(5, last + 1):
                yield i, i % 2

        def wait(eng, s, value):
            if not isinstance(value, int) or value > 0:
                eng.wait_ge(s, value)

        def settle(eng, b):
            if not isinstance(b, int):
                eng.sem_inc(settled, 1)

        def stack(sp, b, par):
            wait(sp, sc_pe, UNITS * (b - 1))
            settle(sp, b)
            for n, done, dst in ((0, q_ok, qs), (1, k_ok, ks)):
                sp.wait_ge(done, b + 1)
                settle(sp, b)
                for c in range(4):
                    part = c // 2 if n == 0 else c % 2
                    sp.dma_start(dst[DH * c:DH * c + DH, par, :, :], parts[:, n, part, :]).then_inc(stack_in, 16)

        def m_row(sp, b, par, half):
            sp.wait_ge(m_neg, 2 * b + half + 1)
            settle(sp, b)
            wait(sp, sc_pe, UNITS * (b - 1))
            settle(sp, b)
            sp.dma_start(qs[4 * DH:SROWS, par, 8 * half:8 * half + 8, :], mneg[:, half, :]).then_inc(m_in[half], 16)

        @block.sync
        def _(sp):
            for c in range(4):
                sp.dma_start(X[:, 4 * c:4 * c + 4, :],
                             x[2 * c:2 * c + 2].rearrange("b (h p) d -> p (b h) d", p=P)).then_inc(x_in[c], 16)
            sp.dma_start(iv[:], inv).then_inc(iv_in, 16)
            sp.wait_ge(soft_ok, 1)
            for b in range(0, B, 2):
                rows = soft[b:b + 1, 193:194]
                src = bass.AP(rows.tensor, rows.offset, [list(rows.ap[0]), [1, S], [1, T]])
                sp.dma_start(circ[0:S, b // 2, :], src).then_inc(circ_in, 16)
            for i, par in steps(sp, -2, 8):
                if has(i + 1):
                    m_row(sp, i + 1, 1 - par, 0)
                if has(i + 2):
                    stack(sp, i + 2, par)
                if has(i + 1):
                    m_row(sp, i + 1, 1 - par, 1)
            for g in range(GROUPS):
                sp.wait_ge(sum_ok, g + 2)
                sp.dma_start(out[2 * g:2 * g + 2].rearrange("b (h p) d -> p (b h) d", p=P),
                             X[:, 4 * g:4 * g + 4, :]).then_inc(stored, 16)
            sp.wait_ge(stored, 16 * GROUPS)

        def negate(act, b, half):
            act.wait_ge(m_pe, 2 * b + half + 1)
            wait(act, m_in[half], 16 * b)
            act.activation(mneg[:, half, :], MISC[0:H // 2, 0:T], ACT.Copy, scale=-1.0).then_inc(m_neg, 1)

        def prep_act(act, b, u):
            if u == 3:
                act.wait_ge(prep_pe, 6 * b + 1)
                act.activation(hT[:], MISC[:, 0:T], ACT.Copy).then_inc(hT_sb, 1)
            if u == 5:
                act.wait_ge(prep_pe, 6 * b + 3)
                wait(act, latn_ok, TT * b)
                act.activation(lat[:].rearrange("p t l -> p (t l)"), MISC[:, 0:TT * L], ACT.Copy).then_inc(lat_sb, 1)
            if u == 6:
                act.wait_ge(prep_pe, 6 * b + 4)
                act.activation(latT[:], MISC[0:L, 0:T], ACT.Identity, bias=w2[0:L, LNB:LNB + 1],
                               scale=w2[0:L, LNG:LNG + 1]).then_inc(latT_sb, 1)

        @block.scalar
        def _(act):
            act.dma_start(w2[:], pack2).then_inc(w2_in, 16)
            act.dma_start(w3[:], pack3).then_inc(w3_in, 16)
            act.dma_start(w1[:], pack1).then_inc(w1_in, 16)
            act.dma_start(fk[:], dft_k).then_inc(fk_in, 16)
            act.dma_start(fx[:], dft_x).then_inc(fx_in, 16)
            for n in range(4):
                act.wait_ge(kdft_pe, n + 1)
                act.activation(kd[:, n, :], PS[:, 4 + n, :], ACT.Copy).then_inc(kdft_sb, 1)
            act.wait_ge(topk, 4)
            act.activation(work[:, 1, :], mean[:], ACT.Exp, bias=tot[:, 0:1]).then_inc(mean_exp, 1)
            act.wait_ge(soft_ok, 1)
            for b in range(1, B, 2):
                rows = soft[b:b + 1, 193:194]
                src = bass.AP(rows.tensor, rows.offset, [list(rows.ap[0]), [1, S], [1, T]])
                act.dma_start(circ[S:P, b // 2, :], src).then_inc(circ_in, 16)

            act.wait_ge(w2_in, 16)
            act.wait_ge(vst_ok, 3)
            for i, par in steps(act, -2, 8):
                for u in range(UNITS):
                    if has(i):
                        n = UNITS * i + u
                        act.wait_ge(sc_pe, n + 1)
                        wait(act, av_pe, n - RING + 1)
                        act.activation(probs[:, u % RING, :], EX[u % 2][:, 0:CHUNK],
                                       ACT.Exp, scale=SCALE).then_inc(exp_ok, 1)
                    if u == 0 and has(i):
                        negate(act, i, 1)
                    if u == 1 and has(i + 1):
                        b = i + 1
                        act.wait_ge(prep_pe, 6 * b + 6)
                        wait(act, av_pe, UNITS * (b - 1))
                        act.activation(blocks(vst[:, 1 - par], 0),
                                       MISC[:, 0:T].rearrange("p (n h d) -> p n h d", n=2 * TT, h=H // 2),
                                       ACT.Copy).then_inc(v_sb, 1)
                    if has(i + 2):
                        prep_act(act, i + 2, u)
                    if u == 6 and has(i + 1):
                        negate(act, i + 1, 0)

            for c in range(4):
                act.wait_ge(yT_pe, c + 1)
                act.activation(yT[:, 512 * c:512 * c + 512], PS[:, c, :], ACT.Copy).then_inc(yT_ok, 1)
            with act.Fori(0, GROUPS) as g:
                for e in range(E):
                    for k in range(HK):
                        act.wait_ge(hid_pe, 16 * g + HK * e + k + 1)
                        act.activation(hid[:, e % 2, k, :], PS[:, k, :], ACT.Relu,
                                       bias=w3[:, B1 + HK * e + k:B1 + HK * e + k + 1]).then_inc(hid_ok, 1)

        def mask(pool, n, u):
            p = probs[:, u % RING, :]
            pool.wait_ge(exp_ok, n + 1)
            settle(pool, n)
            for blocks in (p[:, 0:2 * T].rearrange("p (h q) -> p h q", h=2)[:, :, 0:P],
                           p[:, 2 * T:CHUNK].rearrange("p (h q) -> p h q", h=2)):
                pool.affine_select(out=blocks, in_=blocks, compare_op=ALU.is_ge, fill=0.0, base=0,
                                   pattern=[[0, 2], [1, P]], channel_multiplier=-1).then_inc(mask_ok, 1)

        @block.gpsimd
        def _(pool):
            pool.memset(ident[:], 0.0).then_inc(ids, 1)
            pool.memset(causal[:], 0.0).then_inc(ids, 1)
            pool.wait_ge(ids, 2)
            pool.affine_select(out=ident[:], in_=ident[:], compare_op=ALU.not_equal, fill=1.0, base=0,
                               pattern=[[-1, P]], channel_multiplier=1).then_inc(ids, 1)
            pool.affine_select(out=causal[:], in_=causal[:], compare_op=ALU.is_ge, fill=-1.0e30, base=0,
                               pattern=[[0, 4], [-1, P]], channel_multiplier=1).then_inc(ids, 1)
            pool.memset(half[:], -0.5).then_inc(consts, 1)
            pool.memset(kb[:], 0.0).then_inc(consts, 1)
            pool.memset(flat[:], 1.0 / D).then_inc(consts, 1)
            pool.wait_ge(consts, 3)
            for c in range(4):
                pool.wait_ge(stats_b, 4 * (c + 1))
                pool.tensor_scalar(rstd[:, 4 * c:4 * c + 4, 0:1], mv[:, 4 * c:4 * c + 4, 1:2], 1e-5, None,
                                   ALU.add).then_inc(var_eps, 1)
                pool.wait_ge(var_eps, c + 1)
                pool.tensor_tensor(rstd[:, 4 * c:4 * c + 4, 1:2], rstd[:, 4 * c:4 * c + 4, 0:1],
                                   half[:, 0:4].rearrange("p (a b) -> p a b", b=1), ALU.pow).then_inc(rstd_ok, 1)
            pool.wait_ge(w1_in, 16)
            for c in range(4):
                pool.wait_ge(x_in[c], 16)
                for t in range(4 * c, 4 * c + 4):
                    pool.tensor_tensor(XB[:, t, :], X[:, t, :], w1[:, BO:BO + D], ALU.add).then_inc(xb_ok, 1)

            for i, par in steps(pool, -2, 8):
                for u in range(UNITS):
                    if has(i):
                        mask(pool, UNITS * i + u, u)
                    if u == 1 and has(i + 2):
                        b = i + 2
                        pool.wait_ge(a_aggr, TT * (b + 1))
                        wait(pool, hs_ok, TT * b)
                        settle(pool, b)
                        pool.tensor_scalar(aeps[:, 0, :], amv[:, :, 1], LN_EPS, None, ALU.add).then_inc(a_eps, 1)
                        pool.tensor_scalar(aeps[:, 1, :], amv[:, :, 1], 1.0 + RMS_EPS, LN_EPS * RMS_EPS,
                                           ALU.mult, ALU.add).then_inc(a_eps, 1)
                        pool.wait_ge(a_eps, 2 * b + 2)
                        pool.tensor_tensor(ars[:], aeps[:], half[:, 0:2 * TT].rearrange("p (a b) -> p a b", b=TT),
                                           ALU.pow).then_inc(a_rstd, 1)
                    if u == 5 and has(i + 2):
                        b = i + 2
                        pool.wait_ge(l_aggr, TT * (b + 1))
                        wait(pool, latn_ok, TT * b)
                        settle(pool, b)
                        pool.tensor_scalar(leps[:], lmv[:, :, 1], LN_EPS, None, ALU.add).then_inc(l_eps, 1)
                        pool.wait_ge(l_eps, b + 1)
                        pool.tensor_tensor(lrs[:], leps[:], half[:, 0:TT], ALU.pow).then_inc(l_rstd, 1)
                    if u == 6 and has(i - 1):
                        b = i - 1
                        pool.wait_ge(x2_ok, b + 1)
                        settle(pool, b)
                        pool.tensor_tensor(tile_of(X, b, 0, TT), tile_of(X, b, 0, TT), tile_of(XN, b, 0, TT),
                                           ALU.add).then_inc(xs_ok, 1)

            pool.wait_ge(y_ok, 2)
            pool.tensor_scalar(sqe[:], ssq[:], 1.0 / D, RMS_EPS, ALU.mult, ALU.add).then_inc(y_ok, 1)
            pool.wait_ge(y_ok, 3)
            pool.tensor_tensor(rr[:], sqe[:], half[:, 0:NT], ALU.pow).then_inc(y_ok, 1)

        def scores(pe, b, par, u):
            n = UNITS * b + u
            if u == 0:
                pe.wait_ge(m_in[0], 16 * (b + 1))
            if u == 4:
                pe.wait_ge(m_in[1], 16 * (b + 1))
            wait(pe, exp_ok, n - 1)
            for j in range(2):
                pe.matmul(EX[u % 2][:, T * j:T * j + T], ks[:, par, 2 * u + j, 0:P],
                          qs[:, par, 2 * u + j, :], start=True, stop=True)
            for j in range(2):
                ins = pe.matmul(EX[u % 2][:, 2 * T + P * j:2 * T + P * j + P], ks[:, par, 2 * u + j, P:T],
                                qs[:, par, 2 * u + j, P:T], start=True, stop=True)
            ins.then_inc(sc_pe, 1)

        def weigh(pe, b, par, u):
            n = UNITS * b + u
            pe.wait_ge(mask_ok, 2 * n + 2)
            if u == 0:
                wait(pe, attn_ok, 2 * b)
                pe.wait_ge(v_sb, b + 1)
            for j in range(2):
                h = 2 * u + j
                out = AV[:, T * (h // 8):T * (h // 8) + T]
                pe.matmul(out, vst[:, par, 0, h, :], probs[:, u % RING, T * j:T * j + T], start=(h % 8 == 0),
                          stop=False, skip_group_check=True)
                ins = pe.matmul(out[:, P:T], vst[:, par, 1, h, :], probs[:, u % RING, 2 * T + P * j:2 * T + P * j + P],
                                start=False, stop=(h % 8 == 7), skip_group_check=True)
            ins.then_inc(av_pe, 1)

        def maxima(pe, b, par, v):
            n = MAXU * b + v
            if v == 0:
                pe.wait_ge(stack_in, 128 * (b + 1))
            wait(pe, max_ok, n - 1)
            bank = PS[:, 4 + v % 2, :]
            g, r = v // 3, v % 3
            rows = 4 * DH
            if r < 2:
                for j in range(2):
                    h = 4 * g + 2 * r + j
                    pe.matmul(bank[:, T * j:T * j + T], qs[0:rows, par, h, P:T], ks[0:rows, par, h, :],
                              start=(j == 0), stop=False, skip_group_check=True)
                ins = pe.matmul(bank.rearrange("p (h k) -> p h k", h=2)[:, :, P:T], identb[:], causal[:, 0:2, :],
                                start=False, stop=True, skip_group_check=True)
            else:
                for j in range(4):
                    h = 4 * g + j
                    pe.matmul(bank[:, P * j:P * j + P], qs[0:rows, par, h, 0:P], ks[0:rows, par, h, 0:P],
                              start=(j == 0), stop=False, skip_group_check=True)
                ins = pe.matmul(bank, identb[:], causal[:].rearrange("p a b -> p (a b)"),
                                start=False, stop=True, skip_group_check=True)
            ins.then_inc(max_pe, 1)

        def turn_maxima(pe, b, par, half):
            pe.wait_ge(max_ok, MAXU * b + (half + 1) * MAXU // 2)
            if half == 0 and has(b + 1):
                pe.wait_ge(latT_sb, b + 2)
            elif half == 0:
                pe.wait_ge(x2_ok, b - 1)
            elif has(b + 1):
                pe.wait_ge(k_tmp, b + 2)
            else:
                pe.wait_ge(m_neg, 2 * b + 1)
            for t in range(TT):
                ins = pe.transpose(MISC[0:H // 2, P * t:P * t + P], mx[:, par, t, 8 * half:8 * half + 8], ident[:])
            ins.then_inc(m_pe, 1)

        def prep_pe_step(pe, b, u):
            if u == 3:
                pe.wait_ge(hs_ok, TT * (b + 1))
                wait(pe, v_sb, b)
                wait(pe, x2_ok, b - 2)
                for t in range(TT):
                    ins = pe.transpose(MISC[:, P * t:P * t + P], hs[:, t, :], ident[:])
                ins.then_inc(prep_pe, 1)
            if u == 4:
                pe.wait_ge(hT_sb, b + 1)
                pe.matmul(MISC[:, 0:T], w2[:, WQ:WQ + P], hT[:], start=True, stop=True)
                pe.matmul(MISC[:, T:2 * T], w2[:, WQR:WQR + P], hT[:], start=True, stop=True).then_inc(prep_pe, 1)
            if u == 5:
                pe.wait_ge(q_tmp, b + 1)
                for t in range(TT):
                    ins = pe.matmul(MISC[:, L * t:L * t + L], hT[:, P * t:P * t + P], w2[:, WDKV:WDKV + L],
                                    start=True, stop=True)
                ins.then_inc(prep_pe, 1)
            if u == 6:
                pe.wait_ge(latn_ok, TT * (b + 1))
                settle(pe, b)
                for t in range(TT):
                    ins = pe.transpose(MISC[0:L, P * t:P * t + P], latn[:, t, :], ident[:])
                ins.then_inc(prep_pe, 1)
            if u == 7:
                pe.wait_ge(latT_sb, b + 1)
                wait(pe, m_neg, 2 * b - 1)
                pe.matmul(MISC[:, 0:T], w2[0:L, WUK:WUK + P], latT[:], start=True, stop=True)
                pe.matmul(MISC[:, T:2 * T], w2[0:L, WUKR:WUKR + P], latT[:], start=True,
                          stop=True).then_inc(prep_pe, 1)

        @block.tensor
        def _(pe):
            pe.wait_ge(w1_in, 16)
            pe.matmul(PS[:, 4, 0:129], w1[:, WKT:WKT + P], w1[:, WQB:WQB + 129], start=True, stop=True)
            pe.matmul(PS[:, 4, 129:257], w1[:, WVT:WVT + P], w1[:, WO:WO + P], start=True, stop=True).then_inc(fold_pe, 1)
            pe.wait_ge(bias_rows, 2)
            pe.matmul(PS[:, 5, 0:129], bkv[:, 0, :], w1[:, WQB:WQB + 129], start=True, stop=True)
            pe.matmul(PS[:, 5, 129:257], bkv[:, 1, :], w1[:, WO:WO + P], start=True, stop=True).then_inc(fold_pe, 1)
            pe.wait_ge(fold_sb, 2)
            for n in range(PAIRS):
                pe.matmul(PS[:, n, 0:257], w1[:, CTX + P * n:CTX + P * n + P], mn[:], start=True,
                          stop=True).then_inc(kqv_pe, 1)
            pe.wait_ge(kqv_sb, PAIRS)
            pe.wait_ge(fk_in, 16)
            for par in range(2):
                rows = slice(S * par, S * par + S)
                for f in range(2):
                    pe.matmul(PS[:, 4 + 2 * par + f, :].rearrange("p (a b) -> p a b", b=P),
                              fk[rows, P * f:P * f + P], kqv[rows, :, 0:P],
                              start=True, stop=True).then_inc(kdft_pe, 1)
            pe.wait_ge(fx_in, 16)
            for par in range(2):
                for f in range(2):
                    for h in range(TT):
                        pe.wait_ge(xn_ok, NT)
                        ins = pe.matmul(PS[:, 2 * par + f, :].rearrange("p (a b) -> p a b", b=P),
                                        fx[:, h, P * f:P * f + P],
                                        XN[:].rearrange("p (a c h) d -> p c h a d", c=2, h=2)[:, par, h],
                                        start=(h == 0), stop=(h == TT - 1))
                    ins.then_inc(xdft_pe, 1)
            pe.wait_ge(cross_ok, 4)
            pe.wait_ge(kqv_sb, PAIRS + 2)
            pe.wait_ge(iv_in, 16)
            pe.matmul(PS[0:B, 4, 0:T], cross[:, 0].rearrange("p a b -> p (a b)"), iv[:, 0, :], start=True, stop=False)
            pe.matmul(PS[0:B, 4, 0:T], cross[:, 1].rearrange("p a b -> p (a b)"), iv[:, 1, :], start=False, stop=False)
            pe.matmul(PS[0:B, 4, 0:T], kb[:].rearrange("p a b -> p (a b)"), flat[:], start=False,
                      stop=True).then_inc(mean_pe, 1)
            pe.wait_ge(prod_ok, 4)
            pe.wait_ge(circ_in, 16 * B)
            for b in range(B):
                rows = slice(S * (b % 2), S * (b % 2) + S)
                for h in range(TT):
                    at = T * (b // 2 % 2) + P * h
                    ins = pe.matmul(PS[:, 2 * (b % 2) + b // 4, at:at + P], circ[rows, b // 2, P * h:P * h + P],
                                    kqv[rows, b // 2, 129:257], start=True, stop=True)
                ins.then_inc(x1_pe, 1)

            pe.wait_ge(ids, 4)
            pe.wait_ge(vst_ok, 3)
            pe.wait_ge(w2_ok, 3)
            pe.wait_ge(x1_ok, 4)
            for i, par in steps(pe, -2, 8):
                for u in range(UNITS):
                    if has(i):
                        scores(pe, i, par, u)
                    if u >= 2 and has(i):
                        weigh(pe, i, par, u - 2)
                    if u < 2 and has(i - 1):
                        weigh(pe, i - 1, 1 - par, UNITS - 2 + u)
                    if u == 0 and has(i):
                        turn_maxima(pe, i, par, 1)
                    if u == 1 and has(i + 1):
                        b = i + 1
                        pe.wait_ge(k_tmp, b + 1)
                        wait(pe, m_neg, 2 * b)
                        for t in range(TT):
                            ins = pe.matmul(MISC[:, P * t:P * t + P], latT[:, P * t:P * t + P], w2[0:L, WUV:WUV + P],
                                            start=True, stop=True)
                        ins.then_inc(prep_pe, 1)
                    if u == 3 and has(i - 1):
                        b = i - 1
                        pe.wait_ge(attn_ok, 2 * b + 2)
                        if has(i + 1):
                            pe.wait_ge(v_sb, b + 3)
                        elif has(i):
                            pe.wait_ge(m_neg, 2 * b + 4)
                        else:
                            pe.wait_ge(x2_ok, b)
                        for t in range(TT):
                            ins = pe.matmul(MISC[:, P * t:P * t + P], attnT[:, P * t:P * t + P],
                                            w2[:, WOF:WOF + P], start=True, stop=True)
                        ins.then_inc(fin_pe, 1)
                    if has(i + 2):
                        prep_pe_step(pe, i + 2, u)
                    if u >= 2 and has(i + 1):
                        maxima(pe, i + 1, 1 - par, 2 * (u - 2))
                        maxima(pe, i + 1, 1 - par, 2 * (u - 2) + 1)
                    if u == 6 and has(i + 1):
                        turn_maxima(pe, i + 1, 1 - par, 0)

            pe.wait_ge(y_ok, 5)
            for c in range(4):
                for t in range(4):
                    ins = pe.transpose(PS[:, c, P * t:P * t + P], y[:, 4 * c + t, :], ident[:])
                ins.then_inc(yT_pe, 1)
            pe.wait_ge(w3_ok, 3)
            pe.wait_ge(yT_ok, 4)
            for t in range(NT):
                ins = pe.matmul(PS[:, 6, E * t:E * t + E], yT[:, P * t:P * t + P], w3[:, GATE:GATE + E],
                                start=True, stop=True)
            ins.then_inc(gate_pe, 1)
            with pe.Fori(0, GROUPS) as g:
                for e in range(E):
                    for k in range(HK):
                        at = W1 + HID * e + P * k
                        pe.wait_ge(hid_ok, 16 * g + HK * e + k) if k == 0 and e else None
                        pe.matmul(PS[:, k, :], w3[:, at:at + P], yT[:, bass.ds(512 * g, 512)], start=True,
                                  stop=True).then_inc(hid_pe, 1)
                    pe.wait_ge(hid_ok, 16 * g + HK * e + HK)
                    pe.wait_ge(tmp_ok, E * g + e + 1)
                    for t in range(4):
                        o = PS[:, 4 + e % 2, P * t:P * t + P]
                        for k in range(HK):
                            at = W2 + D * (HK * e + k)
                            pe.matmul(o, hid[:, e % 2, k, P * t:P * t + P], w3[:, at:at + D], start=(k == 0), stop=False)
                        ins = pe.matmul(o, ones[:], w3[0:1, B2 + D * e:B2 + D * e + D], start=False, stop=True)
                    ins.then_inc(out_pe, 1)

        def norm(dve, c):
            dve.wait_ge(rstd_ok, c + 1)
            for t in range(4 * c, 4 * c + 4):
                dve.tensor_scalar(XN[:, t, :], X[:, t, :], mv[:, t, 0:1], rstd[:, t, 1:2],
                                  ALU.subtract, ALU.mult).then_inc(xn_ok, 1)

        def rotate(dve, b, n, filled, tmp, total, high, done):
            dve.wait_ge(prep_pe, filled)
            dve.tensor_tensor(rope[:], MISC, w2[:, ROPE:ROPE + 512], ALU.mult).then_inc(tmp, 1)
            dve.wait_ge(tmp, b + 1)
            dve.tensor_tensor(qk[:], rope[:, 0:T], rope[:, T:2 * T], ALU.add).then_inc(total, 1)
            dve.wait_ge(total, b + 1)
            wait(dve, stack_in, 128 * b)
            dve.tensor_copy(parts[:, n, 0, :], qk[:]).then_inc(high, 1)
            dve.wait_ge(high, b + 1)
            dve.tensor_tensor(parts[:, n, 1, :], qk[:], parts[:, n, 0, :], ALU.subtract).then_inc(done, 1)

        def prep_dve(dve, b, u):
            if u == 0:
                for t in range(TT):
                    dve.bn_stats(ast[:, t, :], tile_of(X, b, t)).then_inc(a_stats, 1)
                for t in range(TT):
                    dve.wait_ge(a_stats, TT * b + t + 1)
                    settle(dve, b)
                    dve.bn_aggr(amv[:, t, :], ast[:, t, :]).then_inc(a_aggr, 1)
            if u == 2:
                dve.wait_ge(a_rstd, b + 1)
                wait(dve, prep_pe, 6 * b - 5)
                for t in range(TT):
                    dve.tensor_scalar(hs[:, t, :], tile_of(X, b, t), amv[:, t, 0:1], ars[:, 1, t:t + 1],
                                      ALU.subtract, ALU.mult).then_inc(hs_ok, 1)
                for t in range(TT):
                    dve.tensor_scalar(tile_of(XN, b, t), tile_of(X, b, t), amv[:, t, 0:1], ars[:, 0, t:t + 1],
                                      ALU.subtract, ALU.mult).then_inc(xn1_ok, 1)
            if u == 4:
                rotate(dve, b, 0, 6 * b + 2, q_tmp, q_sum, q_hi, q_ok)
            if u == 5:
                dve.wait_ge(lat_sb, b + 1)
                for t in range(TT):
                    dve.bn_stats(lst[:, t, :], lat[:, t, :]).then_inc(l_stats, 1)
                for t in range(TT):
                    dve.wait_ge(l_stats, TT * b + t + 1)
                    settle(dve, b)
                    dve.bn_aggr(lmv[:, t, :], lst[:, t, :]).then_inc(l_aggr, 1)
            if u == 6:
                dve.wait_ge(l_rstd, b + 1)
                for t in range(TT):
                    dve.tensor_scalar(latn[:, t, :], lat[:, t, :], lmv[:, t, 0:1], lrs[:, t:t + 1],
                                      ALU.subtract, ALU.mult).then_inc(latn_ok, 1)
            if u == 7:
                rotate(dve, b, 1, 6 * b + 5, k_tmp, k_sum, k_hi, k_ok)

        def row_max(dve, b, par, v):
            dve.wait_ge(max_pe, MAXU * b + v + 1)
            bank = PS[:, 4 + v % 2, :]
            g, r = v // 3, v % 3
            if r < 2:
                dve.tensor_reduce(mx[:, par, 1, 4 * g + 2 * r:4 * g + 2 * r + 2],
                                  bank.rearrange("p (h k) -> p h k", h=2), AX_X, ALU.max).then_inc(max_ok, 1)
            else:
                dve.tensor_reduce(mx[:, par, 0, 4 * g:4 * g + 4],
                                  bank.rearrange("p (h k) -> p h k", h=4), AX_X, ALU.max).then_inc(max_ok, 1)

        @block.vector
        def _(dve):
            dve.wait_ge(w2_in, 16)
            dve.tensor_scalar(w2[:, WQ:WDKV + L], w2[:, WQ:WDKV + L], w2[:, N1:N1 + 1], None,
                              ALU.mult).then_inc(w2_ok, 1)
            dve.memset(ks[4 * DH:SROWS], 1.0).then_inc(w2_ok, 1)
            dve.memset(vst[:], 0.0).then_inc(vst_ok, 1)
            dve.wait_ge(vst_ok, 1)
            for n in range(2):
                dve.memset(blocks(vst[:, n], P // 2), 1.0).then_inc(vst_ok, 1)
            dve.wait_ge(ids, 3)
            dve.tensor_copy(identb[:], ident[:]).then_inc(w2_ok, 1)
            dve.wait_ge(w1_in, 16)
            for n in range(2):
                dve.tensor_copy(bkv[:, n, :], w1[:, BKV + n:BKV + n + 1].broadcast_to([P, P])).then_inc(bias_rows, 1)
            for c in range(4):
                dve.wait_ge(x_in[c], 16)
                for t in range(4 * c, 4 * c + 4):
                    dve.bn_stats(bst[:, t, :], X[:, t, :]).then_inc(stats_a, 1)
                for t in range(4 * c, 4 * c + 4):
                    dve.wait_ge(stats_a, t + 1)
                    dve.bn_aggr(mv[:, t, :], bst[:, t, :]).then_inc(stats_b, 1)
                if c == 0:
                    dve.wait_ge(fold_pe, 1)
                    dve.tensor_copy(mn[:], PS[:, 4, 0:257]).then_inc(fold_sb, 1)
                    dve.wait_ge(fold_pe, 2)
                    dve.tensor_copy(biasbc[:], PS[:, 5, 0:257]).then_inc(fold_sb, 1)
                if c == 1:
                    dve.wait_ge(fold_sb, 2)
                    for n in range(PAIRS):
                        dve.wait_ge(kqv_pe, n + 1)
                        dve.tensor_tensor(kqv[:, n, :], PS[:, n, 0:257], biasbc[:], ALU.add).then_inc(kqv_sb, 1)
                    dve.wait_ge(kqv_sb, PAIRS)
                    dve.wait_ge(consts, 3)
                    for par in range(2):
                        rows = slice(S * par, S * par + S)
                        dve.tensor_copy(kb[rows, :, par:par + 1], kqv[rows, :, P:P + 1]).then_inc(kqv_sb, 1)
                if c >= 1:
                    norm(dve, c - 1)
            norm(dve, 3)
            for n in range(4):
                dve.wait_ge(xdft_pe, n + 1)
                dve.wait_ge(kdft_sb, n + 1)
                dve.tensor_tensor(prod[:, n, :], PS[:, n, :], kd[:, n, :], ALU.mult).then_inc(prod_ok, 1)
                dve.wait_ge(prod_ok, n + 1)
                dve.tensor_reduce(cross[:, n % 2, :, n // 2:n // 2 + 1], prod[:, n, :].rearrange("p (a b) -> p a b", b=P),
                                  AX_X, ALU.add).then_inc(cross_ok, 1)
            dve.memset(top[:, 16:24], LOWEST).then_inc(topk, 1)
            dve.wait_ge(mean_pe, 1)
            dve.tensor_copy(mean[:], PS[0:B, 4, 0:T]).then_inc(topk, 1)
            dve.wait_ge(topk, 2)
            dve.max(top[:, 0:8], mean[:]).then_inc(topk, 1)
            dve.wait_ge(topk, 3)
            dve.tensor_scalar(tot[:, 0:1], top[:, 0:1], -1.0, None, ALU.mult).then_inc(topk, 1)
            dve.match_replace(work[:, 0, :], top[:, 0:8], mean[:], LOWEST).then_inc(topk, 1)
            dve.wait_ge(topk, 5)
            dve.max(top[:, 8:16], work[:, 0, :]).then_inc(topk, 1)
            dve.wait_ge(topk, 6)
            dve.tensor_copy(top[:, 16:16 + TOPK - 8], top[:, 8:8 + TOPK - 8]).then_inc(topk, 1)
            dve.wait_ge(topk, 7)
            dve.match_replace(work[:, 0, :], top[:, 16:24], work[:, 0, :], LOWEST).then_inc(topk, 1)
            dve.wait_ge(topk, 8)
            dve.wait_ge(mean_exp, 1)
            dve.scalar_tensor_tensor(out=work[:, 0, :], in0=work[:, 0, :], scalar=0.99 * LOWEST, in1=work[:, 1, :],
                                     op0=ALU.is_le, op1=ALU.mult, accum_out=tot[:, 1:2]).then_inc(topk, 1)
            dve.wait_ge(topk, 9)
            dve.reciprocal(tot[:, 2:3], tot[:, 1:2]).then_inc(topk, 1)
            dve.wait_ge(topk, 10)
            dve.tensor_scalar(soft[:].rearrange("p (a b) -> p a b", a=2), work[:, 0:1, :].broadcast_to([B, 2, T]),
                              tot[:, 2:3], None, ALU.mult).then_inc(soft_ok, 1)
            dve.wait_ge(xb_ok, NT)
            for n in range(4):
                par, g = n % 2, n // 2
                dve.wait_ge(x1_pe, 4 * g + 3 + par)
                dve.tensor_tensor(tiles(X, par, g), PS[:, 2 * par + g, :].rearrange("p (a d) -> p a d", d=T),
                                  tiles(XB, par, g), ALU.add).then_inc(x1_ok, 1)
            dve.wait_ge(w3_in, 16)
            for a, n in ((W1, E * HID), (GATE, E)):
                dve.tensor_scalar(w3[:, a:a + n], w3[:, a:a + n], w2[:, N2:N2 + 1], None, ALU.mult).then_inc(w3_ok, 1)
            dve.memset(ones[:], 1.0).then_inc(w3_ok, 1)
            dve.wait_ge(x1_ok, 4)
            for i, par in steps(dve, -2, 8):
                for u in range(UNITS):
                    if has(i + 2):
                        prep_dve(dve, i + 2, u)
                    if u == 1 and has(i - 1):
                        b = i - 1
                        dve.wait_ge(av_pe, UNITS * (b + 1))
                        dve.reciprocal(rec[:], AV[P // 2:P, :]).then_inc(rec_ok, 1)
                        dve.wait_ge(rec_ok, b + 1)
                        for n in range(2):
                            dve.tensor_tensor(attnT[64 * n:64 * n + 64, :], AV[0:P // 2, T * n:T * n + T],
                                              rec[:, T * n:T * n + T], ALU.mult).then_inc(attn_ok, 1)
                    if u == 3 and has(i - 1):
                        b = i - 1
                        dve.wait_ge(fin_pe, b + 1)
                        dve.wait_ge(xn1_ok, TT * (b + 1))
                        dve.tensor_tensor(tile_of(XN, b, 0, TT), MISC[:, 0:T], tile_of(XN, b, 0, TT),
                                          ALU.add).then_inc(x2_ok, 1)
                    if u >= 2 and has(i + 1):
                        row_max(dve, i + 1, 1 - par, 2 * (u - 2))
                        row_max(dve, i + 1, 1 - par, 2 * (u - 2) + 1)
            dve.wait_ge(x2_ok, B)
            dve.tensor_tensor(y[:], XN[:], XN[:], ALU.mult).then_inc(y_ok, 1)
            dve.wait_ge(y_ok, 1)
            dve.tensor_reduce(ssq[:], y[:], AX_X, ALU.add).then_inc(y_ok, 1)
            dve.wait_ge(y_ok, 4)
            dve.tensor_tensor(y[:], XN[:], rr[:].rearrange("p (t d) -> p t d", d=1).broadcast_to([P, NT, D]),
                              ALU.mult).then_inc(y_ok, 1)
            dve.wait_ge(gate_pe, 1)
            dve.tensor_tensor(logit[:], PS[:, 6, 0:NT * E].rearrange("p (t e) -> p t e", e=E),
                              w3[:, GB:GB + E].rearrange("p (t e) -> p t e", t=1).broadcast_to([P, NT, E]),
                              ALU.add).then_inc(gate_ok, 1)
            dve.wait_ge(gate_ok, 1)
            dve.tensor_reduce(lead[:], logit[:], AX_X, ALU.max).then_inc(gate_ok, 1)
            dve.wait_ge(gate_ok, 2)
            dve.tensor_tensor(hit[:], logit[:], lead[:].broadcast_to([P, NT, E]), ALU.is_equal).then_inc(gate_ok, 1)
            for e in range(E):
                dve.memset(rank[:, :, e:e + 1], float(E - e)).then_inc(rank_ok, 1)
            dve.wait_ge(gate_ok, 3)
            dve.wait_ge(rank_ok, E)
            dve.tensor_tensor(logit[:], hit[:], rank[:], ALU.mult).then_inc(gate_ok, 1)
            dve.wait_ge(gate_ok, 4)
            dve.tensor_reduce(lead[:], logit[:], AX_X, ALU.max).then_inc(gate_ok, 1)
            dve.wait_ge(gate_ok, 5)
            dve.tensor_tensor(hit[:], rank[:], lead[:].broadcast_to([P, NT, E]), ALU.is_equal).then_inc(gate_ok, 1)
            dve.wait_ge(gate_ok, 6)
            dve.wait_ge(xs_ok, B)
            dve.sem_inc(tmp_ok, 2)
            dve.sem_inc(sum_ok, 1)
            with dve.Fori(0, GROUPS) as g:
                for e in range(E):
                    dve.wait_ge(out_pe, E * g + e + 1)
                    if e:
                        dve.wait_ge(acc_ok, E * g + e)
                    dst = tmp if e else acc
                    if e == 0:
                        dve.wait_ge(sum_ok, g + 1)
                    dve.tensor_tensor(dst[:], PS[:, 4 + e % 2, :].rearrange("p (t d) -> p t d", d=D),
                                      hit[:].rearrange("p t e -> p (t e)")[:, bass.ds(16 * g, 16)].rearrange(
                                          "p (t e) -> p t e", e=E)[:, :, e:e + 1].broadcast_to([P, 4, D]),
                                      ALU.mult).then_inc(tmp_ok, 1)
                    dve.wait_ge(tmp_ok, E * g + e + 3)
                    if e:
                        dve.tensor_tensor(acc[:], acc[:], tmp[:], ALU.add).then_inc(acc_ok, 1)
                    else:
                        dve.sem_inc(acc_ok, 1)
                dve.wait_ge(acc_ok, E * g + E)
                dve.tensor_tensor(tile_of(X, 2 * g, 0, 4), tile_of(X, 2 * g, 0, 4),
                                  acc[:].rearrange("p t d -> p (t d)"), ALU.add).then_inc(sum_ok, 1)


def fourier():
    t, f = np.arange(T), np.arange(T // 2)
    w = 2 * np.pi / T
    forth = np.concatenate([np.cos(w * np.outer(t, f)), np.cos(np.pi * t)[:, None],
                            -np.sin(w * np.outer(t, f[1:]))], 1)
    delay = (-t) % T
    back = np.concatenate([2 * np.cos(w * np.outer(f, delay)), np.cos(np.pi * delay)[None],
                           2 * np.sin(w * np.outer(f[1:], delay))], 0)
    back[0] = 1
    back /= T * D
    tiles = lambda a: np.ascontiguousarray(a.reshape(TT, P, T).transpose(1, 0, 2).astype(np.float32))
    short = forth[S - 1::-1]
    return tiles(forth), np.concatenate([short, short]).astype(np.float32), tiles(back)


def rotation():
    half = DH // 2
    freq = (1.0 / 10000.0 ** (np.arange(half, dtype=np.float32) / np.float32(half))).astype(np.float32)
    ang = (np.arange(T, dtype=np.float32)[:, None] * freq[None]).astype(np.float32)
    cos, sin = np.cos(ang), np.sin(ang)
    return (np.repeat(np.concatenate([cos, cos], 1).T, H, 0), np.repeat(np.concatenate([-sin, sin], 1).T, H, 0))


def kernel(**inputs):
    import concourse.bacc as bacc
    from concourse.bass_utils import run_bass_kernel_spmd

    a = {k: np.asarray(v) for k, v in inputs.items()}
    xa = lambda n: a["L0_xattn_" + n]
    ff = lambda n: a["L0_ffn_" + n]
    ctx_t = a["ctx_1024"][:, ::-1, :].reshape(PAIRS, 2 * S, D).transpose(2, 0, 1).reshape(D, PAIRS * 2 * S)
    pack1 = np.concatenate([xa("Wk").T, xa("Wv").T, xa("Wq").T, xa("bq")[:, None], xa("Wo"), xa("bk")[:, None],
                            xa("bv")[:, None], ctx_t, np.broadcast_to(xa("bo"), (P, D))], 1)
    rows = np.arange(D).reshape(H, DH)
    by_feature, partner = rows.T.reshape(D), np.roll(rows, DH // 2, axis=1).T.reshape(D)
    low = np.concatenate([ff("Wuk")[by_feature].T, ff("Wuk")[partner].T, ff("Wuv").T, ff("ln_g")[:, None],
                          ff("ln_b")[:, None]], 1)
    low = np.concatenate([low, low])
    pack2 = np.concatenate([ff("Wq")[by_feature].T, ff("Wq")[partner].T, ff("Wdkv").T, ff("Wo").T,
                            ff("norm1_w")[:, None], ff("norm2_w")[:, None], *rotation(), low], 1)
    w1 = ff("W1").transpose(2, 0, 1).reshape(D, E * HID)
    w2 = ff("W2").transpose(2, 0, 1).reshape(HK, P, E, D).transpose(1, 2, 0, 3).reshape(P, E * HK * D)
    b1 = ff("b1").reshape(E * HK, P).T
    b2 = np.broadcast_to(ff("b2").reshape(1, E * D), (P, E * D))
    pack3 = np.concatenate([w1, w2, b1, ff("gate_w").T, np.broadcast_to(ff("gate_b"), (P, E)), b2], 1)
    dft_x, dft_k, inv = fourier()
    arrays = {"x": a["x"], "pack1": pack1, "dft_x": dft_x, "dft_k": dft_k, "inv": inv, "pack2": pack2,
              "pack3": pack3}
    arrays = {k: np.ascontiguousarray(v) for k, v in arrays.items()}
    nc = bacc.Bacc("TRN2", target_bir_lowering=False, num_devices=1)
    aps = {k: nc.dram_tensor(k, v.shape, mybir.dt.from_np(v.dtype), kind="ExternalInput").ap()
           for k, v in arrays.items()}
    out = nc.dram_tensor("out", (B, T, D), F32, kind="ExternalOutput").ap()
    build(nc, out=out, **aps)
    res = run_bass_kernel_spmd(nc, [arrays], core_ids=[0])
    return res.results[0]["out"]
```

```python
from contextlib import ExitStack

import concourse.bass as bass
import numpy as np
from concourse import mybir

F32 = mybir.dt.float32
F16 = mybir.dt.float16
BF16 = mybir.dt.bfloat16
I32 = mybir.dt.int32
ALU = mybir.AluOpType
ACT = mybir.ActivationFunctionType
AX_X = mybir.AxisListType.X

P = 128
B, T, D = 8, 256, 128
S = 64
TT = T // P
NT = B * TT
PAIRS = B // 2
LN_EPS, RMS_EPS = 1e-5, 1e-6
TOPK = 11
WARM = 8
LOWEST = -3.0e38

WKT, WVT, WQB, WO, BKV, CTX, BO = 0, 128, 256, 385, 513, 515, 1027
PACK1 = BO + D

H, DH, L = 16, 8, 64
SCALE = float(DH) ** -0.5
SROWS = 4 * DH + 1
RING = 4
CHUNK = 2 * (T + P)
UNITS = H // 2
MAXU = 3 * H // 4
WQ, WQR, WDKV, WOF, N1, N2, ROPE = 0, 128, 256, 320, 448, 449, 450
WUK, WUKR, WUV, LNG, LNB = 962, 1090, 1218, 1346, 1347
PACK2 = 1348

E, HID = 4, 512
HK = HID // P
REGION = TT * B + 1
SLOTS = NT + E - 1
RING3 = 4
ROW = 2 * D + 1
NOWHERE = 2 * NT * P
W1, W2, TOKEN = 0, 2048, 4096
PACK3 = TOKEN + NT + 1
GATE, N2ROW, GB, RANK, EDGE, SLOT, SLOTP, B1, B2 = 0, 512, 640, 644, 648, 712, 731, 750, 2798
PACK4 = B2 + E * D


def build(nc, x, pack1, dft_x, dft_k, inv, pack2, pack3, pack4, sorted_rows, out):
    with ExitStack() as ctx:
        def sb(name, shape, dt=F32):
            return ctx.enter_context(nc.sbuf_tensor(name, shape, dt))

        def sem(name):
            return ctx.enter_context(nc.semaphore(name))

        PS = ctx.enter_context(nc.psum_tensor("PS", [P, 8, 512], F32))

        X = sb("X", [P, NT, D])
        XB = sb("XB", [P, NT, D])
        XN = sb("XN", [P, NT, D])
        w1 = sb("w1", [P, PACK1])
        fx = sb("fx", [P, TT, T])
        fk = sb("fk", [P, T])
        iv = sb("iv", [P, TT, T])
        bst = sb("bst", [P, NT, 6])
        mv = sb("mv", [P, NT, 2])
        rstd = sb("rstd", [P, NT, 2])
        half = sb("half", [P, 2 * NT])
        bkv = sb("bkv", [P, 2, P])
        mn = sb("mn", [P, 257])
        biasbc = sb("biasbc", [P, 257])
        kqv = sb("kqv", [P, PAIRS, 257])
        kb = sb("kb", [P, PAIRS, 2])
        flat = sb("flat", [P, T])
        kd = sb("kd", [P, 4, 512])
        prod = sb("prod", [P, 4, 512])
        cross = sb("cross", [P, 2, PAIRS, 2])
        mean = sb("mean", [B, T])
        top = sb("top", [B, 24])
        work = sb("work", [B, 2, T])
        soft = sb("soft", [B, 2 * T])
        tot = sb("tot", [B, 4])
        circ = sb("circ", [P, PAIRS, T])

        def tiles(a, par, g):
            return a[:].rearrange("p (g a c h) d -> p g c a (h d)", a=2, c=2, h=TT)[:, g, par]

        w2 = sb("w2", [P, PACK2])
        ident = sb("ident", [P, P])
        identb = sb("identb", [P, P], BF16)
        ones16 = sb("ones16", [P, 2 * H * T // P], F16)
        causal = sb("causal", [P, 4, P], BF16)
        ast = sb("ast", [P, TT, 6])
        amv = sb("amv", [P, TT, 2])
        aeps = sb("aeps", [P, 2, TT])
        ars = sb("ars", [P, 2, TT])
        nbias = sb("nbias", [P, 2, TT])
        hs = sb("hs", [P, TT, D])
        hT = sb("hT", [P, T])
        rope = sb("rope", [P, 512])
        qk = sb("qk", [P, T])
        parts = sb("parts", [P, 2, 2, T], F16)
        lat = sb("lat", [P, TT, L])
        lst = sb("lst", [P, TT, 6])
        lmv = sb("lmv", [P, TT, 2])
        leps = sb("leps", [P, TT])
        lrs = sb("lrs", [P, TT])
        latn = sb("latn", [P, TT, L])
        latT = sb("latT", [L, T])
        vst = sb("vst", [P, 2, TT, H, P])
        qs = sb("qs", [SROWS, 2, H, T], F16)
        ks = sb("ks", [SROWS, 2, H, T], F16)
        mx = sb("mx", [P, 2, TT, H])
        mneg = sb("mneg", [H // 2, 2, T], F16)
        probs = sb("probs", [P, RING, CHUNK])
        avs = sb("avs", [P, 2 * T])
        rec = sb("rec", [P // 2, 2 * T])
        attnT = sb("attnT", [P, T])
        EX = [PS[:, 2 * n:2 * n + 2, :].rearrange("p a b -> p (a b)") for n in range(2)]
        AV = PS[:, 6, :]

        def blocks(a, first):
            return bass.AP(a.tensor, a.offset + first, [list(a.ap[0]), [P * H // 2, 2 * TT], [P + DH, H // 2], [1, DH]])

        MISC = PS[:, 7, :]

        def tile_of(a, b, t=0, n=1):
            return a[:].rearrange("p n d -> p (n d)")[:, bass.ds(b * T + t * P, n * P)]

        ones_ok, ones_in = sem("ones_ok"), sem("ones_in")
        settled = sem("settled")
        w3 = sb("w3", [P, PACK3])
        w4 = sb("w4", [P, PACK4])
        tri = sb("tri", [P, P], BF16)
        onesb = sb("onesb", [P, P], BF16)
        blank = sb("blank", [P, ROW])
        rows = sb("rows", [P, 2, TT, ROW])
        sq = sb("sq", [P, TT, P], BF16)
        ssq = sb("ssq", [P, TT])
        sqe = sb("sqe", [P, TT])
        rr = sb("rr", [P, TT])
        dot = sb("dot", [P, TT, E, D], BF16)
        logit = sb("logit", [P, TT, E])
        lead = sb("lead", [P, TT, 1])
        tied = sb("tied", [P, TT, E])
        hit = sb("hit", [P, TT, E], BF16)
        cum = sb("cum", [P, E], BF16)
        place = sb("place", [P, TT, E])
        pos = sb("pos", [P, 2, TT], I32)
        pad_at = sb("pad_at", [1, E], I32)
        full = sb("full", [1, E, NT])
        count = sb("count", [1, E])
        ends = sb("ends", [1, E])
        beyond = sb("beyond", [1, SLOTS, E])
        skip = sb("skip", [1, SLOTS, E])
        shift = sb("shift", [1, E])
        base = sb("base", [1, SLOTS])
        chosen = sb("chosen", [1, SLOTS])
        slot_row = sb("slot_row", [1, SLOTS], I32)
        slot_w = sb("slot_w", [1, SLOTS], I32)
        slot_b = sb("slot_b", [1, SLOTS], I32)
        late, used = vst[:].rearrange("p a t h c -> p (a t h c)"), 0

        def view(*shape):
            nonlocal used
            n = int(np.prod(shape))
            used += n
            names = "abc"[:len(shape)]
            dims = {c: m for c, m in zip(names, shape)}
            return late[:, used - n:used].rearrange(f"p ({' '.join(names)}) -> p {' '.join(names)}", **dims)

        srt = view(RING3, ROW)
        yT, hb, hT3, res, fin = view(2, D), view(2, HID), view(2, HK, P), view(2, D), view(2, D)
        where = sb("where", [P, 2], I32)
        w3_in, w3_ok, w4_in, w4_ok, blank_ok = (sem(n) for n in ("w3_in", "w3_ok", "w4_in", "w4_ok", "blank_ok"))
        ssq_ok, sqe_ok, rr_ok, xs_ok, rows_ok, logit_ok, choice, hit_ok, place_pe, place_ok, pos_ok, cum_ok = (
            sem(n) for n in ("ssq_ok", "sqe_ok", "rr_ok", "xs_ok", "rows_ok", "logit_ok", "choice", "hit_ok",
                             "place_pe", "place_ok", "pos_ok", "cum_ok"))
        sent, pad_in = [sem("sent0"), sem("sent1")], sem("pad_in")
        total_pe, table, slots_ok = sem("total_pe"), sem("table"), sem("slots_ok")
        srt_in = [sem(f"srt_in{k}") for k in range(RING3)]
        yT_pe, yT_sb, hid_pe, hb_ok, hT_pe, relu_ok, out_pe, res_ok, where_ok, fin_ok = (sem(n) for n in (
            "yT_pe", "yT_sb", "hid_pe", "hb_ok", "hT_pe", "relu_ok", "out_pe", "res_ok", "where_ok", "fin_ok"))
        put = [sem("put0"), sem("put1")]
        w2_in, ids, w2_ok = sem("w2_in"), sem("ids"), sem("w2_ok")
        a_stats, a_aggr, a_eps, a_rstd, hs_ok, xn1_ok = (sem(n) for n in (
            "a_stats", "a_aggr", "a_eps", "a_rstd", "hs_ok", "xn1_ok"))
        prep_pe, hT_sb, q_tmp, q_sum, q_hi, q_ok = (sem(n) for n in (
            "prep_pe", "hT_sb", "q_tmp", "q_sum", "q_hi", "q_ok"))
        lat_sb, l_stats, l_aggr, l_eps, l_rstd, latn_ok, latT_sb = (sem(n) for n in (
            "lat_sb", "l_stats", "l_aggr", "l_eps", "l_rstd", "latn_ok", "latT_sb"))
        k_tmp, k_sum, k_hi, k_ok, v_sb = (sem(n) for n in ("k_tmp", "k_sum", "k_hi", "k_ok", "v_sb"))
        stack_in, m_in = sem("stack_in"), [sem("m_in0"), sem("m_in1")]
        max_pe, max_ok, m_pe, m_neg = sem("max_pe"), sem("max_ok"), sem("m_pe"), sem("m_neg")
        sc_pe, exp_ok, mask_ok, av_pe = sem("sc_pe"), sem("exp_ok"), sem("mask_ok"), sem("av_pe")
        rec_ok, attn_ok, fin_pe, x2_ok, vst_ok = (sem(n) for n in (
            "rec_ok", "attn_ok", "fin_pe", "x2_ok", "vst_ok"))
        av_sb, nbias_ok = sem("av_sb"), sem("nbias_ok")

        x_in = [sem(f"x_in{c}") for c in range(4)]
        w1_in, fx_in, fk_in, iv_in = sem("w1_in"), sem("fx_in"), sem("fk_in"), sem("iv_in")
        stats_a, stats_b, var_eps, rstd_ok, xn_ok, xb_ok = (sem(n) for n in (
            "stats_a", "stats_b", "var_eps", "rstd_ok", "xn_ok", "xb_ok"))
        consts, bias_rows = sem("consts"), sem("bias_rows")
        fold_pe, fold_sb, kqv_pe, kqv_sb = sem("fold_pe"), sem("fold_sb"), sem("kqv_pe"), sem("kqv_sb")
        kdft_pe, kdft_sb, xdft_pe, prod_ok, cross_ok = (sem(n) for n in (
            "kdft_pe", "kdft_sb", "xdft_pe", "prod_ok", "cross_ok"))
        mean_pe, topk, mean_exp_in, mean_exp, soft_ok, x1_pe, x1_ok = (sem(n) for n in (
            "mean_pe", "topk", "mean_exp_in", "mean_exp", "soft_ok", "x1_pe", "x1_ok"))
        circ_in = [sem(f"circ_in{b}") for b in range(B)]
        block = ctx.enter_context(nc.Block())

        def table_of(eng, table, first, n, most):
            return nc.values_load_multi_w_load_instructions(
                table[0:1, bass.ds(first, n)], engines=[eng.engine], min_val=0, max_val=most,
                skip_runtime_bounds_check_because="the table's entries are made from counts of tokens")[1]

        def has(b):
            return not isinstance(b, int) or 0 <= b < B

        def steps(eng, first, last):
            for i in range(first, 2):
                yield i, i % 2
            with eng.Fori(1, 3) as pair:
                yield 2 * pair, 0
                yield 2 * pair + 1, 1
            for i in range(6, last + 1):
                yield i, i % 2

        def slots(eng):
            for k in range(RING3):
                yield 0, k
            with eng.Fori(1, SLOTS // RING3) as q:
                for k in range(RING3):
                    yield q, k
            for k in range(SLOTS % RING3):
                yield SLOTS // RING3, k

        def wait(eng, s, value):
            if not isinstance(value, int) or value > 0:
                eng.wait_ge(s, value)

        def settle(eng, b):
            if not isinstance(b, int):
                eng.sem_inc(settled, 1)

        def stack(sp, b, par):
            wait(sp, sc_pe, UNITS * (b - 1))
            settle(sp, b)
            for n, done, dst in ((0, q_ok, qs), (1, k_ok, ks)):
                sp.wait_ge(done, b + 1)
                settle(sp, b)
                for c in range(4):
                    part = c // 2 if n == 0 else c % 2
                    sp.dma_start(dst[DH * c:DH * c + DH, par, :, :], parts[:, n, part, :]).then_inc(stack_in, 16)

        def m_row(sp, b, par, half):
            sp.wait_ge(m_neg, 2 * b + half + 1)
            settle(sp, b)
            wait(sp, sc_pe, UNITS * (b - 1))
            settle(sp, b)
            sp.dma_start(qs[4 * DH:SROWS, par, 8 * half:8 * half + 8, :], mneg[:, half, :]).then_inc(m_in[half], 16)

        def pad(eng, half):
            eng.wait_ge(slots_ok, 1)
            for at in table_of(eng, pad_at, half * E // 2, E // 2, (REGION * E - 1) * P):
                eng.dma_start(sorted_rows[bass.ds(at, P)], blank[:]).then_inc(pad_in, 16)

        @block.sync
        def _(sp):
            for c in range(4):
                sp.dma_start(X[:, 4 * c:4 * c + 4, :],
                             x[2 * c:2 * c + 2].rearrange("b (h p) d -> p (b h) d", p=P)).then_inc(x_in[c], 16)
            sp.dma_start(iv[:], inv).then_inc(iv_in, 16)
            sp.wait_ge(ones_ok, 1)
            sp.dma_start(ks[4 * DH:SROWS, :, :, :], ones16[:]).then_inc(ones_in, 16)
            sp.wait_ge(soft_ok, 1)
            for b in range(0, B, 2):
                run = soft[b:b + 1, 193:194]
                src = bass.AP(run.tensor, run.offset, [list(run.ap[0]), [1, S], [1, T]])
                sp.dma_start(circ[0:S, b // 2, :], src).then_inc(circ_in[b], 16)
            sp.wait_ge(blank_ok, 2)
            for n in range(E - 1):
                at = (REGION * E + n) * P
                sp.dma_start(sorted_rows[at:at + P], blank[:]).then_inc(pad_in, 16)
            for i, par in steps(sp, -2, 8):
                if has(i + 1):
                    m_row(sp, i + 1, 1 - par, 0)
                if has(i + 2):
                    stack(sp, i + 2, par)
                if has(i + 1):
                    m_row(sp, i + 1, 1 - par, 1)
            pad(sp, 0)
            for n in range(2):
                sp.wait_ge(sent[n], 16 * NT // 2)
            sp.wait_ge(pad_in, 16 * (E + E - 1))
            sp.wait_ge(slots_ok, 4)
            for q, k in slots(sp):
                s = RING3 * q + k
                at = sp.value_load(slot_row[0:1, bass.ds(s, 1)], min_val=0, max_val=(REGION * E + E - 2) * P)
                if not isinstance(q, int) or q:
                    sp.wait_ge(yT_pe, s - RING3 + 1)
                    sp.wait_ge(res_ok, s - RING3 + 1)
                    sp.wait_ge(where_ok, s - RING3 + 1)
                sp.dma_start(srt[:, k, :], sorted_rows[bass.ds(at, P)]).then_inc(srt_in[k], 16)
            for n in range(2):
                sp.wait_ge(put[n], 16 * ((SLOTS + 1 - n) // 2))

        def negate(act, b, half):
            act.wait_ge(m_pe, 2 * b + half + 1)
            wait(act, m_in[half], 16 * b)
            act.activation(mneg[:, half, :], MISC[0:H // 2, 0:T], ACT.Copy, scale=-1.0).then_inc(m_neg, 1)

        def high_half(act, b, n, total, high):
            act.wait_ge(total, b + 1)
            wait(act, stack_in, 128 * b)
            act.activation(parts[:, n, 0, :], qk[:], ACT.Copy).then_inc(high, 1)

        def prep_act(act, b, u):
            if u == 2:
                act.wait_ge(nbias_ok, b + 1)
                wait(act, prep_pe, 6 * b - 5)
                settle(act, b)
                for n, to, done in ((1, lambda t: hs[:, t, :], hs_ok), (0, lambda t: tile_of(XN, b, t), xn1_ok)):
                    for t in range(TT):
                        act.activation(to(t), tile_of(X, b, t), ACT.Identity, bias=nbias[:, n, t:t + 1],
                                       scale=ars[:, n, t:t + 1]).then_inc(done, 1)
            if u == 3:
                act.wait_ge(prep_pe, 6 * b + 1)
                act.activation(hT[:], MISC[:, 0:T], ACT.Copy).then_inc(hT_sb, 1)
            if u == 4:
                act.wait_ge(prep_pe, 6 * b + 2)
                wait(act, latn_ok, TT * b)
                act.activation(lat[:].rearrange("p t l -> p (t l)"), MISC[:, 0:TT * L], ACT.Copy).then_inc(lat_sb, 1)
            if u == 5:
                high_half(act, b, 0, q_sum, q_hi)
            if u == 7:
                high_half(act, b, 1, k_sum, k_hi)
            if u == 6:
                act.wait_ge(prep_pe, 6 * b + 4)
                act.activation(latT[:], MISC[0:L, 0:T], ACT.Identity, bias=w2[0:L, LNB:LNB + 1],
                               scale=w2[0:L, LNG:LNG + 1]).then_inc(latT_sb, 1)

        @block.scalar
        def _(act):
            act.dma_start(w1[:], pack1).then_inc(w1_in, 16)
            act.dma_start(fk[:], dft_k).then_inc(fk_in, 16)
            act.dma_start(fx[:], dft_x).then_inc(fx_in, 16)
            act.dma_start(w2[:], pack2).then_inc(w2_in, 16)
            act.dma_start(w3[:], pack3).then_inc(w3_in, 16)
            act.dma_start(w4[:], bass.AP(pack4.tensor, pack4.offset, [[0, P], [1, PACK4]])).then_inc(w4_in, 16)
            for n in range(4):
                act.wait_ge(kdft_pe, n + 1)
                act.activation(kd[:, n, :], PS[:, 4 + n, :], ACT.Copy).then_inc(kdft_sb, 1)
            act.wait_ge(topk, 4)
            act.activation(work[:, 1, :], mean[:], ACT.Exp, bias=tot[:, 0:1]).then_inc(mean_exp, 1)
            act.wait_ge(soft_ok, 1)
            for b in range(1, B, 2):
                run = soft[b:b + 1, 193:194]
                src = bass.AP(run.tensor, run.offset, [list(run.ap[0]), [1, S], [1, T]])
                act.dma_start(circ[S:P, b // 2, :], src).then_inc(circ_in[b], 16)

            act.wait_ge(w2_in, 16)
            act.wait_ge(vst_ok, 3)
            for i, par in steps(act, -2, 9):
                for u in range(UNITS):
                    if has(i):
                        n = UNITS * i + u
                        act.wait_ge(sc_pe, n + 1)
                        wait(act, av_pe, n - RING + 1)
                        act.activation(probs[:, u % RING, :], EX[u % 2][:, 0:CHUNK],
                                       ACT.Exp, scale=SCALE).then_inc(exp_ok, 1)
                    if u == 1 and has(i):
                        negate(act, i, 1)
                    if u == 0 and has(i - 2):
                        b = i - 2
                        act.wait_ge(rr_ok, b + 1)
                        wait(act, sent[par], 16 * (b - par))
                        settle(act, b)
                        for t in range(TT):
                            act.activation(rows[:, par, t, 0:D], tile_of(XN, b, t), ACT.Copy,
                                           scale=rr[:, t:t + 1]).then_inc(rows_ok, 1)
                    if u == 2 and has(i + 1):
                        b = i + 1
                        act.wait_ge(prep_pe, 6 * b + 6)
                        wait(act, av_pe, UNITS * (b - 1))
                        act.activation(blocks(vst[:, 1 - par], 0),
                                       MISC[:, 0:T].rearrange("p (n h d) -> p n h d", n=2 * TT, h=H // 2),
                                       ACT.Copy).then_inc(v_sb, 1)
                    if u == 1 and has(i - 1):
                        b = i - 1
                        act.wait_ge(av_pe, UNITS * (b + 1))
                        wait(act, attn_ok, 2 * b)
                        act.activation(avs[:], AV, ACT.Copy).then_inc(av_sb, 1)
                    if has(i + 2):
                        prep_act(act, i + 2, u)
                    if u == 6 and has(i + 1):
                        negate(act, i + 1, 0)
                    if u == (7 if has(i) else 1) and has(i - 1):
                        b = i - 1
                        act.wait_ge(x2_ok, b + 1)
                        wait(act, sqe_ok, b)
                        settle(act, b)
                        for t in range(TT):
                            act.activation(sq[:, t, :], tile_of(XN, b, t), ACT.Square,
                                           accum_out=ssq[:, t:t + 1]).then_inc(ssq_ok, 1)

            pad(act, 1)

            def features(s, par):
                act.wait_ge(yT_pe, s + 1)
                wait(act, hid_pe, s - 1)
                act.activation(yT[:, par, :], PS[:, 0, 0:P], ACT.Copy).then_inc(yT_sb, 1)

            features(0, 0)
            features(1, 1)
            for q, k in slots(act):
                s, par = RING3 * q + k, k % 2
                act.wait_ge(hT_pe, s + 1)
                wait(act, out_pe, s - 1)
                act.activation(hT3[:, par], PS[:, 3 + par, :].rearrange("p (a b) -> p a b", a=HK),
                               ACT.Relu).then_inc(relu_ok, 1)
                if not isinstance(s, int) or s + 2 < SLOTS:
                    features(s + 2, par)

        def mask(pool, n, u):
            p = probs[:, u % RING, :]
            pool.wait_ge(exp_ok, n + 1)
            settle(pool, n)
            for blocks in (p[:, 0:2 * T].rearrange("p (h q) -> p h q", h=2)[:, :, 0:P],
                           p[:, 2 * T:CHUNK].rearrange("p (h q) -> p h q", h=2)):
                pool.affine_select(out=blocks, in_=blocks, compare_op=ALU.is_ge, fill=0.0, base=0,
                                   pattern=[[0, 2], [1, P]], channel_multiplier=-1).then_inc(mask_ok, 1)

        @block.gpsimd
        def _(pool):
            pool.memset(ident[:], 0.0).then_inc(ids, 1)
            pool.memset(causal[:], 0.0).then_inc(ids, 1)
            pool.wait_ge(ids, 2)
            pool.affine_select(out=ident[:], in_=ident[:], compare_op=ALU.not_equal, fill=1.0, base=0,
                               pattern=[[-1, P]], channel_multiplier=1).then_inc(ids, 1)
            pool.affine_select(out=causal[:], in_=causal[:], compare_op=ALU.is_ge, fill=-1.0e30, base=0,
                               pattern=[[0, 4], [-1, P]], channel_multiplier=1).then_inc(ids, 1)
            pool.memset(ones16[:], 1.0).then_inc(ones_ok, 1)
            pool.memset(half[:], -0.5).then_inc(consts, 1)
            pool.memset(kb[:], 0.0).then_inc(consts, 1)
            pool.memset(flat[:], 1.0 / D).then_inc(consts, 1)
            pool.wait_ge(consts, 3)
            pool.memset(vst[:], 0.0).then_inc(vst_ok, 1)
            pool.wait_ge(vst_ok, 1)
            for n in range(2):
                pool.memset(blocks(vst[:, n], P // 2), 1.0).then_inc(vst_ok, 1)
            for c in range(4):
                pool.wait_ge(stats_b, 4 * (c + 1))
                pool.tensor_scalar(rstd[:, 4 * c:4 * c + 4, 0:1], mv[:, 4 * c:4 * c + 4, 1:2], 1e-5, None,
                                   ALU.add).then_inc(var_eps, 1)
                pool.wait_ge(var_eps, c + 1)
                pool.tensor_tensor(rstd[:, 4 * c:4 * c + 4, 1:2], rstd[:, 4 * c:4 * c + 4, 0:1],
                                   half[:, 0:4].rearrange("p (a b) -> p a b", b=1), ALU.pow).then_inc(rstd_ok, 1)
            pool.wait_ge(w1_in, 16)
            for c in range(4):
                pool.wait_ge(x_in[c], 16)
                for t in range(4 * c, 4 * c + 4):
                    pool.tensor_tensor(XB[:, t, :], X[:, t, :], w1[:, BO:BO + D], ALU.add).then_inc(xb_ok, 1)
            pool.memset(tri[:], 1.0).then_inc(w4_ok, 1)
            pool.memset(onesb[:], 1.0).then_inc(w4_ok, 1)
            for e in range(E):
                pool.memset(cum[:, e:e + 1], float(REGION * e)).then_inc(w4_ok, 1)
            pool.wait_ge(w4_ok, 1)
            pool.affine_select(out=tri[:], in_=tri[:], compare_op=ALU.is_gt, fill=0.0, base=0,
                               pattern=[[1, P]], channel_multiplier=-1).then_inc(w4_ok, 1)
            pool.memset(blank[:, 0:2 * D], 0.0).then_inc(blank_ok, 1)
            pool.wait_ge(w2_in, 16)
            pool.wait_ge(w3_in, 16)
            pool.tensor_copy(blank[:, 2 * D:ROW], w3[:, TOKEN + NT:TOKEN + NT + 1]).then_inc(blank_ok, 1)
            pool.tensor_scalar(w3[:, W1:W1 + E * HID], w3[:, W1:W1 + E * HID], w2[:, N2:N2 + 1], None,
                               ALU.mult).then_inc(w3_ok, 1)
            pool.wait_ge(w4_in, 16)
            gate = w4[:, GATE:GATE + E * D].rearrange("p (e d) -> p e d", e=E)
            pool.tensor_tensor(gate, gate, w4[:, N2ROW:N2ROW + D].rearrange("p (e d) -> p e d", e=1).broadcast_to(
                [P, E, D]), ALU.mult).then_inc(w4_ok, 1)

            for i, par in steps(pool, -2, 9):
                for u in range(UNITS):
                    if has(i):
                        mask(pool, UNITS * i + u, u)
                    if u == 1 and has(i + 2):
                        b = i + 2
                        pool.wait_ge(a_aggr, TT * (b + 1))
                        wait(pool, hs_ok, TT * b)
                        wait(pool, xn1_ok, TT * b)
                        settle(pool, b)
                        pool.tensor_scalar(aeps[:, 0, :], amv[:, :, 1], LN_EPS, None, ALU.add).then_inc(a_eps, 1)
                        pool.tensor_scalar(aeps[:, 1, :], amv[:, :, 1], 1.0 + RMS_EPS, LN_EPS * RMS_EPS,
                                           ALU.mult, ALU.add).then_inc(a_eps, 1)
                        pool.wait_ge(a_eps, 2 * b + 2)
                        pool.tensor_tensor(ars[:], aeps[:], half[:, 0:2 * TT].rearrange("p (a b) -> p a b", b=TT),
                                           ALU.pow).then_inc(a_rstd, 1)
                    if u == 4 and has(i + 2):
                        b = i + 2
                        pool.wait_ge(l_aggr, TT * (b + 1))
                        wait(pool, latn_ok, TT * b)
                        settle(pool, b)
                        pool.tensor_scalar(leps[:], lmv[:, :, 1], LN_EPS, None, ALU.add).then_inc(l_eps, 1)
                        pool.wait_ge(l_eps, b + 1)
                        pool.tensor_tensor(lrs[:], leps[:], half[:, 0:TT], ALU.pow).then_inc(l_rstd, 1)
                    if u == (7 if has(i) else 0) and has(i - 1):
                        b, n = i - 1, 1 - par
                        pool.wait_ge(ssq_ok, TT * b + TT)
                        wait(pool, rr_ok, b)
                        settle(pool, b)
                        pool.tensor_scalar(sqe[:], ssq[:], 1.0 / D, RMS_EPS, ALU.mult, ALU.add).then_inc(sqe_ok, 1)
                        pool.wait_ge(sqe_ok, b + 1)
                        wait(pool, rows_ok, TT * b)
                        settle(pool, b)
                        pool.tensor_tensor(rr[:], sqe[:], half[:, 0:TT], ALU.pow).then_inc(rr_ok, 1)
                        pool.wait_ge(x2_ok, b + 1)
                        wait(pool, sent[n], 16 * (b - n))
                        settle(pool, b)
                        for t in range(TT):
                            pool.tensor_tensor(rows[:, n, t, D:2 * D], tile_of(X, b, t), tile_of(XN, b, t),
                                               ALU.add).then_inc(xs_ok, 1)
                        pool.tensor_copy(rows[:, n, :, 2 * D], w3[:, bass.ds(TT * b + TOKEN, TT)]).then_inc(xs_ok, 1)
                    if u == 3 and has(i - 2):
                        b = i - 2
                        pool.wait_ge(pos_ok, b + 1)
                        pool.wait_ge(xs_ok, (TT + 1) * (b + 1))
                        settle(pool, b)
                        for t in range(TT):
                            pool.indirect_dma_start(sorted_rows, bass.IndirectOffsetOnAxis(ap=pos[:, par, t:t + 1], axis=0),
                                                    rows[:, par, t, :], None).then_inc(sent[par], 16)

            pool.wait_ge(slots_ok, 4)

            def residual(q, k):
                s, par = RING3 * q + k, k % 2
                at = pool.value_load(slot_b[0:1, bass.ds(s, 1)], min_val=0, max_val=D * (E - 1))
                pool.wait_ge(srt_in[k], 16 * (q + 1))
                wait(pool, fin_ok, s - 1)
                settle(pool, s)
                pool.tensor_tensor(res[:, par, :], srt[:, k, D:2 * D], w4[:, bass.ds(at + B2, D)],
                                   ALU.add).then_inc(res_ok, 1)

            residual(0, 0)
            for q, k in slots(pool):
                s, par = RING3 * q + k, k % 2
                if not isinstance(s, int) or s + 1 < SLOTS:
                    residual(q + (k + 1) // RING3, (k + 1) % RING3)
                pool.wait_ge(fin_ok, s + 1)
                settle(pool, s)
                pool.indirect_dma_start(out.rearrange("b t d -> (b t) d"),
                                        bass.IndirectOffsetOnAxis(ap=where[:, par:par + 1], axis=0), fin[:, par, :],
                                        None, bounds_check=NT * P - 1, oob_is_err=False).then_inc(put[par], 16)

        def scores(pe, b, par, u):
            n = UNITS * b + u
            if u == 0:
                pe.wait_ge(m_in[0], 16 * (b + 1))
            if u == 4:
                pe.wait_ge(m_in[1], 16 * (b + 1))
            wait(pe, exp_ok, n - 1)
            for j in range(2):
                pe.matmul(EX[u % 2][:, T * j:T * j + T], ks[:, par, 2 * u + j, 0:P],
                          qs[:, par, 2 * u + j, :], start=True, stop=True)
            for j in range(2):
                ins = pe.matmul(EX[u % 2][:, 2 * T + P * j:2 * T + P * j + P], ks[:, par, 2 * u + j, P:T],
                                qs[:, par, 2 * u + j, P:T], start=True, stop=True)
            ins.then_inc(sc_pe, 1)

        def weigh(pe, b, par, u):
            n = UNITS * b + u
            pe.wait_ge(mask_ok, 2 * n + 2)
            if u == 0:
                wait(pe, av_sb, b)
                pe.wait_ge(v_sb, b + 1)
            for j in range(2):
                h = 2 * u + j
                out = AV[:, T * (h // 8):T * (h // 8) + T]
                pe.matmul(out, vst[:, par, 0, h, :], probs[:, u % RING, T * j:T * j + T], start=(h % 8 == 0),
                          stop=False, skip_group_check=True)
                ins = pe.matmul(out[:, P:T], vst[:, par, 1, h, :], probs[:, u % RING, 2 * T + P * j:2 * T + P * j + P],
                                start=False, stop=(h % 8 == 7), skip_group_check=True)
            ins.then_inc(av_pe, 1)

        def maxima(pe, b, par, v):
            n = MAXU * b + v
            if v == 0:
                pe.wait_ge(stack_in, 128 * (b + 1))
            wait(pe, max_ok, n - 1)
            bank = PS[:, 4 + v % 2, :]
            g, r = v // 3, v % 3
            rows = 4 * DH
            if r < 2:
                for j in range(2):
                    h = 4 * g + 2 * r + j
                    pe.matmul(bank[:, T * j:T * j + T], qs[0:rows, par, h, P:T], ks[0:rows, par, h, :],
                              start=(j == 0), stop=False, skip_group_check=True)
                ins = pe.matmul(bank.rearrange("p (h k) -> p h k", h=2)[:, :, P:T], identb[:], causal[:, 0:2, :],
                                start=False, stop=True, skip_group_check=True)
            else:
                for j in range(4):
                    h = 4 * g + j
                    pe.matmul(bank[:, P * j:P * j + P], qs[0:rows, par, h, 0:P], ks[0:rows, par, h, 0:P],
                              start=(j == 0), stop=False, skip_group_check=True)
                ins = pe.matmul(bank, identb[:], causal[:].rearrange("p a b -> p (a b)"),
                                start=False, stop=True, skip_group_check=True)
            ins.then_inc(max_pe, 1)

        def turn_maxima(pe, b, par, half):
            pe.wait_ge(max_ok, MAXU * b + (half + 1) * MAXU // 2)
            if half == 0 and has(b + 1):
                pe.wait_ge(latT_sb, b + 2)
            elif half == 0:
                pe.wait_ge(x2_ok, b - 1)
            elif has(b + 1):
                pe.wait_ge(k_tmp, b + 2)
            else:
                pe.wait_ge(m_neg, 2 * b + 1)
            for t in range(TT):
                ins = pe.transpose(MISC[0:H // 2, P * t:P * t + P], mx[:, par, t, 8 * half:8 * half + 8], ident[:])
            ins.then_inc(m_pe, 1)

        def finish(pe, b):
            pe.wait_ge(attn_ok, 2 * b + 2)
            if has(b + 3):
                pe.wait_ge(q_tmp, b + 4)
            elif has(b + 1):
                pe.wait_ge(place_ok, b)
            else:
                pe.wait_ge(x2_ok, b)
            for t in range(TT):
                ins = pe.matmul(MISC[:, P * t:P * t + P], attnT[:, P * t:P * t + P], w2[:, WOF:WOF + P],
                                start=True, stop=True)
            ins.then_inc(fin_pe, 1)

        def places(pe, b):
            pe.wait_ge(hit_ok, b + 1)
            wait(pe, cum_ok, TT * b)
            if has(b + 3):
                pe.wait_ge(v_sb, b + 4)
            elif has(b + 2):
                pe.wait_ge(m_neg, 2 * b + 6)
            elif has(b + 1):
                pe.wait_ge(x2_ok, b + 2)
            else:
                pe.wait_ge(place_ok, b)
            settle(pe, b)
            for t in range(TT):
                o = MISC[:, E * t:E * t + E]
                pe.matmul(o, tri[:], hit[:, t, :], start=True, stop=False)
                for before in range(t):
                    pe.matmul(o, onesb[:], hit[:, before, :], start=False, stop=False)
                ins = pe.matmul(o, onesb[:], cum[:], start=False, stop=True)
            ins.then_inc(place_pe, 1)

        def prep_pe_step(pe, b, u):
            if u == 3:
                pe.wait_ge(hs_ok, TT * (b + 1))
                if has(b - 4):
                    pe.wait_ge(place_ok, b - 3)
                else:
                    wait(pe, v_sb, b)
                for t in range(TT):
                    ins = pe.transpose(MISC[:, P * t:P * t + P], hs[:, t, :], ident[:])
                ins.then_inc(prep_pe, 1)
            if u == 4:
                pe.wait_ge(hT_sb, b + 1)
                for t in range(TT):
                    ins = pe.matmul(MISC[:, L * t:L * t + L], hT[:, P * t:P * t + P], w2[:, WDKV:WDKV + L],
                                    start=True, stop=True)
                ins.then_inc(prep_pe, 1)
            if u == 5:
                pe.wait_ge(lat_sb, b + 1)
                pe.matmul(MISC[:, 0:T], w2[:, WQ:WQ + P], hT[:], start=True, stop=True)
                pe.matmul(MISC[:, T:2 * T], w2[:, WQR:WQR + P], hT[:], start=True, stop=True).then_inc(prep_pe, 1)
            if u == 6:
                pe.wait_ge(latn_ok, TT * (b + 1))
                if has(b - 3):
                    pe.wait_ge(x2_ok, b - 2)
                else:
                    pe.wait_ge(q_tmp, b + 1)
                settle(pe, b)
                for t in range(TT):
                    ins = pe.transpose(MISC[0:L, P * t:P * t + P], latn[:, t, :], ident[:])
                ins.then_inc(prep_pe, 1)
            if u == 7:
                pe.wait_ge(latT_sb, b + 1)
                wait(pe, m_neg, 2 * b - 1)
                pe.matmul(MISC[:, 0:T], w2[0:L, WUK:WUK + P], latT[:], start=True, stop=True)
                pe.matmul(MISC[:, T:2 * T], w2[0:L, WUKR:WUKR + P], latT[:], start=True,
                          stop=True).then_inc(prep_pe, 1)

        @block.tensor
        def _(pe):
            pe.wait_ge(w1_in, 16)
            pe.matmul(PS[:, 4, 0:129], w1[:, WKT:WKT + P], w1[:, WQB:WQB + 129], start=True, stop=True)
            pe.matmul(PS[:, 4, 129:257], w1[:, WVT:WVT + P], w1[:, WO:WO + P], start=True, stop=True).then_inc(fold_pe, 1)
            pe.wait_ge(bias_rows, 2)
            pe.matmul(PS[:, 5, 0:129], bkv[:, 0, :], w1[:, WQB:WQB + 129], start=True, stop=True)
            pe.matmul(PS[:, 5, 129:257], bkv[:, 1, :], w1[:, WO:WO + P], start=True, stop=True).then_inc(fold_pe, 1)
            pe.wait_ge(fold_sb, 2)
            for n in range(PAIRS):
                pe.matmul(PS[:, n, 0:257], w1[:, CTX + P * n:CTX + P * n + P], mn[:], start=True,
                          stop=True).then_inc(kqv_pe, 1)
            pe.wait_ge(kqv_sb, PAIRS)
            pe.wait_ge(fk_in, 16)
            for par in range(2):
                rows = slice(S * par, S * par + S)
                for f in range(2):
                    pe.matmul(PS[:, 4 + 2 * par + f, :].rearrange("p (a b) -> p a b", b=P),
                              fk[rows, P * f:P * f + P], kqv[rows, :, 0:P],
                              start=True, stop=True).then_inc(kdft_pe, 1)
            pe.wait_ge(fx_in, 16)
            for par in range(2):
                for f in range(2):
                    for h in range(TT):
                        pe.wait_ge(xn_ok, NT)
                        ins = pe.matmul(PS[:, 2 * par + f, :].rearrange("p (a b) -> p a b", b=P),
                                        fx[:, h, P * f:P * f + P],
                                        XN[:].rearrange("p (a c h) d -> p c h a d", c=2, h=2)[:, par, h],
                                        start=(h == 0), stop=(h == TT - 1))
                    ins.then_inc(xdft_pe, 1)
            pe.wait_ge(cross_ok, 4)
            pe.wait_ge(kqv_sb, PAIRS + 2)
            pe.wait_ge(iv_in, 16)
            pe.matmul(PS[0:B, 4, 0:T], cross[:, 0].rearrange("p a b -> p (a b)"), iv[:, 0, :], start=True, stop=False)
            pe.matmul(PS[0:B, 4, 0:T], cross[:, 1].rearrange("p a b -> p (a b)"), iv[:, 1, :], start=False, stop=False)
            pe.matmul(PS[0:B, 4, 0:T], kb[:].rearrange("p a b -> p (a b)"), flat[:], start=False,
                      stop=True).then_inc(mean_pe, 1)
            pe.wait_ge(prod_ok, 4)
            for n in range(WARM):
                pe.matmul(PS[:, 5, :], w1[:, 0:P], fx[:].rearrange("p a b -> p (a b)"), start=True, stop=True)
            for b in range(B):
                pe.wait_ge(circ_in[b], 16)
                rows = slice(S * (b % 2), S * (b % 2) + S)
                for h in range(TT):
                    at = T * (b // 2 % 2) + P * h
                    ins = pe.matmul(PS[:, 2 * (b % 2) + b // 4, at:at + P], circ[rows, b // 2, P * h:P * h + P],
                                    kqv[rows, b // 2, 129:257], start=True, stop=True)
                ins.then_inc(x1_pe, 1)

            pe.wait_ge(ids, 4)
            pe.wait_ge(vst_ok, 3)
            pe.wait_ge(w2_ok, 2)
            pe.wait_ge(ones_in, 16)
            pe.wait_ge(x1_ok, 4)
            pe.wait_ge(w4_ok, 3 + E + 1)
            pe.wait_ge(w3_ok, 1)
            for i, par in steps(pe, -2, 9):
                for u in range(UNITS):
                    if has(i):
                        scores(pe, i, par, u)
                    if u >= 2 and has(i):
                        weigh(pe, i, par, u - 2)
                    if u < 2 and has(i - 1):
                        weigh(pe, i - 1, 1 - par, UNITS - 2 + u)
                    if u == 1 and has(i):
                        turn_maxima(pe, i, par, 1)
                    if u == 2 and has(i + 1):
                        b = i + 1
                        pe.wait_ge(k_tmp, b + 1)
                        wait(pe, m_neg, 2 * b)
                        for t in range(TT):
                            ins = pe.matmul(MISC[:, P * t:P * t + P], latT[:, P * t:P * t + P], w2[0:L, WUV:WUV + P],
                                            start=True, stop=True)
                        ins.then_inc(prep_pe, 1)
                    if has(i + 2):
                        prep_pe_step(pe, i + 2, u)
                    if u >= 2 and has(i + 1):
                        maxima(pe, i + 1, 1 - par, 2 * (u - 2))
                        maxima(pe, i + 1, 1 - par, 2 * (u - 2) + 1)
                    if u == (5 if has(i) else 1) and has(i - 1):
                        finish(pe, i - 1)
                    if u == 2 and has(i - 2):
                        places(pe, i - 2)
                    if u == 6 and has(i + 1):
                        turn_maxima(pe, i + 1, 1 - par, 0)

            pe.wait_ge(cum_ok, TT * B)
            pe.matmul(MISC[:, 0:E], onesb[:], cum[:], start=True, stop=True).then_inc(total_pe, 1)

            def turn_rows(q, k):
                s = RING3 * q + k
                pe.wait_ge(srt_in[k], 16 * (q + 1))
                wait(pe, yT_sb, s)
                pe.transpose(PS[:, 0, 0:P], srt[:, k, 0:D], ident[:]).then_inc(yT_pe, 1)

            def hidden(s, par, at):
                pe.wait_ge(yT_sb, s + 1)
                wait(pe, hb_ok, s - 1)
                pe.matmul(PS[:, 1 + par, :], yT[:, par, :], w3[:, bass.ds(at + W1, HID)], start=True,
                          stop=True).then_inc(hid_pe, 1)

            pe.wait_ge(slots_ok, 4)
            turn_rows(0, 0)
            turn_rows(0, 1)
            weights = table_of(pe, slot_w, 0, 1, HID * (E - 1))
            hidden(0, 0, weights[0])
            for q, k in slots(pe):
                s, par = RING3 * q + k, k % 2
                if k == 0:
                    weights = table_of(pe, slot_w, RING3 * q, RING3 + 1 if not isinstance(q, int) or q == 0
                                       else SLOTS % RING3, HID * (E - 1))
                pe.wait_ge(hb_ok, s + 1)
                wait(pe, relu_ok, s - 1)
                for c in range(HK):
                    ins = pe.transpose(PS[:, 3 + par, P * c:P * c + P], hb[:, par, P * c:P * c + P], ident[:])
                ins.then_inc(hT_pe, 1)
                if not isinstance(s, int) or s + 2 < SLOTS:
                    turn_rows(q + (k + 2) // RING3, (k + 2) % RING3)
                if not isinstance(s, int) or s + 1 < SLOTS:
                    hidden(s + 1, 1 - par, weights[k + 1])
                at = weights[k]
                pe.wait_ge(relu_ok, s + 1)
                wait(pe, fin_ok, s - 1)
                for c in range(HK):
                    ins = pe.matmul(PS[:, 5 + par, 0:D], hT3[:, par, c], w3[:, bass.ds(at + (W2 + D * c), D)],
                                    start=(c == 0), stop=(c == HK - 1))
                ins.then_inc(out_pe, 1)

        def norm(dve, c):
            dve.wait_ge(rstd_ok, c + 1)
            for t in range(4 * c, 4 * c + 4):
                dve.tensor_scalar(XN[:, t, :], X[:, t, :], mv[:, t, 0:1], rstd[:, t, 1:2],
                                  ALU.subtract, ALU.mult).then_inc(xn_ok, 1)

        def rotate(dve, b, n, filled, tmp, total, high, done):
            dve.wait_ge(prep_pe, filled)
            dve.tensor_tensor(rope[:], MISC, w2[:, ROPE:ROPE + 512], ALU.mult).then_inc(tmp, 1)
            dve.wait_ge(tmp, b + 1)
            dve.tensor_tensor(qk[:], rope[:, 0:T], rope[:, T:2 * T], ALU.add).then_inc(total, 1)
            dve.wait_ge(total, b + 1)
            wait(dve, stack_in, 128 * b)
            dve.wait_ge(high, b + 1)
            dve.tensor_tensor(parts[:, n, 1, :], qk[:], parts[:, n, 0, :], ALU.subtract).then_inc(done, 1)

        def prep_dve(dve, b, u):
            if u == 0:
                for t in range(TT):
                    dve.bn_stats(ast[:, t, :], tile_of(X, b, t)).then_inc(a_stats, 1)
                for t in range(TT):
                    dve.wait_ge(a_stats, TT * b + t + 1)
                    settle(dve, b)
                    dve.bn_aggr(amv[:, t, :], ast[:, t, :]).then_inc(a_aggr, 1)
            if u == 1:
                dve.wait_ge(a_rstd, b + 1)
                wait(dve, hs_ok, TT * b)
                wait(dve, xn1_ok, TT * b)
                dve.scalar_tensor_tensor(out=nbias[:], in0=amv[:, :, 0:1].rearrange("p t a -> p a t").broadcast_to(
                    [P, 2, TT]), scalar=-1.0, in1=ars[:], op0=ALU.mult, op1=ALU.mult).then_inc(nbias_ok, 1)
            if u == 5:
                rotate(dve, b, 0, 6 * b + 3, q_tmp, q_sum, q_hi, q_ok)
            if u == 4:
                dve.wait_ge(lat_sb, b + 1)
                for t in range(TT):
                    dve.bn_stats(lst[:, t, :], lat[:, t, :]).then_inc(l_stats, 1)
                for t in range(TT):
                    dve.wait_ge(l_stats, TT * b + t + 1)
                    settle(dve, b)
                    dve.bn_aggr(lmv[:, t, :], lst[:, t, :]).then_inc(l_aggr, 1)
            if u == 6:
                dve.wait_ge(l_rstd, b + 1)
                for t in range(TT):
                    dve.tensor_scalar(latn[:, t, :], lat[:, t, :], lmv[:, t, 0:1], lrs[:, t:t + 1],
                                      ALU.subtract, ALU.mult).then_inc(latn_ok, 1)
            if u == 7:
                rotate(dve, b, 1, 6 * b + 5, k_tmp, k_sum, k_hi, k_ok)

        def normalize(dve, b):
            dve.wait_ge(av_sb, b + 1)
            dve.reciprocal(rec[:], avs[P // 2:P, :]).then_inc(rec_ok, 1)
            dve.wait_ge(rec_ok, b + 1)
            wait(dve, fin_pe, b)
            for n in range(2):
                dve.tensor_tensor(attnT[64 * n:64 * n + 64, :], avs[0:P // 2, T * n:T * n + T],
                                  rec[:, T * n:T * n + T], ALU.mult).then_inc(attn_ok, 1)

        def row_max(dve, b, par, v):
            dve.wait_ge(max_pe, MAXU * b + v + 1)
            bank = PS[:, 4 + v % 2, :]
            g, r = v // 3, v % 3
            if r < 2:
                dve.tensor_reduce(mx[:, par, 1, 4 * g + 2 * r:4 * g + 2 * r + 2],
                                  bank.rearrange("p (h k) -> p h k", h=2), AX_X, ALU.max).then_inc(max_ok, 1)
            else:
                dve.tensor_reduce(mx[:, par, 0, 4 * g:4 * g + 4],
                                  bank.rearrange("p (h k) -> p h k", h=4), AX_X, ALU.max).then_inc(max_ok, 1)

        def score(dve, b, par):
            dve.wait_ge(rows_ok, TT * b + TT)
            for t in range(TT):
                for e in range(E):
                    dve.scalar_tensor_tensor(out=dot[:, t, e], in0=rows[:, par, t, 0:D], scalar=1.0,
                                             in1=w4[:, GATE + D * e:GATE + D * e + D], op0=ALU.mult, op1=ALU.mult,
                                             accum_out=logit[:, t, e:e + 1]).then_inc(logit_ok, 1)

        def choose(dve, b):
            row = lambda at: w4[:, at:at + E].rearrange("p (t e) -> p t e", t=1).broadcast_to([P, TT, E])
            dve.wait_ge(logit_ok, TT * E * (b + 1))
            dve.tensor_tensor(logit[:], logit[:], row(GB), ALU.add).then_inc(choice, 1)
            dve.wait_ge(choice, 5 * b + 1)
            dve.tensor_reduce(lead[:], logit[:], AX_X, ALU.max).then_inc(choice, 1)
            dve.wait_ge(choice, 5 * b + 2)
            dve.tensor_tensor(tied[:], logit[:], lead[:].broadcast_to([P, TT, E]), ALU.is_equal).then_inc(choice, 1)
            dve.wait_ge(choice, 5 * b + 3)
            dve.tensor_tensor(tied[:], tied[:], row(RANK), ALU.mult).then_inc(choice, 1)
            dve.wait_ge(choice, 5 * b + 4)
            dve.tensor_reduce(lead[:], tied[:], AX_X, ALU.max).then_inc(choice, 1)
            dve.wait_ge(choice, 5 * b + 5)
            wait(dve, cum_ok, TT * b)
            dve.tensor_tensor(hit[:], row(RANK), lead[:].broadcast_to([P, TT, E]), ALU.is_equal).then_inc(hit_ok, 1)

        def rank(dve, b, par):
            dve.wait_ge(place_pe, b + 1)
            dve.tensor_tensor(place[:], MISC[:, 0:TT * E].rearrange("p (t e) -> p t e", t=TT), hit[:],
                              ALU.mult).then_inc(place_ok, 1)
            dve.wait_ge(hit_ok, b + 1)
            for t in range(TT):
                wait(dve, cum_ok, TT * b + t)
                dve.tensor_tensor(cum[:], cum[:], hit[:, t, :], ALU.add).then_inc(cum_ok, 1)
            dve.wait_ge(place_ok, b + 1)
            with nc.allow_low_precision(reason="row numbers are whole"):
                dve.tensor_reduce(pos[:, par, :].rearrange("p (t e) -> p t e", e=1), place[:], AX_X,
                                  ALU.add).then_inc(pos_ok, 1)

        @block.vector
        def _(dve):
            for c in range(4):
                dve.wait_ge(x_in[c], 16)
                for t in range(4 * c, 4 * c + 4):
                    dve.bn_stats(bst[:, t, :], X[:, t, :]).then_inc(stats_a, 1)
                for t in range(4 * c, 4 * c + 4):
                    dve.wait_ge(stats_a, t + 1)
                    dve.bn_aggr(mv[:, t, :], bst[:, t, :]).then_inc(stats_b, 1)
                if c == 0:
                    dve.wait_ge(w1_in, 16)
                    for n in range(2):
                        dve.tensor_copy(bkv[:, n, :], w1[:, BKV + n:BKV + n + 1].broadcast_to([P, P])).then_inc(
                            bias_rows, 1)
                    dve.wait_ge(fold_pe, 1)
                    dve.tensor_copy(mn[:], PS[:, 4, 0:257]).then_inc(fold_sb, 1)
                if c == 1:
                    dve.wait_ge(fold_pe, 2)
                    dve.tensor_copy(biasbc[:], PS[:, 5, 0:257]).then_inc(fold_sb, 1)
                    norm(dve, 0)
                    dve.wait_ge(fold_sb, 2)
                    for n in range(PAIRS):
                        dve.wait_ge(kqv_pe, n + 1)
                        dve.tensor_tensor(kqv[:, n, :], PS[:, n, 0:257], biasbc[:], ALU.add).then_inc(kqv_sb, 1)
                if c > 1:
                    norm(dve, c - 1)
            norm(dve, 3)
            dve.wait_ge(kqv_sb, PAIRS)
            dve.wait_ge(consts, 3)
            for par in range(2):
                part = slice(S * par, S * par + S)
                dve.tensor_copy(kb[part, :, par:par + 1], kqv[part, :, P:P + 1]).then_inc(kqv_sb, 1)
            for n in range(4):
                dve.wait_ge(xdft_pe, n + 1)
                dve.wait_ge(kdft_sb, n + 1)
                dve.tensor_tensor(prod[:, n, :], PS[:, n, :], kd[:, n, :], ALU.mult).then_inc(prod_ok, 1)
                dve.wait_ge(prod_ok, n + 1)
                dve.tensor_reduce(cross[:, n % 2, :, n // 2:n // 2 + 1], prod[:, n, :].rearrange("p (a b) -> p a b", b=P),
                                  AX_X, ALU.add).then_inc(cross_ok, 1)
            dve.wait_ge(w2_in, 16)
            dve.tensor_scalar(w2[:, WQ:WDKV + L], w2[:, WQ:WDKV + L], w2[:, N1:N1 + 1], None,
                              ALU.mult).then_inc(w2_ok, 1)
            dve.wait_ge(ids, 3)
            dve.tensor_copy(identb[:], ident[:]).then_inc(w2_ok, 1)
            dve.memset(top[:, 16:24], LOWEST).then_inc(topk, 1)
            dve.wait_ge(mean_pe, 1)
            dve.tensor_copy(mean[:], PS[0:B, 4, 0:T]).then_inc(topk, 1)
            dve.wait_ge(topk, 2)
            dve.max(top[:, 0:8], mean[:]).then_inc(topk, 1)
            dve.wait_ge(topk, 3)
            dve.tensor_scalar(tot[:, 0:1], top[:, 0:1], -1.0, None, ALU.mult).then_inc(topk, 1)
            dve.match_replace(work[:, 0, :], top[:, 0:8], mean[:], LOWEST).then_inc(topk, 1)
            dve.wait_ge(topk, 5)
            dve.max(top[:, 8:16], work[:, 0, :]).then_inc(topk, 1)
            dve.wait_ge(topk, 6)
            dve.tensor_copy(top[:, 16:16 + TOPK - 8], top[:, 8:8 + TOPK - 8]).then_inc(topk, 1)
            dve.wait_ge(topk, 7)
            dve.match_replace(work[:, 0, :], top[:, 16:24], work[:, 0, :], LOWEST).then_inc(topk, 1)
            dve.wait_ge(topk, 8)
            dve.wait_ge(mean_exp, 1)
            dve.scalar_tensor_tensor(out=work[:, 0, :], in0=work[:, 0, :], scalar=0.99 * LOWEST, in1=work[:, 1, :],
                                     op0=ALU.is_le, op1=ALU.mult, accum_out=tot[:, 1:2]).then_inc(topk, 1)
            dve.wait_ge(topk, 9)
            dve.reciprocal(tot[:, 2:3], tot[:, 1:2]).then_inc(topk, 1)
            dve.wait_ge(topk, 10)
            dve.tensor_scalar(soft[:].rearrange("p (a b) -> p a b", a=2), work[:, 0:1, :].broadcast_to([B, 2, T]),
                              tot[:, 2:3], None, ALU.mult).then_inc(soft_ok, 1)
            dve.wait_ge(xb_ok, NT)
            for n in range(4):
                par, g = n % 2, n // 2
                dve.wait_ge(x1_pe, 4 * g + 3 + par)
                dve.tensor_tensor(tiles(X, par, g), PS[:, 2 * par + g, :].rearrange("p (a d) -> p a d", d=T),
                                  tiles(XB, par, g), ALU.add).then_inc(x1_ok, 1)
                if n == 0:
                    dve.wait_ge(x1_ok, 1)
                    prep_dve(dve, 0, 0)
                if n == 1:
                    prep_dve(dve, 0, 1)
            dve.wait_ge(w4_ok, 3 + E + 1)
            dve.wait_ge(x1_ok, 4)
            for i, par in steps(dve, -2, 9):
                for u in range(UNITS):
                    if has(i + 2) and not (isinstance(i, int) and i == -2 and u < 2):
                        prep_dve(dve, i + 2, u)
                    if u == (1 if has(i) else 0) and has(i - 1):
                        normalize(dve, i - 1)
                    if u == (6 if has(i) else 1) and has(i - 1):
                        b = i - 1
                        dve.wait_ge(fin_pe, b + 1)
                        dve.wait_ge(xn1_ok, TT * (b + 1))
                        dve.tensor_tensor(tile_of(XN, b, 0, TT), MISC[:, 0:T], tile_of(XN, b, 0, TT),
                                          ALU.add).then_inc(x2_ok, 1)
                    if u == 0 and has(i - 2):
                        score(dve, i - 2, par)
                    if u == (0 if has(i) else 1) and has(i - 2):
                        choose(dve, i - 2)
                    if u == 2 and has(i - 2):
                        rank(dve, i - 2, par)
                    if u >= 2 and has(i + 1):
                        row_max(dve, i + 1, 1 - par, 2 * (u - 2))
                        row_max(dve, i + 1, 1 - par, 2 * (u - 2) + 1)
            dve.wait_ge(total_pe, 1)
            flat_of = lambda a: a.rearrange("p (e n) -> p e n", n=1)
            edges = w4[0:1, EDGE:EDGE + E * NT].rearrange("p (e n) -> p e n", e=E)
            dve.tensor_tensor(full[:], flat_of(MISC[0:1, 0:E]).broadcast_to([1, E, NT]), edges,
                              ALU.is_gt).then_inc(table, 1)
            dve.tensor_copy(pad_at[:], MISC[0:1, 0:E]).then_inc(slots_ok, 1)
            dve.wait_ge(table, 1)
            dve.tensor_reduce(flat_of(count[:]), full[:], AX_X, ALU.add).then_inc(table, 1)
            dve.wait_ge(table, 2)
            dve.tensor_scalar(shift[:], count[:], -1.0, float(REGION), ALU.mult, ALU.add).then_inc(table, 1)
            dve.tensor_copy(ends[:, 0:1], count[:, 0:1]).then_inc(table, 1)
            for e in range(1, E):
                dve.wait_ge(table, 3 + e)
                dve.tensor_tensor(ends[:, e:e + 1], ends[:, e - 1:e], count[:, e:e + 1], ALU.add).then_inc(table, 1)
            dve.wait_ge(table, 3 + E)
            slot = w4[0:1, SLOT:SLOT + SLOTS]
            across = lambda a: a.rearrange("p (n e) -> p n e", n=1).broadcast_to([1, SLOTS, E])
            dve.tensor_tensor(beyond[:], slot.rearrange("p (n e) -> p n e", e=1).broadcast_to([1, SLOTS, E]),
                              across(ends[:]), ALU.is_ge).then_inc(table, 1)
            dve.wait_ge(table, 4 + E)
            dve.tensor_tensor(skip[:], beyond[:], across(shift[:]), ALU.mult).then_inc(table, 1)
            dve.tensor_reduce(chosen[:].rearrange("p (n e) -> p n e", e=1), beyond[:, :, 0:E - 1], AX_X,
                              ALU.add).then_inc(table, 1)
            dve.wait_ge(table, 5 + E)
            dve.tensor_reduce(base[:].rearrange("p (n e) -> p n e", e=1), skip[:], AX_X, ALU.add).then_inc(table, 1)
            dve.wait_ge(table, 6 + E)
            dve.tensor_scalar(slot_w[:], chosen[:], float(HID), None, ALU.mult).then_inc(slots_ok, 1)
            dve.tensor_scalar(slot_b[:], chosen[:], float(D), None, ALU.mult).then_inc(slots_ok, 1)
            dve.wait_ge(table, 7 + E)
            dve.scalar_tensor_tensor(out=slot_row[:], in0=base[:], scalar=float(P), in1=w4[0:1, SLOTP:SLOTP + SLOTS],
                                     op0=ALU.mult, op1=ALU.add).then_inc(slots_ok, 1)

            def bias(s, par, at):
                dve.wait_ge(hid_pe, s + 1)
                wait(dve, hT_pe, s - 1)
                dve.tensor_tensor(hb[:, par, :], PS[:, 1 + par, :], w4[:, bass.ds(at + B1, HID)],
                                  ALU.add).then_inc(hb_ok, 1)

            dve.wait_ge(slots_ok, 4)
            biases = table_of(dve, slot_w, 0, 1, HID * (E - 1))
            bias(0, 0, biases[0])
            for q, k in slots(dve):
                s, par = RING3 * q + k, k % 2
                if k == 0:
                    biases = table_of(dve, slot_w, RING3 * q, RING3 + 1 if not isinstance(q, int) or q == 0
                                      else SLOTS % RING3, HID * (E - 1))
                if not isinstance(s, int) or s + 1 < SLOTS:
                    bias(s + 1, 1 - par, biases[k + 1])
                dve.wait_ge(srt_in[k], 16 * (q + 1))
                wait(dve, put[par], 32 * q + 16 * (k // 2))
                dve.tensor_copy(where[:, par:par + 1], srt[:, k, 2 * D:ROW]).then_inc(where_ok, 1)
                dve.wait_ge(out_pe, s + 1)
                dve.wait_ge(res_ok, s + 1)
                dve.tensor_tensor(fin[:, par, :], PS[:, 5 + par, 0:D], res[:, par, :], ALU.add).then_inc(fin_ok, 1)


def fourier():
    t, f = np.arange(T), np.arange(T // 2)
    w = 2 * np.pi / T
    forth = np.concatenate([np.cos(w * np.outer(t, f)), np.cos(np.pi * t)[:, None],
                            -np.sin(w * np.outer(t, f[1:]))], 1)
    delay = (-t) % T
    back = np.concatenate([2 * np.cos(w * np.outer(f, delay)), np.cos(np.pi * delay)[None],
                           2 * np.sin(w * np.outer(f[1:], delay))], 0)
    back[0] = 1
    back /= T * D
    tiles = lambda a: np.ascontiguousarray(a.reshape(TT, P, T).transpose(1, 0, 2).astype(np.float32))
    short = forth[S - 1::-1]
    return tiles(forth), np.concatenate([short, short]).astype(np.float32), tiles(back)


def rotation():
    half = DH // 2
    freq = (1.0 / 10000.0 ** (np.arange(half, dtype=np.float32) / np.float32(half))).astype(np.float32)
    ang = (np.arange(T, dtype=np.float32)[:, None] * freq[None]).astype(np.float32)
    cos, sin = np.cos(ang), np.sin(ang)
    return (np.repeat(np.concatenate([cos, cos], 1).T, H, 0), np.repeat(np.concatenate([-sin, sin], 1).T, H, 0))


def kernel(**inputs):
    import concourse.bacc as bacc
    from concourse.bass_utils import run_bass_kernel_spmd

    a = {k: np.asarray(v) for k, v in inputs.items()}
    xa = lambda n: a["L0_xattn_" + n]
    ff = lambda n: a["L0_ffn_" + n]
    ctx_t = a["ctx_1024"][:, ::-1, :].reshape(PAIRS, 2 * S, D).transpose(2, 0, 1).reshape(D, PAIRS * 2 * S)
    pack1 = np.concatenate([xa("Wk").T, xa("Wv").T, xa("Wq").T, xa("bq")[:, None], xa("Wo"), xa("bk")[:, None],
                            xa("bv")[:, None], ctx_t, np.broadcast_to(xa("bo"), (P, D))], 1)
    rows = np.arange(D).reshape(H, DH)
    by_feature, partner = rows.T.reshape(D), np.roll(rows, DH // 2, axis=1).T.reshape(D)
    low = np.concatenate([ff("Wuk")[by_feature].T, ff("Wuk")[partner].T, ff("Wuv").T, ff("ln_g")[:, None],
                          ff("ln_b")[:, None]], 1)
    low = np.concatenate([low, low])
    pack2 = np.concatenate([ff("Wq")[by_feature].T, ff("Wq")[partner].T, ff("Wdkv").T, ff("Wo").T,
                            ff("norm1_w")[:, None], ff("norm2_w")[:, None], *rotation(), low], 1)
    w1 = ff("W1").transpose(2, 0, 1).reshape(D, E * HID)
    w2 = ff("W2").transpose(2, 0, 1).reshape(HK, P, E, D).transpose(1, 2, 0, 3).reshape(P, E * HK * D)
    tokens = (P * np.arange(NT)[None] + np.arange(P)[:, None]).astype(np.float32)
    pack3 = np.concatenate([w1, w2, tokens, NOWHERE + np.arange(P, dtype=np.float32)[:, None]], 1)
    edges = P * (REGION * np.arange(E)[:, None] + np.arange(NT)[None])
    constants = [E - np.arange(E), edges.ravel(), np.arange(SLOTS), P * np.arange(SLOTS)]
    pack4 = np.concatenate([ff("gate_w").ravel(), ff("norm2_w"), ff("gate_b"),
                            *(c.astype(np.float32) for c in constants), ff("b1").ravel(), ff("b2").ravel()])[None]
    dft_x, dft_k, inv = fourier()
    arrays = {"x": a["x"], "pack1": pack1, "dft_x": dft_x, "dft_k": dft_k, "inv": inv, "pack2": pack2,
              "pack3": pack3, "pack4": pack4}
    arrays = {k: np.ascontiguousarray(v) for k, v in arrays.items()}
    nc = bacc.Bacc("TRN2", target_bir_lowering=False, num_devices=1)
    aps = {k: nc.dram_tensor(k, v.shape, mybir.dt.from_np(v.dtype), kind="ExternalInput").ap()
           for k, v in arrays.items()}
    out = nc.dram_tensor("out", (B, T, D), F32, kind="ExternalOutput").ap()
    sorted_rows = nc.dram_tensor("sorted_rows", ((REGION * E + E - 1) * P, ROW), F32, kind="Internal").ap()
    build(nc, sorted_rows=sorted_rows, out=out, **aps)
    res = run_bass_kernel_spmd(nc, [arrays], core_ids=[0])
    return res.results[0]["out"]
```

```python
from contextlib import ExitStack

import concourse.bass as bass
import numpy as np
from concourse import mybir

F32 = mybir.dt.float32
F16 = mybir.dt.float16
BF16 = mybir.dt.bfloat16
I32 = mybir.dt.int32
ALU = mybir.AluOpType
ACT = mybir.ActivationFunctionType
AX_X = mybir.AxisListType.X

P = 128
B, T, D = 8, 256, 128
S = 64
TT = T // P
NT = B * TT
PAIRS = B // 2
LN_EPS, RMS_EPS = 1e-5, 1e-6
TOPK = 11
WARM = 8
GAIN = 64.0
LOWEST = -3.0e38

WKT, WVT, WQB, WO, BKV, CTX, BO = 0, 128, 256, 385, 513, 515, 1027
PACK1 = BO + D

H, DH, L = 16, 8, 64
SCALE = float(DH) ** -0.5
SROWS = 4 * DH + 1
RING = 4
CHUNK = 2 * (T + P)
UNITS = H // 2
MAXU = 3 * H // 4
WQ, WQR, WDKV, WOF, N1, N2, ROPE = 0, 128, 256, 320, 448, 449, 450
WUK, WUKR, WUV, LNG, LNB = 962, 1090, 1218, 1346, 1347
PACK2 = 1348

E, HID = 4, 512
HK = HID // P
REGION = TT * B + 1
SLOTS = NT + E - 1
RING3 = 4
ROW = 2 * D + 1
NOWHERE = 2 * NT * P
W1, TOKEN, B1, W2 = 0, 2048, 2065, 2081
PACK3 = W2
GATE, N2ROW, GB, RANK, EDGE, SLOT, SLOTP, B2 = 0, 512, 640, 644, 648, 712, 731, 750
PACK4 = B2 + E * D


def build(nc, x, pack1, dft_x, dft_k, inv, pack2, pack3, pack4, sorted_rows, out):
    with ExitStack() as ctx:
        def sb(name, shape, dt=F32):
            return ctx.enter_context(nc.sbuf_tensor(name, shape, dt))

        def sem(name):
            return ctx.enter_context(nc.semaphore(name))

        PS = ctx.enter_context(nc.psum_tensor("PS", [P, 8, 512], F32))

        X = sb("X", [P, NT, D])
        XB = sb("XB", [P, NT, D])
        XN = sb("XN", [P, NT, D])
        w1 = sb("w1", [P, PACK1])
        fx = sb("fx", [P, TT, T])
        fk = sb("fk", [P, T])
        iv = sb("iv", [P, TT, T])
        bst = sb("bst", [P, NT, 6])
        mv = sb("mv", [P, NT, 2])
        rstd = sb("rstd", [P, NT, 2])
        half = sb("half", [P, 2 * NT])
        bkv = sb("bkv", [P, 2, P])
        mn = sb("mn", [P, 257])
        biasbc = sb("biasbc", [P, 257])
        kqv = sb("kqv", [P, PAIRS, 257])
        kb = sb("kb", [P, PAIRS, 2])
        flat = sb("flat", [P, T])
        kd = sb("kd", [P, 4, 512])
        prod = sb("prod", [P, 4, 512])
        cross = sb("cross", [P, 2, PAIRS, 2])
        mean = sb("mean", [B, T])
        top = sb("top", [B, 24])
        work = sb("work", [B, 2, T])
        soft = sb("soft", [B, 2 * T])
        tot = sb("tot", [B, 4])
        circ = sb("circ", [P, PAIRS, T])

        def tiles(a, par, g):
            return a[:].rearrange("p (g a c h) d -> p g c a (h d)", a=2, c=2, h=TT)[:, g, par]

        w2 = sb("w2", [P, PACK2])
        ident = sb("ident", [P, P])
        identb = sb("identb", [P, P], BF16)
        ones16 = sb("ones16", [P, 2 * H * T // P], F16)
        causal = sb("causal", [P, 4, P], BF16)
        ast = sb("ast", [P, TT, 6])
        amv = sb("amv", [P, TT, 2])
        aeps = sb("aeps", [P, 2, TT])
        ars = sb("ars", [P, 2, TT])
        nbias = sb("nbias", [P, 2, TT])
        hs = sb("hs", [P, TT, D])
        hT = sb("hT", [P, T])
        rope = sb("rope", [P, 512])
        qk = sb("qk", [P, T])
        parts = sb("parts", [P, 2, 2, T], F16)
        lat = sb("lat", [P, TT, L])
        lst = sb("lst", [P, TT, 6])
        lmv = sb("lmv", [P, TT, 2])
        leps = sb("leps", [P, TT])
        lrs = sb("lrs", [P, TT])
        latn = sb("latn", [P, TT, L])
        latT = sb("latT", [L, T])
        vst = sb("vst", [P, 2, TT, H, P])
        qs = sb("qs", [SROWS, 2, H, T], F16)
        ks = sb("ks", [SROWS, 2, H, T], F16)
        mx = sb("mx", [P, 2, TT, H])
        mneg = sb("mneg", [H // 2, 2, T], F16)
        probs = sb("probs", [P, RING, CHUNK])
        avs = sb("avs", [P, 2 * T])
        rec = sb("rec", [P // 2, 2 * T])
        attnT = sb("attnT", [P, T])
        EX = [PS[:, 2 * n:2 * n + 2, :].rearrange("p a b -> p (a b)") for n in range(2)]
        AV = PS[:, 6, :]

        def blocks(a, first):
            return bass.AP(a.tensor, a.offset + first, [list(a.ap[0]), [P * H // 2, 2 * TT], [P + DH, H // 2], [1, DH]])

        MISC = PS[:, 7, :]

        def tile_of(a, b, t=0, n=1):
            return a[:].rearrange("p n d -> p (n d)")[:, bass.ds(b * T + t * P, n * P)]

        ones_ok, ones_in = sem("ones_ok"), sem("ones_in")
        settled = sem("settled")
        w3 = sb("w3", [P, PACK3])
        w4 = sb("w4", [P, PACK4])
        tri = sb("tri", [P, P], BF16)
        onesb = sb("onesb", [P, P], BF16)
        blank = sb("blank", [P, ROW])
        rows = sb("rows", [P, 2, TT, ROW])
        sq = sb("sq", [P, TT, P], BF16)
        ssq = sb("ssq", [P, TT])
        sqe = sb("sqe", [P, TT])
        rr = sb("rr", [P, TT])
        dot = sb("dot", [P, TT, E, D], BF16)
        logit = sb("logit", [P, TT, E])
        lead = sb("lead", [P, TT, 1])
        tied = sb("tied", [P, TT, E])
        hit = sb("hit", [P, TT, E], BF16)
        cum = sb("cum", [P, E], BF16)
        place = sb("place", [P, TT, E])
        pos = sb("pos", [P, 2, TT], I32)
        pad_at = sb("pad_at", [1, E], I32)
        full = sb("full", [1, E, NT])
        count = sb("count", [1, E])
        ends = sb("ends", [1, E])
        beyond = sb("beyond", [1, SLOTS, E])
        skip = sb("skip", [1, SLOTS, E])
        shift = sb("shift", [1, E])
        base = sb("base", [1, SLOTS])
        chosen = sb("chosen", [1, SLOTS])
        slot_row = sb("slot_row", [1, SLOTS], I32)
        slot_b = sb("slot_b", [1, SLOTS], I32)
        slot_h = sb("slot_h", [1, SLOTS], I32)
        w1h = [sb(f"w1h{c}", [P, E * P], F16) for c in range(HK)]
        w1l = [sb(f"w1l{c}", [P, E * P], F16) for c in range(HK)]
        second = [sb(f"second{c}", [P, E * D]) for c in range(HK)]
        yh = sb("yh", [P, 2, P], F16)
        yl = sb("yl", [P, 2, P], F16)
        late, used = vst[:].rearrange("p a t h c -> p (a t h c)"), 0

        def view(*shape):
            nonlocal used
            n = int(np.prod(shape))
            used += n
            names = "abc"[:len(shape)]
            dims = {c: m for c, m in zip(names, shape)}
            return late[:, used - n:used].rearrange(f"p ({' '.join(names)}) -> p {' '.join(names)}", **dims)

        srt = view(RING3, ROW)
        hT3, res, fin = view(2, HK, P), view(RING3, D), view(RING3, D)
        where = sb("where", [P, RING3], I32)
        w3_in, w3_ok, w4_in, w4_ok, blank_ok = (sem(n) for n in ("w3_in", "w3_ok", "w4_in", "w4_ok", "blank_ok"))
        ssq_ok, sqe_ok, rr_ok, xs_ok, rows_ok, logit_ok, choice, hit_ok, place_pe, place_ok, pos_ok, cum_ok = (
            sem(n) for n in ("ssq_ok", "sqe_ok", "rr_ok", "xs_ok", "rows_ok", "logit_ok", "choice", "hit_ok",
                             "place_pe", "place_ok", "pos_ok", "cum_ok"))
        sent, pad_in = [sem("sent0"), sem("sent1")], sem("pad_in")
        total_pe, table, slots_ok = sem("total_pe"), sem("table"), sem("slots_ok")
        srt_in = [sem(f"srt_in{k}") for k in range(RING3)]
        yT_pe, yh_ok, yl_ok, hid_pe, out_pe, res_ok, where_ok, fin_ok, w1_halves = (sem(n) for n in (
            "yT_pe", "yh_ok", "yl_ok", "hid_pe", "out_pe", "res_ok", "where_ok", "fin_ok", "w1_halves"))
        second_in = sem("second_in")
        relu_ok = [sem("relu_ok0"), sem("relu_ok1")]
        put = [sem("put0"), sem("put1")]
        w2_in, ids, w2_ok = sem("w2_in"), sem("ids"), sem("w2_ok")
        a_stats, a_aggr, a_eps, a_rstd, hs_ok, xn1_ok = (sem(n) for n in (
            "a_stats", "a_aggr", "a_eps", "a_rstd", "hs_ok", "xn1_ok"))
        prep_pe, hT_sb, q_tmp, q_sum, q_hi, q_ok = (sem(n) for n in (
            "prep_pe", "hT_sb", "q_tmp", "q_sum", "q_hi", "q_ok"))
        lat_sb, l_stats, l_aggr, l_eps, l_rstd, latn_ok, latT_sb = (sem(n) for n in (
            "lat_sb", "l_stats", "l_aggr", "l_eps", "l_rstd", "latn_ok", "latT_sb"))
        k_tmp, k_sum, k_hi, k_ok, v_sb = (sem(n) for n in ("k_tmp", "k_sum", "k_hi", "k_ok", "v_sb"))
        stack_in, m_in = sem("stack_in"), [sem("m_in0"), sem("m_in1")]
        max_pe, max_ok, m_pe, m_neg = sem("max_pe"), sem("max_ok"), sem("m_pe"), sem("m_neg")
        sc_pe, exp_ok, mask_ok, av_pe = sem("sc_pe"), sem("exp_ok"), sem("mask_ok"), sem("av_pe")
        rec_ok, attn_ok, fin_pe, x2_ok, vst_ok = (sem(n) for n in (
            "rec_ok", "attn_ok", "fin_pe", "x2_ok", "vst_ok"))
        av_sb, nbias_ok = sem("av_sb"), sem("nbias_ok")

        x_in = [sem(f"x_in{c}") for c in range(4)]
        w1_in, fx_in, fk_in, iv_in = sem("w1_in"), sem("fx_in"), sem("fk_in"), sem("iv_in")
        stats_a, stats_b, var_eps, rstd_ok, xn_ok, xb_ok = (sem(n) for n in (
            "stats_a", "stats_b", "var_eps", "rstd_ok", "xn_ok", "xb_ok"))
        consts, bias_rows = sem("consts"), sem("bias_rows")
        fold_pe, fold_sb, kqv_pe, kqv_sb = sem("fold_pe"), sem("fold_sb"), sem("kqv_pe"), sem("kqv_sb")
        kdft_pe, kdft_sb, xdft_pe, prod_ok, cross_ok = (sem(n) for n in (
            "kdft_pe", "kdft_sb", "xdft_pe", "prod_ok", "cross_ok"))
        mean_pe, topk, mean_exp_in, mean_exp, soft_ok, x1_pe, x1_ok = (sem(n) for n in (
            "mean_pe", "topk", "mean_exp_in", "mean_exp", "soft_ok", "x1_pe", "x1_ok"))
        circ_in = [sem(f"circ_in{b}") for b in range(B)]
        block = ctx.enter_context(nc.Block())

        def table_of(eng, table, first, n, most):
            return nc.values_load_multi_w_load_instructions(
                table[0:1, bass.ds(first, n)], engines=[eng.engine], min_val=0, max_val=most,
                skip_runtime_bounds_check_because="the table's entries are made from counts of tokens")[1]

        def hidden_tile(c):
            return w3[:, W1:W1 + E * HID].rearrange("p (e c k) -> p e c k", e=E, c=HK)[:, :, c]

        def by_expert(a):
            return a[:].rearrange("p (e k) -> p e k", e=E)

        def group(q, ahead):
            return RING3 + ahead if not isinstance(q, int) or q == 0 else SLOTS % RING3

        def later(s, n):
            return not isinstance(s, int) or s + n < SLOTS

        def has(b):
            return not isinstance(b, int) or 0 <= b < B

        def steps(eng, first, last):
            for i in range(first, 2):
                yield i, i % 2
            with eng.Fori(1, 3) as pair:
                yield 2 * pair, 0
                yield 2 * pair + 1, 1
            for i in range(6, last + 1):
                yield i, i % 2

        def slots(eng):
            for k in range(RING3):
                yield 0, k
            with eng.Fori(1, SLOTS // RING3) as q:
                for k in range(RING3):
                    yield q, k
            for k in range(SLOTS % RING3):
                yield SLOTS // RING3, k

        def early(i):
            return isinstance(i, int) and i < 0

        def wait(eng, s, value):
            if not isinstance(value, int) or value > 0:
                eng.wait_ge(s, value)

        def settle(eng, b):
            if not isinstance(b, int):
                eng.sem_inc(settled, 1)

        def stack(sp, b, par):
            wait(sp, sc_pe, UNITS * (b - 1))
            settle(sp, b)
            for n, done, dst in ((0, q_ok, qs), (1, k_ok, ks)):
                sp.wait_ge(done, b + 1)
                settle(sp, b)
                for c in range(4):
                    part = c // 2 if n == 0 else c % 2
                    sp.dma_start(dst[DH * c:DH * c + DH, par, :, :], parts[:, n, part, :]).then_inc(stack_in, 16)

        def m_row(sp, b, par, half):
            sp.wait_ge(m_neg, 2 * b + half + 1)
            settle(sp, b)
            wait(sp, sc_pe, UNITS * (b - 1))
            settle(sp, b)
            sp.dma_start(qs[4 * DH:SROWS, par, 8 * half:8 * half + 8, :], mneg[:, half, :]).then_inc(m_in[half], 16)

        def pad(eng, half):
            eng.wait_ge(slots_ok, 1)
            for at in table_of(eng, pad_at, half * E // 2, E // 2, (REGION * E - 1) * P):
                eng.dma_start(sorted_rows[bass.ds(at, P)], blank[:]).then_inc(pad_in, 16)

        @block.sync
        def _(sp):
            for c in range(4):
                sp.dma_start(X[:, 4 * c:4 * c + 4, :],
                             x[2 * c:2 * c + 2].rearrange("b (h p) d -> p (b h) d", p=P)).then_inc(x_in[c], 16)
            sp.dma_start(iv[:], inv).then_inc(iv_in, 16)
            sp.wait_ge(ones_ok, 1)
            sp.dma_start(ks[4 * DH:SROWS, :, :, :], ones16[:]).then_inc(ones_in, 16)
            sp.wait_ge(soft_ok, 1)
            for b in range(0, B, 2):
                run = soft[b:b + 1, 193:194]
                src = bass.AP(run.tensor, run.offset, [list(run.ap[0]), [1, S], [1, T]])
                sp.dma_start(circ[0:S, b // 2, :], src).then_inc(circ_in[b], 16)
            sp.wait_ge(blank_ok, 2)
            for n in range(E - 1):
                at = (REGION * E + n) * P
                sp.dma_start(sorted_rows[at:at + P], blank[:]).then_inc(pad_in, 16)
            for i, par in steps(sp, -2, 8):
                if has(i + 1):
                    m_row(sp, i + 1, 1 - par, 0)
                if has(i + 2):
                    stack(sp, i + 2, par)
                if has(i + 1):
                    m_row(sp, i + 1, 1 - par, 1)
            pad(sp, 0)
            for n in range(2):
                sp.wait_ge(sent[n], 16 * NT // 2)
            sp.wait_ge(pad_in, 16 * (E + E - 1))
            sp.wait_ge(slots_ok, 4)
            for q, k in slots(sp):
                s = RING3 * q + k
                at = sp.value_load(slot_row[0:1, bass.ds(s, 1)], min_val=0, max_val=(REGION * E + E - 2) * P)
                if not isinstance(q, int) or q:
                    sp.wait_ge(yT_pe, s - RING3 + 1)
                    sp.wait_ge(res_ok, s - RING3 + 1)
                    sp.wait_ge(where_ok, s - RING3 + 1)
                sp.dma_start(srt[:, k, :], sorted_rows[bass.ds(at, P)]).then_inc(srt_in[k], 16)
            for n in range(2):
                sp.wait_ge(put[n], 16 * ((SLOTS + 1 - n) // 2))

        def negate(act, b, half):
            act.wait_ge(m_pe, 2 * b + half + 1)
            wait(act, m_in[half], 16 * b)
            act.activation(mneg[:, half, :], MISC[0:H // 2, 0:T], ACT.Copy, scale=-1.0).then_inc(m_neg, 1)

        def high_half(act, b, n, total, high):
            act.wait_ge(total, b + 1)
            wait(act, stack_in, 128 * b)
            act.activation(parts[:, n, 0, :], qk[:], ACT.Copy).then_inc(high, 1)

        def scaled(act, b):
            act.wait_ge(nbias_ok, b + 1)
            wait(act, prep_pe, 6 * b - 5)
            settle(act, b)
            for t in range(TT):
                act.activation(hs[:, t, :], tile_of(X, b, t), ACT.Identity, bias=nbias[:, 1, t:t + 1],
                               scale=ars[:, 1, t:t + 1]).then_inc(hs_ok, 1)

        def prep_act(act, b, u):
            if u == 3:
                act.wait_ge(prep_pe, 6 * b + 1)
                act.activation(hT[:], MISC[:, 0:T], ACT.Copy).then_inc(hT_sb, 1)
                for t in range(TT):
                    act.activation(tile_of(XN, b, t), tile_of(X, b, t), ACT.Identity, bias=nbias[:, 0, t:t + 1],
                                   scale=ars[:, 0, t:t + 1]).then_inc(xn1_ok, 1)
            if u == 4:
                act.wait_ge(prep_pe, 6 * b + 2)
                wait(act, latn_ok, TT * b)
                act.activation(lat[:].rearrange("p t l -> p (t l)"), MISC[:, 0:TT * L], ACT.Copy).then_inc(lat_sb, 1)
            if u == 6:
                act.wait_ge(prep_pe, 6 * b + 4)
                act.activation(latT[:], MISC[0:L, 0:T], ACT.Identity, bias=w2[0:L, LNB:LNB + 1],
                               scale=w2[0:L, LNG:LNG + 1]).then_inc(latT_sb, 1)

            if u == 4:
                high_half(act, b, 0, q_sum, q_hi)
            if u == 7:
                high_half(act, b, 1, k_sum, k_hi)

        @block.scalar
        def _(act):
            act.dma_start(w1[:], pack1).then_inc(w1_in, 16)
            act.dma_start(fk[:], dft_k).then_inc(fk_in, 16)
            act.dma_start(fx[:], dft_x).then_inc(fx_in, 16)
            act.dma_start(w2[:], pack2).then_inc(w2_in, 16)
            act.dma_start(w3[:], pack3[:, 0:PACK3]).then_inc(w3_in, 16)
            for c in range(HK):
                act.dma_start(second[c][:], pack3[:, W2 + E * D * c:W2 + E * D * (c + 1)]).then_inc(second_in, 16)
            act.dma_start(w4[:], bass.AP(pack4.tensor, pack4.offset, [[0, P], [1, PACK4]])).then_inc(w4_in, 16)
            for n in range(4):
                act.wait_ge(kdft_pe, n + 1)
                act.activation(kd[:, n, :], PS[:, 4 + n, :], ACT.Copy).then_inc(kdft_sb, 1)
            act.wait_ge(w3_ok, 1)
            for c in range(HK):
                act.activation(by_expert(w1h[c]), hidden_tile(c), ACT.Copy).then_inc(w1_halves, 1)
            act.wait_ge(topk, 4)
            act.activation(work[:, 1, :], mean[:], ACT.Exp, bias=tot[:, 0:1]).then_inc(mean_exp, 1)
            act.wait_ge(soft_ok, 1)
            for b in range(1, B, 2):
                run = soft[b:b + 1, 193:194]
                src = bass.AP(run.tensor, run.offset, [list(run.ap[0]), [1, S], [1, T]])
                act.dma_start(circ[S:P, b // 2, :], src).then_inc(circ_in[b], 16)

            act.wait_ge(w2_in, 16)
            act.wait_ge(vst_ok, 3)
            for i, par in steps(act, -2, 9):
                for u in range(UNITS):
                    if has(i):
                        n = UNITS * i + u
                        act.wait_ge(sc_pe, n + 1)
                        wait(act, av_pe, n - RING + 1)
                        act.activation(probs[:, u % RING, :], EX[u % 2][:, 0:CHUNK],
                                       ACT.Exp, scale=SCALE).then_inc(exp_ok, 1)
                    if u == 0 and has(i - 2):
                        b = i - 2
                        act.wait_ge(rr_ok, b + 1)
                        wait(act, sent[par], 16 * (b - par))
                        settle(act, b)
                        for t in range(TT):
                            act.activation(rows[:, par, t, 0:D], tile_of(XN, b, t), ACT.Copy,
                                           scale=rr[:, t:t + 1]).then_inc(rows_ok, 1)
                    if u == 1 and has(i):
                        negate(act, i, 1)
                    if u == 1 and has(i - 1):
                        b = i - 1
                        act.wait_ge(av_pe, UNITS * (b + 1))
                        wait(act, attn_ok, 4 * b)
                        act.activation(avs[:], AV, ACT.Copy).then_inc(av_sb, 1)
                    if u == 7 and early(i) and not has(i + 1):
                        scaled(act, i + 3)
                    if u == 2 and has(i + 1):
                        b = i + 1
                        act.wait_ge(prep_pe, 6 * b + 6)
                        wait(act, av_pe, UNITS * (b - 1))
                        act.activation(blocks(vst[:, 1 - par], 0),
                                       MISC[:, 0:T].rearrange("p (n h d) -> p n h d", n=2 * TT, h=H // 2),
                                       ACT.Copy).then_inc(v_sb, 1)
                    if u == 2 and has(i + 2) and not (early(i) and has(i + 1)):
                        scaled(act, i + 2)
                    if has(i + 2):
                        prep_act(act, i + 2, u)
                    if u == 6 and has(i + 1):
                        negate(act, i + 1, 0)
                    if u == (6 if has(i) else 1) and has(i - 1):
                        b = i - 1
                        act.wait_ge(x2_ok, b + 1)
                        wait(act, sqe_ok, b)
                        settle(act, b)
                        for t in range(TT):
                            act.activation(sq[:, t, :], tile_of(XN, b, t), ACT.Square,
                                           accum_out=ssq[:, t:t + 1]).then_inc(ssq_ok, 1)

            pad(act, 1)

            def high_features(s, par):
                act.wait_ge(yT_pe, s + 1)
                wait(act, hid_pe, 2 * s - 2)
                act.activation(yh[:, par, :], PS[:, 0, 0:P], ACT.Copy).then_inc(yh_ok, 1)

            def relus(s, par, at):
                act.wait_ge(hid_pe, 2 * s + 1)
                wait(act, out_pe, s - 1)
                settle(act, s)
                for c in range(HK // 2):
                    act.activation(hT3[:, par, c], PS[:, 1 + 2 * par, P * c:P * c + P], ACT.Relu,
                                   bias=w3[:, B1:B1 + E * HK][:, bass.ds(at, HK)][:, c:c + 1]).then_inc(relu_ok[0], 1)

            act.wait_ge(slots_ok, 4)
            columns = table_of(act, slot_h, 0, 1, HK * (E - 1))
            for s in range(3):
                high_features(s, s % 2)
            relus(0, 0, columns[0])
            for q, k in slots(act):
                s, par = RING3 * q + k, k % 2
                if k == 0:
                    columns = table_of(act, slot_h, RING3 * q, group(q, 1), HK * (E - 1))
                if later(s, 1):
                    relus(s + 1, 1 - par, columns[k + 1])
                if later(s, 3):
                    high_features(s + 3, 1 - par)

        def mask(pool, n, u):
            p = probs[:, u % RING, :]
            pool.wait_ge(exp_ok, n + 1)
            settle(pool, n)
            for blocks in (p[:, 0:2 * T].rearrange("p (h q) -> p h q", h=2)[:, :, 0:P],
                           p[:, 2 * T:CHUNK].rearrange("p (h q) -> p h q", h=2)):
                pool.affine_select(out=blocks, in_=blocks, compare_op=ALU.is_ge, fill=0.0, base=0,
                                   pattern=[[0, 2], [1, P]], channel_multiplier=-1).then_inc(mask_ok, 1)

        @block.gpsimd
        def _(pool):
            pool.memset(ident[:], 0.0).then_inc(ids, 1)
            pool.memset(causal[:], 0.0).then_inc(ids, 1)
            pool.wait_ge(ids, 2)
            pool.affine_select(out=ident[:], in_=ident[:], compare_op=ALU.not_equal, fill=1.0, base=0,
                               pattern=[[-1, P]], channel_multiplier=1).then_inc(ids, 1)
            pool.affine_select(out=causal[:], in_=causal[:], compare_op=ALU.is_ge, fill=-1.0e30, base=0,
                               pattern=[[0, 4], [-1, P]], channel_multiplier=1).then_inc(ids, 1)
            pool.memset(ones16[:], 1.0).then_inc(ones_ok, 1)
            pool.memset(half[:], -0.5).then_inc(consts, 1)
            pool.memset(kb[:], 0.0).then_inc(consts, 1)
            pool.memset(flat[:], 1.0 / D).then_inc(consts, 1)
            pool.wait_ge(consts, 3)
            pool.memset(vst[:], 0.0).then_inc(vst_ok, 1)
            pool.wait_ge(vst_ok, 1)
            for n in range(2):
                pool.memset(blocks(vst[:, n], P // 2), 1.0).then_inc(vst_ok, 1)
            for c in range(4):
                pool.wait_ge(stats_b, 4 * (c + 1))
                pool.tensor_scalar(rstd[:, 4 * c:4 * c + 4, 0:1], mv[:, 4 * c:4 * c + 4, 1:2], 1e-5, None,
                                   ALU.add).then_inc(var_eps, 1)
                pool.wait_ge(var_eps, c + 1)
                pool.tensor_tensor(rstd[:, 4 * c:4 * c + 4, 1:2], rstd[:, 4 * c:4 * c + 4, 0:1],
                                   half[:, 0:4].rearrange("p (a b) -> p a b", b=1), ALU.pow).then_inc(rstd_ok, 1)
            pool.wait_ge(w1_in, 16)
            for c in range(4):
                pool.wait_ge(x_in[c], 16)
                for t in range(4 * c, 4 * c + 4):
                    pool.tensor_tensor(XB[:, t, :], X[:, t, :], w1[:, BO:BO + D], ALU.add).then_inc(xb_ok, 1)
            pool.memset(tri[:], 1.0).then_inc(w4_ok, 1)
            pool.memset(onesb[:], 1.0).then_inc(w4_ok, 1)
            for e in range(E):
                pool.memset(cum[:, e:e + 1], float(REGION * e)).then_inc(w4_ok, 1)
            pool.wait_ge(w4_ok, 1)
            pool.affine_select(out=tri[:], in_=tri[:], compare_op=ALU.is_gt, fill=0.0, base=0,
                               pattern=[[1, P]], channel_multiplier=-1).then_inc(w4_ok, 1)
            pool.memset(blank[:, 0:2 * D], 0.0).then_inc(blank_ok, 1)
            pool.wait_ge(w2_in, 16)
            pool.wait_ge(w3_in, 16)
            pool.tensor_copy(blank[:, 2 * D:ROW], w3[:, TOKEN + NT:TOKEN + NT + 1]).then_inc(blank_ok, 1)
            pool.tensor_scalar(w3[:, W1:W1 + E * HID], w3[:, W1:W1 + E * HID], w2[:, N2:N2 + 1], GAIN,
                               ALU.mult, ALU.mult).then_inc(w3_ok, 1)
            pool.tensor_scalar(w3[:, B1:B1 + E * HK], w3[:, B1:B1 + E * HK], GAIN, None, ALU.mult).then_inc(w3_ok, 1)
            pool.wait_ge(w4_in, 16)
            gate = w4[:, GATE:GATE + E * D].rearrange("p (e d) -> p e d", e=E)
            pool.tensor_tensor(gate, gate, w4[:, N2ROW:N2ROW + D].rearrange("p (e d) -> p e d", e=1).broadcast_to(
                [P, E, D]), ALU.mult).then_inc(w4_ok, 1)
            for c in range(HK):
                pool.wait_ge(w1_halves, HK + c)
                pool.tensor_tensor(by_expert(w1l[c]), hidden_tile(c), by_expert(w1h[c]), ALU.subtract).then_inc(
                    w1_halves, 1)

            for i, par in steps(pool, -2, 9):
                for u in range(UNITS):
                    if has(i):
                        mask(pool, UNITS * i + u, u)
                    if (u == 0 and has(i + 2) and not (early(i) and has(i + 1))) or (u == 3 and early(i) and not has(i + 1)):
                        b = i + 2 if u == 0 else i + 3
                        pool.wait_ge(a_aggr, TT * (b + 1))
                        wait(pool, hs_ok, TT * b)
                        wait(pool, xn1_ok, TT * b)
                        settle(pool, b)
                        pool.tensor_scalar(aeps[:, 0, :], amv[:, :, 1], LN_EPS, None, ALU.add).then_inc(a_eps, 1)
                        pool.tensor_scalar(aeps[:, 1, :], amv[:, :, 1], 1.0 + RMS_EPS, LN_EPS * RMS_EPS,
                                           ALU.mult, ALU.add).then_inc(a_eps, 1)
                        pool.wait_ge(a_eps, 2 * b + 2)
                        pool.tensor_tensor(ars[:], aeps[:], half[:, 0:2 * TT].rearrange("p (a b) -> p a b", b=TT),
                                           ALU.pow).then_inc(a_rstd, 1)
                    if u == 4 and has(i + 2):
                        b = i + 2
                        pool.wait_ge(l_aggr, TT * (b + 1))
                        wait(pool, latn_ok, TT * b)
                        settle(pool, b)
                        pool.tensor_scalar(leps[:], lmv[:, :, 1], LN_EPS, None, ALU.add).then_inc(l_eps, 1)
                        pool.wait_ge(l_eps, b + 1)
                        pool.tensor_tensor(lrs[:], leps[:], half[:, 0:TT], ALU.pow).then_inc(l_rstd, 1)
                    if u == (7 if has(i) else 0) and has(i - 1):
                        b = i - 1
                        pool.wait_ge(ssq_ok, TT * b + TT)
                        wait(pool, rr_ok, b)
                        settle(pool, b)
                        pool.tensor_scalar(sqe[:], ssq[:], 1.0 / D, RMS_EPS, ALU.mult, ALU.add).then_inc(sqe_ok, 1)
                        pool.wait_ge(sqe_ok, b + 1)
                        wait(pool, rows_ok, TT * b)
                        settle(pool, b)
                        pool.tensor_tensor(rr[:], sqe[:], half[:, 0:TT], ALU.pow).then_inc(rr_ok, 1)
                    if u == (7 if has(i) else 0) and has(i - 1):
                        b, n = i - 1, 1 - par
                        pool.wait_ge(x2_ok, b + 1)
                        wait(pool, sent[n], 16 * (b - n))
                        settle(pool, b)
                        for t in range(TT):
                            pool.tensor_tensor(rows[:, n, t, D:2 * D], tile_of(X, b, t), tile_of(XN, b, t),
                                               ALU.add).then_inc(xs_ok, 1)
                        pool.tensor_copy(rows[:, n, :, 2 * D], w3[:, bass.ds(TT * b + TOKEN, TT)]).then_inc(xs_ok, 1)
                    if u == (6 if has(i) else 4) and has(i - 2):
                        b = i - 2
                        pool.wait_ge(pos_ok, b + 1)
                        pool.wait_ge(xs_ok, (TT + 1) * (b + 1))
                        settle(pool, b)
                        for t in range(TT):
                            pool.indirect_dma_start(sorted_rows, bass.IndirectOffsetOnAxis(ap=pos[:, par, t:t + 1], axis=0),
                                                    rows[:, par, t, :], None).then_inc(sent[par], 16)

            pool.wait_ge(slots_ok, 4)

            def residual(q, k):
                s = RING3 * q + k
                at = pool.value_load(slot_b[0:1, bass.ds(s, 1)], min_val=0, max_val=D * (E - 1))
                pool.wait_ge(srt_in[k], 16 * (q + 1))
                wait(pool, fin_ok, s - RING3 + 1)
                settle(pool, s)
                pool.tensor_tensor(res[:, k, :], srt[:, k, D:2 * D], w4[:, B2:B2 + E * D][:, bass.ds(at, D)],
                                   ALU.add).then_inc(res_ok, 1)

            residual(0, 0)
            residual(0, 1)
            for q, k in slots(pool):
                s, par = RING3 * q + k, k % 2
                if later(s, 2):
                    residual(q + (k + 2) // RING3, (k + 2) % RING3)
                pool.wait_ge(fin_ok, s + 1)
                settle(pool, s)
                pool.indirect_dma_start(out.rearrange("b t d -> (b t) d"),
                                        bass.IndirectOffsetOnAxis(ap=where[:, k:k + 1], axis=0), fin[:, k, :],
                                        None, bounds_check=NT * P - 1, oob_is_err=False).then_inc(put[par], 16)

        def scores(pe, b, par, u):
            n = UNITS * b + u
            if u == 0:
                pe.wait_ge(m_in[0], 16 * (b + 1))
            if u == 4:
                pe.wait_ge(m_in[1], 16 * (b + 1))
            wait(pe, exp_ok, n - 1)
            for j in range(2):
                pe.matmul(EX[u % 2][:, T * j:T * j + T], ks[:, par, 2 * u + j, 0:P],
                          qs[:, par, 2 * u + j, :], start=True, stop=True)
            for j in range(2):
                ins = pe.matmul(EX[u % 2][:, 2 * T + P * j:2 * T + P * j + P], ks[:, par, 2 * u + j, P:T],
                                qs[:, par, 2 * u + j, P:T], start=True, stop=True)
            ins.then_inc(sc_pe, 1)

        def weigh(pe, b, par, u):
            n = UNITS * b + u
            pe.wait_ge(mask_ok, 2 * n + 2)
            if u == 0:
                wait(pe, av_sb, b)
                pe.wait_ge(v_sb, b + 1)
            for j in range(2):
                h = 2 * u + j
                out = AV[:, T * (h // 8):T * (h // 8) + T]
                pe.matmul(out, vst[:, par, 0, h, :], probs[:, u % RING, T * j:T * j + T], start=(h % 8 == 0),
                          stop=False, skip_group_check=True)
                ins = pe.matmul(out[:, P:T], vst[:, par, 1, h, :], probs[:, u % RING, 2 * T + P * j:2 * T + P * j + P],
                                start=False, stop=(h % 8 == 7), skip_group_check=True)
            ins.then_inc(av_pe, 1)

        def maxima(pe, b, par, v):
            n = MAXU * b + v
            if v == 0:
                pe.wait_ge(stack_in, 128 * (b + 1))
            wait(pe, max_ok, n - 1)
            bank = PS[:, 4 + v % 2, :]
            g, r = v // 3, v % 3
            rows = 4 * DH
            if r < 2:
                for j in range(2):
                    h = 4 * g + 2 * r + j
                    pe.matmul(bank[:, T * j:T * j + T], qs[0:rows, par, h, P:T], ks[0:rows, par, h, :],
                              start=(j == 0), stop=False, skip_group_check=True)
                ins = pe.matmul(bank.rearrange("p (h k) -> p h k", h=2)[:, :, P:T], identb[:], causal[:, 0:2, :],
                                start=False, stop=True, skip_group_check=True)
            else:
                for j in range(4):
                    h = 4 * g + j
                    pe.matmul(bank[:, P * j:P * j + P], qs[0:rows, par, h, 0:P], ks[0:rows, par, h, 0:P],
                              start=(j == 0), stop=False, skip_group_check=True)
                ins = pe.matmul(bank, identb[:], causal[:].rearrange("p a b -> p (a b)"),
                                start=False, stop=True, skip_group_check=True)
            ins.then_inc(max_pe, 1)

        def turn_maxima(pe, b, par, half):
            pe.wait_ge(max_ok, MAXU * b + (half + 1) * MAXU // 2)
            if half == 0 and has(b + 1):
                pe.wait_ge(latT_sb, b + 2)
            elif half == 0:
                pe.wait_ge(place_ok, b - 2)
            elif has(b + 1):
                pe.wait_ge(k_tmp, b + 2)
            else:
                pe.wait_ge(m_neg, 2 * b + 1)
            for t in range(TT):
                ins = pe.transpose(MISC[0:H // 2, P * t:P * t + P], mx[:, par, t, 8 * half:8 * half + 8], ident[:])
            ins.then_inc(m_pe, 1)

        def finish(pe, b):
            pe.wait_ge(attn_ok, 4 * b + 4)
            if has(b + 3):
                pe.wait_ge(q_tmp, b + 4)
            elif has(b + 2):
                pe.wait_ge(v_sb, b + 3)
            elif has(b + 1):
                pe.wait_ge(m_neg, 2 * b + 4)
            else:
                pe.wait_ge(place_ok, b - 1)
            for t in range(TT):
                ins = pe.matmul(MISC[:, P * t:P * t + P], attnT[:, P * t:P * t + P], w2[:, WOF:WOF + P],
                                start=True, stop=True)
            ins.then_inc(fin_pe, 1)

        def places(pe, b):
            pe.wait_ge(hit_ok, b + 1)
            wait(pe, cum_ok, TT * b)
            if has(b + 1):
                pe.wait_ge(x2_ok, b + 2)
            else:
                pe.wait_ge(place_ok, b)
            settle(pe, b)
            for t in range(TT):
                o = MISC[:, E * t:E * t + E]
                pe.matmul(o, tri[:], hit[:, t, :], start=True, stop=False)
                for before in range(t):
                    pe.matmul(o, onesb[:], hit[:, before, :], start=False, stop=False)
                ins = pe.matmul(o, onesb[:], cum[:], start=False, stop=True)
            ins.then_inc(place_pe, 1)

        def values(pe, b):
            pe.wait_ge(k_tmp, b + 1)
            wait(pe, m_neg, 2 * b)
            for t in range(TT):
                ins = pe.matmul(MISC[:, P * t:P * t + P], latT[:, P * t:P * t + P], w2[0:L, WUV:WUV + P],
                                start=True, stop=True)
            ins.then_inc(prep_pe, 1)

        def prep_pe_step(pe, b, n):
            if n == 0:
                pe.wait_ge(hs_ok, TT * (b + 1))
                wait(pe, v_sb, b)
                for t in range(TT):
                    ins = pe.transpose(MISC[:, P * t:P * t + P], hs[:, t, :], ident[:])
                ins.then_inc(prep_pe, 1)
            if n == 1:
                pe.wait_ge(hT_sb, b + 1)
                for t in range(TT):
                    ins = pe.matmul(MISC[:, L * t:L * t + L], hT[:, P * t:P * t + P], w2[:, WDKV:WDKV + L],
                                    start=True, stop=True)
                ins.then_inc(prep_pe, 1)
            if n == 2:
                pe.wait_ge(lat_sb, b + 1)
                pe.matmul(MISC[:, 0:T], w2[:, WQ:WQ + P], hT[:], start=True, stop=True)
                pe.matmul(MISC[:, T:2 * T], w2[:, WQR:WQR + P], hT[:], start=True, stop=True).then_inc(prep_pe, 1)
            if n == 3:
                pe.wait_ge(latn_ok, TT * (b + 1))
                if has(b - 4):
                    pe.wait_ge(place_ok, b - 3)
                elif has(b - 3):
                    pe.wait_ge(x2_ok, b - 2)
                else:
                    pe.wait_ge(q_tmp, b + 1)
                settle(pe, b)
                for t in range(TT):
                    ins = pe.transpose(MISC[0:L, P * t:P * t + P], latn[:, t, :], ident[:])
                ins.then_inc(prep_pe, 1)
            if n == 4:
                pe.wait_ge(latT_sb, b + 1)
                wait(pe, m_neg, 2 * b - 1)
                pe.matmul(MISC[:, 0:T], w2[0:L, WUK:WUK + P], latT[:], start=True, stop=True)
                pe.matmul(MISC[:, T:2 * T], w2[0:L, WUKR:WUKR + P], latT[:], start=True,
                          stop=True).then_inc(prep_pe, 1)

        @block.tensor
        def _(pe):
            pe.wait_ge(w1_in, 16)
            pe.matmul(PS[:, 4, 0:129], w1[:, WKT:WKT + P], w1[:, WQB:WQB + 129], start=True, stop=True)
            pe.matmul(PS[:, 4, 129:257], w1[:, WVT:WVT + P], w1[:, WO:WO + P], start=True, stop=True).then_inc(fold_pe, 1)
            pe.wait_ge(bias_rows, 2)
            pe.matmul(PS[:, 5, 0:129], bkv[:, 0, :], w1[:, WQB:WQB + 129], start=True, stop=True)
            pe.matmul(PS[:, 5, 129:257], bkv[:, 1, :], w1[:, WO:WO + P], start=True, stop=True).then_inc(fold_pe, 1)
            pe.wait_ge(fold_sb, 2)
            for n in range(PAIRS):
                pe.matmul(PS[:, n, 0:257], w1[:, CTX + P * n:CTX + P * n + P], mn[:], start=True,
                          stop=True).then_inc(kqv_pe, 1)
            pe.wait_ge(kqv_sb, PAIRS)
            pe.wait_ge(fk_in, 16)
            for par in range(2):
                rows = slice(S * par, S * par + S)
                for f in range(2):
                    pe.matmul(PS[:, 4 + 2 * par + f, :].rearrange("p (a b) -> p a b", b=P),
                              fk[rows, P * f:P * f + P], kqv[rows, :, 0:P],
                              start=True, stop=True).then_inc(kdft_pe, 1)
            pe.wait_ge(fx_in, 16)
            for par in range(2):
                for f in range(2):
                    for h in range(TT):
                        pe.wait_ge(xn_ok, NT)
                        ins = pe.matmul(PS[:, 2 * par + f, :].rearrange("p (a b) -> p a b", b=P),
                                        fx[:, h, P * f:P * f + P],
                                        XN[:].rearrange("p (a c h) d -> p c h a d", c=2, h=2)[:, par, h],
                                        start=(h == 0), stop=(h == TT - 1))
                    ins.then_inc(xdft_pe, 1)
            pe.wait_ge(cross_ok, 4)
            pe.wait_ge(kqv_sb, PAIRS + 2)
            pe.wait_ge(iv_in, 16)
            pe.matmul(PS[0:B, 4, 0:T], cross[:, 0].rearrange("p a b -> p (a b)"), iv[:, 0, :], start=True, stop=False)
            pe.matmul(PS[0:B, 4, 0:T], cross[:, 1].rearrange("p a b -> p (a b)"), iv[:, 1, :], start=False, stop=False)
            pe.matmul(PS[0:B, 4, 0:T], kb[:].rearrange("p a b -> p (a b)"), flat[:], start=False,
                      stop=True).then_inc(mean_pe, 1)
            pe.wait_ge(prod_ok, 4)
            for n in range(WARM):
                pe.matmul(PS[:, 5, :], w1[:, 0:P], fx[:].rearrange("p a b -> p (a b)"), start=True, stop=True)
            for b in range(B):
                pe.wait_ge(circ_in[b], 16)
                rows = slice(S * (b % 2), S * (b % 2) + S)
                for h in range(TT):
                    at = T * (b // 2 % 2) + P * h
                    ins = pe.matmul(PS[:, 2 * (b % 2) + b // 4, at:at + P], circ[rows, b // 2, P * h:P * h + P],
                                    kqv[rows, b // 2, 129:257], start=True, stop=True)
                ins.then_inc(x1_pe, 1)

            pe.wait_ge(ids, 4)
            pe.wait_ge(vst_ok, 3)
            pe.wait_ge(w2_ok, 2)
            pe.wait_ge(ones_in, 16)
            pe.wait_ge(x1_ok, 4)
            pe.wait_ge(w4_ok, 3 + E)
            for i, par in steps(pe, -2, 9):
                for u in range(UNITS):
                    if has(i):
                        scores(pe, i, par, u)
                    if u == 1 and has(i):
                        turn_maxima(pe, i, par, 1)
                    if u == 2 and has(i + 1):
                        values(pe, i + 1)
                    if u == 3 and has(i + 2) and has(i):
                        prep_pe_step(pe, i + 2, 0)
                    if u == 5 and has(i - 1) and has(i):
                        finish(pe, i - 1)
                    if u == 6 and has(i + 2):
                        prep_pe_step(pe, i + 2, 3)
                    if u >= 2 and has(i):
                        weigh(pe, i, par, u - 2)
                    if u < 2 and has(i - 1):
                        weigh(pe, i - 1, 1 - par, UNITS - 2 + u)
                    if u == 4 and has(i + 2):
                        prep_pe_step(pe, i + 2, 2)
                    if u == 1 and has(i - 1) and not has(i):
                        finish(pe, i - 1)
                    if u == (5 if has(i) else 3) and has(i - 2):
                        places(pe, i - 2)
                    if u == 6 and has(i + 1):
                        turn_maxima(pe, i + 1, 1 - par, 0)
                    if u in (2, 3, 6) and has(i + 2) and not has(i):
                        prep_pe_step(pe, i + 2, u - 2)
                    if u >= 2 and has(i + 1):
                        maxima(pe, i + 1, 1 - par, 2 * (u - 2))
                        maxima(pe, i + 1, 1 - par, 2 * (u - 2) + 1)
                    if u in (3, 6) and has(i + 2) and has(i):
                        prep_pe_step(pe, i + 2, u - 2)

            pe.wait_ge(cum_ok, TT * B)
            pe.matmul(MISC[:, 0:E], onesb[:], cum[:], start=True, stop=True).then_inc(total_pe, 1)

            def turn_rows(q, k):
                s = RING3 * q + k
                pe.wait_ge(srt_in[k], 16 * (q + 1))
                wait(pe, yl_ok, s)
                pe.transpose(PS[:, 0, 0:P], srt[:, k, 0:D], ident[:]).then_inc(yT_pe, 1)

            def hidden(s, par, c, at):
                o = PS[:, 1 + 2 * par + c // 2, P * (c % 2):P * (c % 2) + P]
                high, low = w1h[c][:, bass.ds(at, P)], w1l[c][:, bass.ds(at, P)]
                pe.matmul(o, high, yh[:, par, :], start=True, stop=False)
                pe.matmul(o, high, yl[:, par, :], start=False, stop=False)
                ins = pe.matmul(o, low, yh[:, par, :], start=False, stop=True)
                if c % 2:
                    ins.then_inc(hid_pe, 1)

            pe.wait_ge(slots_ok, 4)
            pe.wait_ge(w1_halves, 2 * HK)
            pe.wait_ge(second_in, 16 * HK)
            weights = table_of(pe, slot_b, 0, 2, D * (E - 1))
            for s in range(3):
                turn_rows(0, s)
            for s in range(2):
                pe.wait_ge(yl_ok, s + 1)
                for c in range(HK):
                    hidden(s, s, c, weights[s])
            for q, k in slots(pe):
                s, par = RING3 * q + k, k % 2
                if k == 0:
                    weights = table_of(pe, slot_b, RING3 * q, group(q, 2), D * (E - 1))
                pe.wait_ge(relu_ok[0], 2 * s + 2)
                pe.wait_ge(relu_ok[1], 2 * s + 2)
                wait(pe, fin_ok, s - 1)
                if later(s, 2):
                    pe.wait_ge(yl_ok, s + 3)
                if later(s, 3):
                    turn_rows(q + (k + 3) // RING3, (k + 3) % RING3)
                for c in range(HK):
                    ins = pe.matmul(PS[:, 5 + par, 0:D], hT3[:, par, c], second[c][:, bass.ds(weights[k], D)],
                                    start=(c == 0), stop=(c == HK - 1))
                    if c == HK - 1:
                        ins.then_inc(out_pe, 1)
                    if later(s, 2):
                        hidden(s + 2, par, c, weights[k + 2])

        def norm(dve, c):
            dve.wait_ge(rstd_ok, c + 1)
            for t in range(4 * c, 4 * c + 4):
                dve.tensor_scalar(XN[:, t, :], X[:, t, :], mv[:, t, 0:1], rstd[:, t, 1:2],
                                  ALU.subtract, ALU.mult).then_inc(xn_ok, 1)

        def rotate(dve, b, filled, tmp, total):
            dve.wait_ge(prep_pe, filled)
            dve.tensor_tensor(rope[:], MISC, w2[:, ROPE:ROPE + 512], ALU.mult).then_inc(tmp, 1)
            dve.wait_ge(tmp, b + 1)
            dve.tensor_tensor(qk[:], rope[:, 0:T], rope[:, T:2 * T], ALU.add).then_inc(total, 1)
            dve.wait_ge(total, b + 1)

        def low_half(dve, b, n, high, done):
            wait(dve, stack_in, 128 * b)
            dve.wait_ge(high, b + 1)
            dve.tensor_tensor(parts[:, n, 1, :], qk[:], parts[:, n, 0, :], ALU.subtract).then_inc(done, 1)

        def prep_dve(dve, b, u):
            if u == 0:
                for t in range(TT):
                    dve.bn_stats(ast[:, t, :], tile_of(X, b, t)).then_inc(a_stats, 1)
                for t in range(TT):
                    dve.wait_ge(a_stats, TT * b + t + 1)
                    settle(dve, b)
                    dve.bn_aggr(amv[:, t, :], ast[:, t, :]).then_inc(a_aggr, 1)
            if u == 1:
                dve.wait_ge(a_rstd, b + 1)
                wait(dve, hs_ok, TT * b)
                wait(dve, xn1_ok, TT * b)
                dve.scalar_tensor_tensor(out=nbias[:], in0=amv[:, :, 0:1].rearrange("p t a -> p a t").broadcast_to(
                    [P, 2, TT]), scalar=-1.0, in1=ars[:], op0=ALU.mult, op1=ALU.mult).then_inc(nbias_ok, 1)
            if u == 4:
                dve.wait_ge(lat_sb, b + 1)
                for t in range(TT):
                    dve.bn_stats(lst[:, t, :], lat[:, t, :]).then_inc(l_stats, 1)
                for t in range(TT):
                    dve.wait_ge(l_stats, TT * b + t + 1)
                    settle(dve, b)
                    dve.bn_aggr(lmv[:, t, :], lst[:, t, :]).then_inc(l_aggr, 1)
            if u == 4:
                rotate(dve, b, 6 * b + 3, q_tmp, q_sum)
            if u == 5:
                dve.wait_ge(l_rstd, b + 1)
                for t in range(TT):
                    dve.tensor_scalar(latn[:, t, :], lat[:, t, :], lmv[:, t, 0:1], lrs[:, t:t + 1],
                                      ALU.subtract, ALU.mult).then_inc(latn_ok, 1)
            if u == 7:
                rotate(dve, b, 6 * b + 5, k_tmp, k_sum)

        def normalize(dve, b, parts_of):
            for c in parts_of:
                dve.wait_ge(av_sb, b + 1)
                dve.reciprocal(rec[:, P * c:P * c + P], avs[P // 2:P, P * c:P * c + P]).then_inc(rec_ok, 1)
            for c in parts_of:
                dve.wait_ge(rec_ok, 4 * b + c + 1)
                wait(dve, fin_pe, b)
                n, at = c // 2, P * (c % 2)
                dve.tensor_tensor(attnT[64 * n:64 * n + 64, at:at + P], avs[0:P // 2, P * c:P * c + P],
                                  rec[:, P * c:P * c + P], ALU.mult).then_inc(attn_ok, 1)

        def row_max(dve, b, par, v):
            dve.wait_ge(max_pe, MAXU * b + v + 1)
            bank = PS[:, 4 + v % 2, :]
            g, r = v // 3, v % 3
            if r < 2:
                dve.tensor_reduce(mx[:, par, 1, 4 * g + 2 * r:4 * g + 2 * r + 2],
                                  bank.rearrange("p (h k) -> p h k", h=2), AX_X, ALU.max).then_inc(max_ok, 1)
            else:
                dve.tensor_reduce(mx[:, par, 0, 4 * g:4 * g + 4],
                                  bank.rearrange("p (h k) -> p h k", h=4), AX_X, ALU.max).then_inc(max_ok, 1)

        def score(dve, b, par):
            dve.wait_ge(rows_ok, TT * b + TT)
            for t in range(TT):
                for e in range(E):
                    dve.scalar_tensor_tensor(out=dot[:, t, e], in0=rows[:, par, t, 0:D], scalar=1.0,
                                             in1=w4[:, GATE + D * e:GATE + D * e + D], op0=ALU.mult, op1=ALU.mult,
                                             accum_out=logit[:, t, e:e + 1]).then_inc(logit_ok, 1)

        def choose(dve, b):
            row = lambda at: w4[:, at:at + E].rearrange("p (t e) -> p t e", t=1).broadcast_to([P, TT, E])
            dve.wait_ge(logit_ok, TT * E * (b + 1))
            dve.tensor_tensor(logit[:], logit[:], row(GB), ALU.add).then_inc(choice, 1)
            dve.wait_ge(choice, 5 * b + 1)
            dve.tensor_reduce(lead[:], logit[:], AX_X, ALU.max).then_inc(choice, 1)
            dve.wait_ge(choice, 5 * b + 2)
            dve.tensor_tensor(tied[:], logit[:], lead[:].broadcast_to([P, TT, E]), ALU.is_equal).then_inc(choice, 1)
            dve.wait_ge(choice, 5 * b + 3)
            dve.tensor_tensor(tied[:], tied[:], row(RANK), ALU.mult).then_inc(choice, 1)
            dve.wait_ge(choice, 5 * b + 4)
            dve.tensor_reduce(lead[:], tied[:], AX_X, ALU.max).then_inc(choice, 1)
            dve.wait_ge(choice, 5 * b + 5)
            wait(dve, cum_ok, TT * b)
            dve.tensor_tensor(hit[:], row(RANK), lead[:].broadcast_to([P, TT, E]), ALU.is_equal).then_inc(hit_ok, 1)

        def rank(dve, b, par):
            dve.wait_ge(place_pe, b + 1)
            dve.tensor_tensor(place[:], MISC[:, 0:TT * E].rearrange("p (t e) -> p t e", t=TT), hit[:],
                              ALU.mult).then_inc(place_ok, 1)
            dve.wait_ge(hit_ok, b + 1)
            for t in range(TT):
                wait(dve, cum_ok, TT * b + t)
                dve.tensor_tensor(cum[:], cum[:], hit[:, t, :], ALU.add).then_inc(cum_ok, 1)
            dve.wait_ge(place_ok, b + 1)
            with nc.allow_low_precision(reason="row numbers are whole"):
                dve.tensor_reduce(pos[:, par, :].rearrange("p (t e) -> p t e", e=1), place[:], AX_X,
                                  ALU.add).then_inc(pos_ok, 1)

        @block.vector
        def _(dve):
            for c in range(4):
                dve.wait_ge(x_in[c], 16)
                for t in range(4 * c, 4 * c + 4):
                    dve.bn_stats(bst[:, t, :], X[:, t, :]).then_inc(stats_a, 1)
                for t in range(4 * c, 4 * c + 4):
                    dve.wait_ge(stats_a, t + 1)
                    dve.bn_aggr(mv[:, t, :], bst[:, t, :]).then_inc(stats_b, 1)
                if c == 0:
                    dve.wait_ge(w1_in, 16)
                    for n in range(2):
                        dve.tensor_copy(bkv[:, n, :], w1[:, BKV + n:BKV + n + 1].broadcast_to([P, P])).then_inc(
                            bias_rows, 1)
                    dve.wait_ge(fold_pe, 1)
                    dve.tensor_copy(mn[:], PS[:, 4, 0:257]).then_inc(fold_sb, 1)
                if c == 1:
                    dve.wait_ge(fold_pe, 2)
                    dve.tensor_copy(biasbc[:], PS[:, 5, 0:257]).then_inc(fold_sb, 1)
                    norm(dve, 0)
                    dve.wait_ge(fold_sb, 2)
                    for n in range(PAIRS):
                        dve.wait_ge(kqv_pe, n + 1)
                        dve.tensor_tensor(kqv[:, n, :], PS[:, n, 0:257], biasbc[:], ALU.add).then_inc(kqv_sb, 1)
                if c > 1:
                    norm(dve, c - 1)
            norm(dve, 3)
            dve.wait_ge(kqv_sb, PAIRS)
            dve.wait_ge(consts, 3)
            for par in range(2):
                part = slice(S * par, S * par + S)
                dve.tensor_copy(kb[part, :, par:par + 1], kqv[part, :, P:P + 1]).then_inc(kqv_sb, 1)
            for n in range(4):
                dve.wait_ge(xdft_pe, n + 1)
                dve.wait_ge(kdft_sb, n + 1)
                dve.tensor_tensor(prod[:, n, :], PS[:, n, :], kd[:, n, :], ALU.mult).then_inc(prod_ok, 1)
                dve.wait_ge(prod_ok, n + 1)
                dve.tensor_reduce(cross[:, n % 2, :, n // 2:n // 2 + 1], prod[:, n, :].rearrange("p (a b) -> p a b", b=P),
                                  AX_X, ALU.add).then_inc(cross_ok, 1)
            dve.wait_ge(w2_in, 16)
            dve.tensor_scalar(w2[:, WQ:WDKV + L], w2[:, WQ:WDKV + L], w2[:, N1:N1 + 1], None,
                              ALU.mult).then_inc(w2_ok, 1)
            dve.wait_ge(ids, 3)
            dve.tensor_copy(identb[:], ident[:]).then_inc(w2_ok, 1)
            dve.memset(top[:, 16:24], LOWEST).then_inc(topk, 1)
            dve.wait_ge(mean_pe, 1)
            dve.tensor_copy(mean[:], PS[0:B, 4, 0:T]).then_inc(topk, 1)
            dve.wait_ge(topk, 2)
            dve.max(top[:, 0:8], mean[:]).then_inc(topk, 1)
            dve.wait_ge(topk, 3)
            dve.tensor_scalar(tot[:, 0:1], top[:, 0:1], -1.0, None, ALU.mult).then_inc(topk, 1)
            dve.match_replace(work[:, 0, :], top[:, 0:8], mean[:], LOWEST).then_inc(topk, 1)
            dve.wait_ge(topk, 5)
            dve.max(top[:, 8:16], work[:, 0, :]).then_inc(topk, 1)
            dve.wait_ge(topk, 6)
            dve.tensor_copy(top[:, 16:16 + TOPK - 8], top[:, 8:8 + TOPK - 8]).then_inc(topk, 1)
            dve.wait_ge(topk, 7)
            dve.match_replace(work[:, 0, :], top[:, 16:24], work[:, 0, :], LOWEST).then_inc(topk, 1)
            dve.wait_ge(topk, 8)
            dve.wait_ge(mean_exp, 1)
            dve.scalar_tensor_tensor(out=work[:, 0, :], in0=work[:, 0, :], scalar=0.99 * LOWEST, in1=work[:, 1, :],
                                     op0=ALU.is_le, op1=ALU.mult, accum_out=tot[:, 1:2]).then_inc(topk, 1)
            dve.wait_ge(topk, 9)
            dve.reciprocal(tot[:, 2:3], tot[:, 1:2]).then_inc(topk, 1)
            dve.wait_ge(topk, 10)
            dve.tensor_scalar(soft[:].rearrange("p (a b) -> p a b", a=2), work[:, 0:1, :].broadcast_to([B, 2, T]),
                              tot[:, 2:3], None, ALU.mult).then_inc(soft_ok, 1)
            dve.wait_ge(xb_ok, NT)
            for n in range(4):
                par, g = n % 2, n // 2
                dve.wait_ge(x1_pe, 4 * g + 3 + par)
                dve.tensor_tensor(tiles(X, par, g), PS[:, 2 * par + g, :].rearrange("p (a d) -> p a d", d=T),
                                  tiles(XB, par, g), ALU.add).then_inc(x1_ok, 1)
                if n == 0:
                    dve.wait_ge(x1_ok, 1)
                    prep_dve(dve, 0, 0)
                if n == 1:
                    prep_dve(dve, 0, 1)
            dve.wait_ge(w4_ok, 3 + E + 1)
            dve.wait_ge(x1_ok, 4)
            for i, par in steps(dve, -2, 9):
                for u in range(UNITS):
                    if u == (5 if has(i) else 1) and has(i - 1):
                        b = i - 1
                        dve.wait_ge(fin_pe, b + 1)
                        dve.wait_ge(xn1_ok, TT * (b + 1))
                        dve.tensor_tensor(tile_of(XN, b, 0, TT), MISC[:, 0:T], tile_of(XN, b, 0, TT),
                                          ALU.add).then_inc(x2_ok, 1)
                    if has(i + 2) and u == 0 and not early(i):
                        prep_dve(dve, i + 2, 0)
                    if has(i - 1) and not has(i) and u == 0:
                        normalize(dve, i - 1, range(4))
                    if u == 0 and has(i - 2):
                        score(dve, i - 2, par)
                    if u == (0 if has(i) else 2) and has(i - 2):
                        choose(dve, i - 2)
                    if has(i + 2) and u == 1 and not early(i):
                        prep_dve(dve, i + 2, 1)
                    if u == 3 and has(i + 3) and not has(i + 1):
                        prep_dve(dve, i + 3, 0)
                    if has(i - 1) and has(i) and 1 <= u <= 4:
                        normalize(dve, i - 1, [u - 1])
                    if has(i + 2) and u >= 2:
                        prep_dve(dve, i + 2, u)
                    if u == 6 and has(i + 3) and not has(i + 1):
                        prep_dve(dve, i + 3, 1)
                    if u == (5 if has(i) else 3) and has(i - 2):
                        rank(dve, i - 2, par)
                    if u == 7 and has(i + 2) and not has(i):
                        low_half(dve, i + 2, 1, k_hi, k_ok)
                    if u >= 2 and has(i + 1):
                        row_max(dve, i + 1, 1 - par, 2 * (u - 2))
                        row_max(dve, i + 1, 1 - par, 2 * (u - 2) + 1)
                    if u == 4 and has(i + 2):
                        low_half(dve, i + 2, 0, q_hi, q_ok)
                    if u == 7 and has(i + 2) and has(i):
                        low_half(dve, i + 2, 1, k_hi, k_ok)
            dve.wait_ge(total_pe, 1)
            flat_of = lambda a: a.rearrange("p (e n) -> p e n", n=1)
            edges = w4[0:1, EDGE:EDGE + E * NT].rearrange("p (e n) -> p e n", e=E)
            dve.tensor_tensor(full[:], flat_of(MISC[0:1, 0:E]).broadcast_to([1, E, NT]), edges,
                              ALU.is_gt).then_inc(table, 1)
            dve.tensor_copy(pad_at[:], MISC[0:1, 0:E]).then_inc(slots_ok, 1)
            dve.wait_ge(table, 1)
            dve.tensor_reduce(flat_of(count[:]), full[:], AX_X, ALU.add).then_inc(table, 1)
            dve.wait_ge(table, 2)
            dve.tensor_scalar(shift[:], count[:], -1.0, float(REGION), ALU.mult, ALU.add).then_inc(table, 1)
            dve.tensor_copy(ends[:, 0:1], count[:, 0:1]).then_inc(table, 1)
            for e in range(1, E):
                dve.wait_ge(table, 3 + e)
                dve.tensor_tensor(ends[:, e:e + 1], ends[:, e - 1:e], count[:, e:e + 1], ALU.add).then_inc(table, 1)
            dve.wait_ge(table, 3 + E)
            slot = w4[0:1, SLOT:SLOT + SLOTS]
            across = lambda a: a.rearrange("p (n e) -> p n e", n=1).broadcast_to([1, SLOTS, E])
            dve.tensor_tensor(beyond[:], slot.rearrange("p (n e) -> p n e", e=1).broadcast_to([1, SLOTS, E]),
                              across(ends[:]), ALU.is_ge).then_inc(table, 1)
            dve.wait_ge(table, 4 + E)
            dve.tensor_tensor(skip[:], beyond[:], across(shift[:]), ALU.mult).then_inc(table, 1)
            dve.tensor_reduce(chosen[:].rearrange("p (n e) -> p n e", e=1), beyond[:, :, 0:E - 1], AX_X,
                              ALU.add).then_inc(table, 1)
            dve.wait_ge(table, 5 + E)
            dve.tensor_reduce(base[:].rearrange("p (n e) -> p n e", e=1), skip[:], AX_X, ALU.add).then_inc(table, 1)
            dve.wait_ge(table, 6 + E)
            dve.tensor_scalar(slot_b[:], chosen[:], float(D), None, ALU.mult).then_inc(slots_ok, 1)
            dve.tensor_scalar(slot_h[:], chosen[:], float(HK), None, ALU.mult).then_inc(slots_ok, 1)
            dve.wait_ge(table, 7 + E)
            dve.scalar_tensor_tensor(out=slot_row[:], in0=base[:], scalar=float(P), in1=w4[0:1, SLOTP:SLOTP + SLOTS],
                                     op0=ALU.mult, op1=ALU.add).then_inc(slots_ok, 1)

            def low_features(s, par):
                dve.wait_ge(yh_ok, s + 1)
                wait(dve, hid_pe, 2 * s - 2)
                dve.tensor_tensor(yl[:, par, :], PS[:, 0, 0:P], yh[:, par, :], ALU.subtract).then_inc(yl_ok, 1)

            def relus(s, par, at):
                dve.wait_ge(hid_pe, 2 * s + 2)
                wait(dve, out_pe, s - 1)
                for c in range(HK // 2, HK):
                    dve.tensor_scalar(hT3[:, par, c], PS[:, 2 + 2 * par, P * (c % 2):P * (c % 2) + P],
                                      w3[:, B1:B1 + E * HK][:, bass.ds(at, HK)][:, c:c + 1], 0.0, ALU.add,
                                      ALU.max).then_inc(relu_ok[1], 1)

            dve.wait_ge(slots_ok, 4)
            columns = table_of(dve, slot_h, 0, 1, HK * (E - 1))
            def numbers(q, k):
                dve.wait_ge(srt_in[k], 16 * (q + 1))
                wait(dve, put[k % 2], 32 * q - 16 + 16 * (k // 2) if not isinstance(q, int) or q else 0)
                dve.tensor_copy(where[:, k:k + 1], srt[:, k, 2 * D:ROW]).then_inc(where_ok, 1)

            for s in range(3):
                low_features(s, s % 2)
            numbers(0, 0)
            numbers(0, 1)
            relus(0, 0, columns[0])
            for q, k in slots(dve):
                s, par = RING3 * q + k, k % 2
                if k == 0:
                    columns = table_of(dve, slot_h, RING3 * q, group(q, 1), HK * (E - 1))
                if later(s, 1):
                    relus(s + 1, 1 - par, columns[k + 1])
                if later(s, 3):
                    low_features(s + 3, 1 - par)
                if later(s, 2):
                    numbers(q + (k + 2) // RING3, (k + 2) % RING3)
                dve.wait_ge(out_pe, s + 1)
                dve.wait_ge(res_ok, s + 1)
                dve.scalar_tensor_tensor(out=fin[:, k, :], in0=PS[:, 5 + par, 0:D], scalar=1.0 / GAIN,
                                         in1=res[:, k, :], op0=ALU.mult, op1=ALU.add).then_inc(fin_ok, 1)


def fourier():
    t, f = np.arange(T), np.arange(T // 2)
    w = 2 * np.pi / T
    forth = np.concatenate([np.cos(w * np.outer(t, f)), np.cos(np.pi * t)[:, None],
                            -np.sin(w * np.outer(t, f[1:]))], 1)
    delay = (-t) % T
    back = np.concatenate([2 * np.cos(w * np.outer(f, delay)), np.cos(np.pi * delay)[None],
                           2 * np.sin(w * np.outer(f[1:], delay))], 0)
    back[0] = 1
    back /= T * D
    tiles = lambda a: np.ascontiguousarray(a.reshape(TT, P, T).transpose(1, 0, 2).astype(np.float32))
    short = forth[S - 1::-1]
    return tiles(forth), np.concatenate([short, short]).astype(np.float32), tiles(back)


def rotation():
    half = DH // 2
    freq = (1.0 / 10000.0 ** (np.arange(half, dtype=np.float32) / np.float32(half))).astype(np.float32)
    ang = (np.arange(T, dtype=np.float32)[:, None] * freq[None]).astype(np.float32)
    cos, sin = np.cos(ang), np.sin(ang)
    return (np.repeat(np.concatenate([cos, cos], 1).T, H, 0), np.repeat(np.concatenate([-sin, sin], 1).T, H, 0))


def kernel(**inputs):
    import concourse.bacc as bacc
    from concourse.bass_utils import run_bass_kernel_spmd

    a = {k: np.asarray(v) for k, v in inputs.items()}
    xa = lambda n: a["L0_xattn_" + n]
    ff = lambda n: a["L0_ffn_" + n]
    ctx_t = a["ctx_1024"][:, ::-1, :].reshape(PAIRS, 2 * S, D).transpose(2, 0, 1).reshape(D, PAIRS * 2 * S)
    pack1 = np.concatenate([xa("Wk").T, xa("Wv").T, xa("Wq").T, xa("bq")[:, None], xa("Wo"), xa("bk")[:, None],
                            xa("bv")[:, None], ctx_t, np.broadcast_to(xa("bo"), (P, D))], 1)
    rows = np.arange(D).reshape(H, DH)
    by_feature, partner = rows.T.reshape(D), np.roll(rows, DH // 2, axis=1).T.reshape(D)
    low = np.concatenate([ff("Wuk")[by_feature].T, ff("Wuk")[partner].T, ff("Wuv").T, ff("ln_g")[:, None],
                          ff("ln_b")[:, None]], 1)
    low = np.concatenate([low, low])
    pack2 = np.concatenate([ff("Wq")[by_feature].T, ff("Wq")[partner].T, ff("Wdkv").T, ff("Wo").T,
                            ff("norm1_w")[:, None], ff("norm2_w")[:, None], *rotation(), low], 1)
    w1 = ff("W1").transpose(2, 0, 1).reshape(D, E * HID)
    w2 = ff("W2").transpose(2, 0, 1).reshape(HK, P, E, D).transpose(1, 0, 2, 3).reshape(P, HK * E * D)
    tokens = (P * np.arange(NT)[None] + np.arange(P)[:, None]).astype(np.float32)
    b1 = ff("b1").reshape(E * HK, P).T
    pack3 = np.concatenate([w1, tokens, NOWHERE + np.arange(P, dtype=np.float32)[:, None], b1, w2], 1)
    edges = P * (REGION * np.arange(E)[:, None] + np.arange(NT)[None])
    constants = [E - np.arange(E), edges.ravel(), np.arange(SLOTS), P * np.arange(SLOTS)]
    pack4 = np.concatenate([ff("gate_w").ravel(), ff("norm2_w"), ff("gate_b"),
                            *(c.astype(np.float32) for c in constants), ff("b2").ravel()])[None]
    dft_x, dft_k, inv = fourier()
    arrays = {"x": a["x"], "pack1": pack1, "dft_x": dft_x, "dft_k": dft_k, "inv": inv, "pack2": pack2,
              "pack3": pack3, "pack4": pack4}
    arrays = {k: np.ascontiguousarray(v) for k, v in arrays.items()}
    nc = bacc.Bacc("TRN2", target_bir_lowering=False, num_devices=1)
    aps = {k: nc.dram_tensor(k, v.shape, mybir.dt.from_np(v.dtype), kind="ExternalInput").ap()
           for k, v in arrays.items()}
    out = nc.dram_tensor("out", (B, T, D), F32, kind="ExternalOutput").ap()
    sorted_rows = nc.dram_tensor("sorted_rows", ((REGION * E + E - 1) * P, ROW), F32, kind="Internal").ap()
    build(nc, sorted_rows=sorted_rows, out=out, **aps)
    res = run_bass_kernel_spmd(nc, [arrays], core_ids=[0])
    return res.results[0]["out"]
```
